# Optimizing a Trainium2 kernel written in Bass

```python
import numpy as np
import jax
import jax.numpy as jnp

def _softmax(x, axis=-1):
    return jax.nn.softmax(x, axis=axis)

def _gelu(x):
    return jax.nn.gelu(x, approximate=True)

def _silu(x):
    return jax.nn.silu(x)

def _sigmoid(x):
    return jax.nn.sigmoid(x)

def _layernorm(x, axis=-1, eps=1e-05):
    m = jnp.mean(x, axis=axis, keepdims=True)
    v = jnp.var(x, axis=axis, keepdims=True)
    return (x - m) / jnp.sqrt(v + eps)

def _scatter_add(tgt, idx, src, axis=0):
    return tgt.at[idx].add(src)

def _segment_sum(src, seg, n):
    return jax.ops.segment_sum(src, seg, n)
kernel_name = 'mk_perceiver_d1_seqx_r2_6f9a16'

def setup_inputs(seed: int=0):
    np.random.seed(seed)
    _w = jnp.asarray

    def _rec_inputs():
        import jax
        import jax.numpy as jnp
        _rk = jax.random.key(seed)
        x = 7.22e-05 + 1 * jax.random.normal(jax.random.fold_in(_rk, 1), (8, 64, 512), jnp.float32)
        _lenS = 64 - jax.random.randint(jax.random.fold_in(_rk, 7), (8,), 0, max(1, 64 // 4) + 1, jnp.int32)
        _lenS2 = 512 - jax.random.randint(jax.random.fold_in(_rk, 8), (8,), 0, max(1, 512 // 4) + 1, jnp.int32)
        _ctx_1024P = jax.random.normal(jax.random.fold_in(_rk, 11), (8, 16, 512), jnp.float32)
        _ctx_1024c = jax.random.dirichlet(jax.random.fold_in(_rk, 511), 0.3 * jnp.ones((16,), jnp.float32), (8, 512))
        _ctx_1024t = jnp.einsum('bsk,bkd->bsd', _ctx_1024c, _ctx_1024P)
        _ctx_1024t = _ctx_1024t * jax.lax.rsqrt(jnp.mean(jnp.square(_ctx_1024t)) + 1e-12) * 0.953939
        ctx_1024 = 4.13588e-05 + 0.999923 * (_ctx_1024t + 0.3 * jax.random.normal(jax.random.fold_in(_rk, 611), (8, 512, 512), jnp.float32))
        return (x, ctx_1024)
    x, ctx_1024 = _rec_inputs()

    def _L0_xattn_setup():
        import jax, jax.numpy as jnp
        import numpy as np
        B, SD, SE, D, H = (4, 1024, 1024, 512, 16)
        HD = D // H

        def _mha(xq, xk, xv, Wq, bq, Wk, bk, Wv, bv, Wo, bo, causal):
            q = jnp.einsum('bsd,hde->bhse', xq, Wq) + bq[None, :, None, :]
            k = jnp.einsum('bsd,hde->bhse', xk, Wk) + bk[None, :, None, :]
            v = jnp.einsum('bsd,hde->bhse', xv, Wv) + bv[None, :, None, :]
            scale = 1.0 / jnp.sqrt(jnp.asarray(HD, q.dtype))
            scores = jnp.einsum('bhqe,bhke->bhqk', q, k) * scale
            if causal:
                mask = jnp.tril(jnp.ones((q.shape[2], k.shape[2]), bool))
                scores = jnp.where(mask, scores, jnp.finfo(scores.dtype).min)
            w = jax.nn.softmax(scores, axis=-1)
            out = jnp.einsum('bhqk,bhke->bhqe', w, v)
            out = out.transpose(0, 2, 1, 3).reshape(out.shape[0], out.shape[2], D)
            return out @ Wo + bo
        key = jax.random.key(seed)
        ks = jax.random.split(key, 19)
        sd = 1.0 / np.sqrt(D)
        n = lambda k, shape, s: jax.random.normal(k, shape, jnp.float32) * s
        inp = {'x': n(ks[0], (B, SD, D), 1.0), 'encoder_k': n(ks[1], (B, SE, D), 1.0), 'encoder_v': n(ks[2], (B, SE, D), 1.0), 'Wq1': n(ks[3], (H, D, HD), sd), 'bq1': jnp.zeros((H, HD), jnp.float32), 'Wk1': n(ks[4], (H, D, HD), sd), 'bk1': jnp.zeros((H, HD), jnp.float32), 'Wv1': n(ks[5], (H, D, HD), sd), 'bv1': jnp.zeros((H, HD), jnp.float32), 'Wo1': n(ks[6], (D, D), sd), 'bo1': jnp.zeros((D,), jnp.float32), 'Wq2': n(ks[7], (H, D, HD), sd), 'bq2': jnp.zeros((H, HD), jnp.float32), 'Wk2': n(ks[8], (H, D, HD), sd), 'bk2': jnp.zeros((H, HD), jnp.float32), 'Wv2': n(ks[9], (H, D, HD), sd), 'bv2': jnp.zeros((H, HD), jnp.float32), 'Wo2': n(ks[10], (D, D), sd), 'bo2': jnp.zeros((D,), jnp.float32)}
        return inp
    _L0_xattn_all = _L0_xattn_setup()
    _L0_xattn_in = {k: v for k, v in _L0_xattn_all.items() if k in ('Wq1', 'bq1', 'Wk1', 'bk1', 'Wv1', 'bv1', 'Wo1', 'bo1', 'Wq2', 'bq2', 'Wk2', 'bk2', 'Wv2', 'bv2', 'Wo2', 'bo2')}
    del _L0_xattn_all

    def _L0_attn_setup():
        import jax, jax.numpy as jnp
        import numpy as np
        HIDDEN = 512
        STATE = 16
        DT_RANK = 64
        key = jax.random.key(seed)
        ks = jax.random.split(key, 5)
        B, S = (2, 1024)
        x = jax.random.normal(ks[0], (B, S, HIDDEN), dtype=jnp.float32)
        W_xproj = jax.random.normal(ks[1], (HIDDEN, STATE * 2 + DT_RANK), dtype=jnp.float32) / np.sqrt(HIDDEN)
        W_dt = jax.random.normal(ks[2], (DT_RANK, HIDDEN), dtype=jnp.float32) / np.sqrt(DT_RANK)
        b_dt = jnp.zeros((HIDDEN,), dtype=jnp.float32)
        A_log = jax.random.normal(ks[3], (STATE, HIDDEN), dtype=jnp.float32) / np.sqrt(STATE)
        return {'x': x, 'W_xproj': W_xproj, 'W_dt': W_dt, 'b_dt': b_dt, 'A_log': A_log}
    _L0_attn_all = _L0_attn_setup()
    _L0_attn_in = {k: v for k, v in _L0_attn_all.items() if k in ('W_xproj', 'W_dt', 'b_dt', 'A_log')}
    del _L0_attn_all

    def _L0_ffn_setup():
        import jax, jax.numpy as jnp
        import numpy as np
        N_EXPERTS = 32
        TOP_K = 8
        N_GROUP = 4
        TOPK_GROUP = 2
        ROUTED_SCALING = 2.5

        def _gate(x, gate_w, gate_bias):
            T, E = (x.shape[0], gate_w.shape[0])
            logits = jnp.einsum('th,eh->te', x, gate_w)
            scores = jax.nn.sigmoid(logits)
            scores_choice = scores + gate_bias[None, :]
            grp = scores_choice.reshape(T, N_GROUP, E // N_GROUP)
            top2, _ = jax.lax.top_k(grp, 2)
            group_scores = top2.sum(-1)
            _, grp_idx = jax.lax.top_k(group_scores, TOPK_GROUP)
            group_mask = jax.nn.one_hot(grp_idx, N_GROUP, dtype=scores.dtype).sum(1)
            expert_mask = jnp.repeat(group_mask, E // N_GROUP, axis=1)
            masked = jnp.where(expert_mask > 0, scores_choice, 0.0)
            _, topk_idx = jax.lax.top_k(masked, TOP_K)
            topk_w = jnp.take_along_axis(scores, topk_idx, axis=1)
            topk_w = topk_w / (topk_w.sum(-1, keepdims=True) + 1e-20)
            topk_w = topk_w * ROUTED_SCALING
            return (topk_idx, topk_w)

        def _mlp(x, wg, wu, wd):
            return jnp.einsum('...i,hi->...h', jax.nn.silu(jnp.einsum('...h,ih->...i', x, wg)) * jnp.einsum('...h,ih->...i', x, wu), wd)
        key = jax.random.key(seed)
        ks = jax.random.split(key, 9)
        B, S, H, I = (2, 256, 512, 256)
        w = 0.02
        return {'hidden_states': jax.random.normal(ks[0], (B, S, H), jnp.float32), 'gate_w': jax.random.normal(ks[1], (N_EXPERTS, H), jnp.float32) * w, 'gate_bias': jax.random.normal(ks[2], (N_EXPERTS,), jnp.float32) * w, 'expert_gate': jax.random.normal(ks[3], (N_EXPERTS, I, H), jnp.float32) * w, 'expert_up': jax.random.normal(ks[4], (N_EXPERTS, I, H), jnp.float32) * w, 'expert_down': jax.random.normal(ks[5], (N_EXPERTS, H, I), jnp.float32) * w, 'shared_gate': jax.random.normal(ks[6], (2 * I, H), jnp.float32) * w, 'shared_up': jax.random.normal(ks[7], (2 * I, H), jnp.float32) * w, 'shared_down': jax.random.normal(ks[8], (H, 2 * I), jnp.float32) * w}
    _L0_ffn_all = _L0_ffn_setup()
    _L0_ffn_in = {k: v for k, v in _L0_ffn_all.items() if k in ('gate_w', 'gate_bias', 'expert_gate', 'expert_up', 'expert_down', 'shared_gate', 'shared_up', 'shared_down')}
    del _L0_ffn_all
    return {'x': x, 'ctx_1024': ctx_1024, 'L0_xattn_Wq1': _L0_xattn_in['Wq1'], 'L0_xattn_bq1': _L0_xattn_in['bq1'], 'L0_xattn_Wk1': _L0_xattn_in['Wk1'], 'L0_xattn_bk1': _L0_xattn_in['bk1'], 'L0_xattn_Wv1': _L0_xattn_in['Wv1'], 'L0_xattn_bv1': _L0_xattn_in['bv1'], 'L0_xattn_Wo1': _L0_xattn_in['Wo1'], 'L0_xattn_bo1': _L0_xattn_in['bo1'], 'L0_xattn_Wq2': _L0_xattn_in['Wq2'], 'L0_xattn_bq2': _L0_xattn_in['bq2'], 'L0_xattn_Wk2': _L0_xattn_in['Wk2'], 'L0_xattn_bk2': _L0_xattn_in['bk2'], 'L0_xattn_Wv2': _L0_xattn_in['Wv2'], 'L0_xattn_bv2': _L0_xattn_in['bv2'], 'L0_xattn_Wo2': _L0_xattn_in['Wo2'], 'L0_xattn_bo2': _L0_xattn_in['bo2'], 'L0_attn_W_xproj': _L0_attn_in['W_xproj'], 'L0_attn_W_dt': _L0_attn_in['W_dt'], 'L0_attn_b_dt': _L0_attn_in['b_dt'], 'L0_attn_A_log': _L0_attn_in['A_log'], 'L0_ffn_gate_w': _L0_ffn_in['gate_w'], 'L0_ffn_gate_bias': _L0_ffn_in['gate_bias'], 'L0_ffn_expert_gate': _L0_ffn_in['expert_gate'], 'L0_ffn_expert_up': _L0_ffn_in['expert_up'], 'L0_ffn_expert_down': _L0_ffn_in['expert_down'], 'L0_ffn_shared_gate': _L0_ffn_in['shared_gate'], 'L0_ffn_shared_up': _L0_ffn_in['shared_up'], 'L0_ffn_shared_down': _L0_ffn_in['shared_down']}

def reference(x, ctx_1024, L0_xattn_Wq1, L0_xattn_bq1, L0_xattn_Wk1, L0_xattn_bk1, L0_xattn_Wv1, L0_xattn_bv1, L0_xattn_Wo1, L0_xattn_bo1, L0_xattn_Wq2, L0_xattn_bq2, L0_xattn_Wk2, L0_xattn_bk2, L0_xattn_Wv2, L0_xattn_bv2, L0_xattn_Wo2, L0_xattn_bo2, L0_attn_W_xproj, L0_attn_W_dt, L0_attn_b_dt, L0_attn_A_log, L0_ffn_gate_w, L0_ffn_gate_bias, L0_ffn_expert_gate, L0_ffn_expert_up, L0_ffn_expert_down, L0_ffn_shared_gate, L0_ffn_shared_up, L0_ffn_shared_down):
    import jax
    import jax.numpy as jnp

    def _L0_xattn_ref(x, encoder_k, encoder_v, Wq1, bq1, Wk1, bk1, Wv1, bv1, Wo1, bo1, Wq2, bq2, Wk2, bk2, Wv2, bv2, Wo2, bo2):
        import jax, jax.numpy as jnp
        import numpy as np
        B, SD, SE, D, H = (4, 1024, 1024, 512, 16)
        HD = D // H

        def _mha(xq, xk, xv, Wq, bq, Wk, bk, Wv, bv, Wo, bo, causal):
            q = jnp.einsum('bsd,hde->bhse', xq, Wq) + bq[None, :, None, :]
            k = jnp.einsum('bsd,hde->bhse', xk, Wk) + bk[None, :, None, :]
            v = jnp.einsum('bsd,hde->bhse', xv, Wv) + bv[None, :, None, :]
            scale = 1.0 / jnp.sqrt(jnp.asarray(HD, q.dtype))
            scores = jnp.einsum('bhqe,bhke->bhqk', q, k) * scale
            if causal:
                mask = jnp.tril(jnp.ones((q.shape[2], k.shape[2]), bool))
                scores = jnp.where(mask, scores, jnp.finfo(scores.dtype).min)
            w = jax.nn.softmax(scores, axis=-1)
            out = jnp.einsum('bhqk,bhke->bhqe', w, v)
            out = out.transpose(0, 2, 1, 3).reshape(out.shape[0], out.shape[2], D)
            return out @ Wo + bo
        h = _mha(x, x, x, Wq1, bq1, Wk1, bk1, Wv1, bv1, Wo1, bo1, causal=True)
        out = _mha(h, encoder_k, encoder_v, Wq2, bq2, Wk2, bk2, Wv2, bv2, Wo2, bo2, causal=False)
        return out

    def _L0_attn_ref(x, W_xproj, W_dt, b_dt, A_log):
        import jax, jax.numpy as jnp
        import numpy as np
        HIDDEN = 512
        STATE = 16
        DT_RANK = 64
        xp = x @ W_xproj
        Bm = xp[..., :STATE]
        Cm = xp[..., STATE:2 * STATE]
        dt = jax.nn.softplus(xp[..., 2 * STATE:] @ W_dt + b_dt)
        A = -jnp.exp(A_log)
        A_bar = jnp.exp(A[None, None] * dt[:, :, None, :])
        Bu = Bm[:, :, :, None] * dt[:, :, None, :] * x[:, :, None, :]

        def scan_fn(h, inp):
            A_t, Bu_t = inp
            h = A_t * h + Bu_t
            return (h, h)
        h0 = jnp.zeros(Bu.shape[:1] + Bu.shape[2:], dtype=x.dtype)
        _, h_all = jax.lax.scan(scan_fn, h0, (A_bar.transpose(1, 0, 2, 3), Bu.transpose(1, 0, 2, 3)))
        y = jnp.einsum('bsn,sbnd->bsd', Cm, h_all)
        return y

    def _L0_ffn_ref(hidden_states, gate_w, gate_bias, expert_gate, expert_up, expert_down, shared_gate, shared_up, shared_down):
        import jax, jax.numpy as jnp
        import numpy as np
        N_EXPERTS = 32
        TOP_K = 8
        N_GROUP = 4
        TOPK_GROUP = 2
        ROUTED_SCALING = 2.5

        def _gate(x, gate_w, gate_bias):
            T, E = (x.shape[0], gate_w.shape[0])
            logits = jnp.einsum('th,eh->te', x, gate_w)
            scores = jax.nn.sigmoid(logits)
            scores_choice = scores + gate_bias[None, :]
            grp = scores_choice.reshape(T, N_GROUP, E // N_GROUP)
            top2, _ = jax.lax.top_k(grp, 2)
            group_scores = top2.sum(-1)
            _, grp_idx = jax.lax.top_k(group_scores, TOPK_GROUP)
            group_mask = jax.nn.one_hot(grp_idx, N_GROUP, dtype=scores.dtype).sum(1)
            expert_mask = jnp.repeat(group_mask, E // N_GROUP, axis=1)
            masked = jnp.where(expert_mask > 0, scores_choice, 0.0)
            _, topk_idx = jax.lax.top_k(masked, TOP_K)
            topk_w = jnp.take_along_axis(scores, topk_idx, axis=1)
            topk_w = topk_w / (topk_w.sum(-1, keepdims=True) + 1e-20)
            topk_w = topk_w * ROUTED_SCALING
            return (topk_idx, topk_w)

        def _mlp(x, wg, wu, wd):
            return jnp.einsum('...i,hi->...h', jax.nn.silu(jnp.einsum('...h,ih->...i', x, wg)) * jnp.einsum('...h,ih->...i', x, wu), wd)
        orig_shape = hidden_states.shape
        H = orig_shape[-1]
        residuals = hidden_states
        x = hidden_states.reshape(-1, H)
        topk_idx, topk_w = _gate(x, gate_w, gate_bias)
        g = jnp.einsum('th,eih->eti', x, expert_gate)
        u = jnp.einsum('th,eih->eti', x, expert_up)
        outs = jnp.einsum('eti,ehi->eth', jax.nn.silu(g) * u, expert_down)
        outs_t = jnp.transpose(outs, (1, 0, 2))
        gathered = jnp.take_along_axis(outs_t, topk_idx[:, :, None], axis=1)
        final = (gathered * topk_w[:, :, None]).sum(1)
        shared = _mlp(residuals, shared_gate, shared_up, shared_down)
        return final.reshape(orig_shape) + shared
    x = x + _L0_xattn_ref(_layernorm(x, axis=-1), ctx_1024, ctx_1024, L0_xattn_Wq1, L0_xattn_bq1, L0_xattn_Wk1, L0_xattn_bk1, L0_xattn_Wv1, L0_xattn_bv1, L0_xattn_Wo1, L0_xattn_bo1, L0_xattn_Wq2, L0_xattn_bq2, L0_xattn_Wk2, L0_xattn_bk2, L0_xattn_Wv2, L0_xattn_bv2, L0_xattn_Wo2, L0_xattn_bo2)
    x = x + _L0_attn_ref(_layernorm(x, axis=-1), L0_attn_W_xproj, L0_attn_W_dt, L0_attn_b_dt, L0_attn_A_log)
    x = x + _L0_ffn_ref(_layernorm(x, axis=-1), L0_ffn_gate_w, L0_ffn_gate_bias, L0_ffn_expert_gate, L0_ffn_expert_up, L0_ffn_expert_down, L0_ffn_shared_gate, L0_ffn_shared_up, L0_ffn_shared_down)
    return x

_drawn_inputs = setup_inputs


def setup_inputs(seed=0):
    import zlib

    import numpy as np

    out = dict(_drawn_inputs(seed))
    spreads = {'L0_xattn_bq1': (0.0, 0.8),
     'L0_xattn_bk1': (0.0, 0.8),
     'L0_xattn_bv1': (0.0, 0.1),
     'L0_xattn_bo1': (0.0, 0.268),
     'L0_xattn_bq2': (0.0, 0.1),
     'L0_xattn_bk2': (0.0, 0.8),
     'L0_xattn_bv2': (0.0, 0.1),
     'L0_xattn_bo2': (0.0, 0.1),
     'L0_attn_b_dt': (0.0, 0.1)}
    factors = {'L0_ffn_gate_w': 8.0,
     'L0_ffn_gate_bias': 8.0,
     'L0_ffn_expert_gate': 8.0,
     'L0_ffn_expert_up': 8.0,
     'L0_ffn_expert_down': 8.0,
     'L0_ffn_shared_gate': 5.811,
     'L0_ffn_shared_up': 5.665,
     'L0_ffn_shared_down': 5.692}
    for name, (base, spread) in spreads.items():
        noise = np.random.default_rng([zlib.crc32(name.encode()), seed]).standard_normal(out[name].shape)
        drawn = base * np.exp(spread * noise) if base else spread * noise
        out[name] = jnp.asarray(drawn.astype(out[name].dtype))
    for name, factor in factors.items():
        out[name] = (out[name] * factor).astype(out[name].dtype)
    return out
```

```python
from contextlib import ExitStack

import numpy as np
import concourse.bass as bass
from concourse import mybir

P = 128
B, S, D = 8, 64, 512
SC = 512
H, HD = 16, 32
T = B * S
NT = T // P
KC = D // P
GH = P // HD
NS = 16
RANK = 64
E, EI = 32, 256
NG, EG = 4, 8
NSH = 2
NU = E + NSH
IC = EI // P
EPS = 1e-5
QSCALE = float(HD) ** -0.5
ROUTED_SCALING = 2.5
LOWEST = -3.0e38
N_W = 7
WQ1, WK1, WV1, WO1, WQ2, WK2, WV2, WO2 = range(N_W + 1)
BQ1, BK1, BV1, BO1, BQ2, BK2, BV2, BDT = [KC * n for n in range(8)]
ALOG = KC * 8
N_SMALL = ALOG + KC * NS


def perceiver_block(nc, x, ctx_t, w_proj, small, bo2, w_xp, w_dt, gate_w, gate_b, w_moe, out):
    fp32 = mybir.dt.float32
    f32r = mybir.dt.float32r
    ALU = mybir.AluOpType
    ACT = mybir.ActivationFunctionType
    AX = mybir.AxisListType

    es = ExitStack()
    with es:
        def sb(name, shape, dt=fp32):
            return es.enter_context(nc.sbuf_tensor(name, shape, dt))

        def sem(name):
            return es.enter_context(nc.semaphore(name))

        HALF = KC * D
        RA, RB, RC, RD, RX, RQ = [sb(n, [P, 2 * HALF], f32r) for n in ("RA", "RB", "RC", "RD", "RX", "RQ")]

        def pair(r):
            return [r[:, k * HALF:(k + 1) * HALF].rearrange("p (k n) -> p k n", k=KC) for k in range(2)]

        xT = pair(RX)
        w_of = {WQ1: pair(RA), WK1: pair(RB), WV1: pair(RC), WO1: pair(RD),
                WQ2: pair(RX), WK2: pair(RA), WV2: pair(RB)}
        o1T = pair(RC)
        hT = pair(RQ)
        ctxT = pair(RD)
        k2 = pair(RC)
        v2 = pair(RX)
        qb = [RQ[:, k * 1024:(k + 1) * 1024].rearrange("p (g h q) -> p g h q", g=KC, h=2) for k in range(2)]
        pT = [RQ[:, 2048 + k * 1024:2048 + (k + 1) * 1024].rearrange("p (c q) -> p c q", c=4) for k in range(2)]
        gu_w = [[r[:, k * HALF:(k + 1) * HALF] for k in range(2)] for r in (RA, RB)]
        dn_w = [[RC[:, j * HALF + k * IC * D:j * HALF + (k + 1) * IC * D] for k in range(2)] for j in range(2)]
        inner = [[RD[:, j * HALF + k * IC * T:j * HALF + (k + 1) * IC * T].rearrange("p (i n) -> p i n", i=IC)
                  for k in range(2)] for j in range(2)]
        gw = [RQ[:, k * KC * E:(k + 1) * KC * E].rearrange("p (k e) -> p k e", k=KC) for k in range(2)]

        arena = sb("arena", [P, 3 * HALF])
        xn_all = arena[:, 0:HALF].rearrange("p (t n) -> p t n", t=NT)
        q1, k1, v1 = [arena[:, n * HALF:(n + 1) * HALF].rearrange("p (k n) -> p k n", k=KC) for n in range(3)]
        decay, drive, c_bc = [arena[:, n * HALF:(n + 1) * HALF].rearrange("p (s n) -> p s n", s=NS) for n in range(3)]
        b_bc = sb("b_bc", [P, NS, P])
        wo2 = sb("wo2", [P, KC, D])
        x_tok = sb("x_tok", [P, NT, D])
        q2 = sb("q2", [P, KC, T])
        raw = [sb(f"raw{j}", [P, HALF]) for j in range(2)]
        prob = [sb(f"prob{j}", [P, 512]) for j in range(2)]
        tmp = [sb(f"tmp{j}", [P, 512]) for j in range(6)]
        scr1 = tmp[0:2]
        xn2, x2T, dt_z, dt_x, dt_e, o2f = tmp
        yT = dt_e
        raw_dn = [arena[:, HALF + j * IC * D:HALF + (j + 1) * IC * D] for j in range(2)]
        w_bc = [q2.rearrange("p k n -> p (k n)")[:, j * T:(j + 1) * T] for j in range(2)]
        silu = tmp[0:2]
        act_f = tmp[2:4]
        gw_raw = sb("gw_raw", [P, KC, E])
        gb_bc = sb("gb_bc", [P, E])
        post = b_bc[:, :, :].rearrange("p s n -> p (s n)")
        wT_sb = post[0:E, 0:T]
        ones = post[0:NSH, T:2 * T]
        rt = post[:, 2 * T:2 * T + 5 * NT * E].rearrange("p (a t e) -> p a t e", a=5, t=NT)
        top = sb("top", [P, NT, NG, 8])
        grp = sb("grp", [P, 4, NT, NG])
        top8 = sb("top8", [P, NT, 8])
        rsum = sb("rsum", [P, NT])
        zero = sb("zero", [P, P])
        x1s = sb("x1s", [P, D])
        smallp = sb("smallp", [P, N_SMALL])
        a_pos = sb("a_pos", [P, KC, NS])
        bo2_bc = tmp[5]
        ident = sb("ident", [P, P])
        mask = sb("mask", [P, P])
        wxp = sb("wxp", [P, KC, 2 * NS + RANK])
        wdt = sb("wdt", [RANK, D])
        bc_sb = sb("bc_sb", [2 * NS, P])
        dtr = sb("dtr", [RANK, P])
        st = sb("st", [P, NT, 6])
        mv = sb("mv", [P, NT, 2])
        ln = sb("ln", [P, 5, NT])
        nm = sb("nm", [P, 16])
        sm = sb("sm", [P, 64])
        rs = sb("rs", [P, 64])
        bank = [es.enter_context(nc.psum_tensor(f"bank{n}", [P, 512], fp32)) for n in range(8)]

        def bias(col):
            return smallp[:, col:col + 1]

        w_dram = nc.dram_tensor("route_scratch", (NU, T), fp32, kind="Internal").ap()
        bc_dram = nc.dram_tensor("bc_scratch", (NT, 2 * NS, P), fp32, kind="Internal").ap()

        s_x_in = sem("x_in")
        s_wo2_in = sem("wo2_in")
        s_small_in = sem("small_in")
        s_w_in0 = sem("w_in0")
        s_w_in1 = sem("w_in1")
        s_ctx_in0 = sem("ctx_in0")
        s_ctx_in1 = sem("ctx_in1")
        s_bc_out = sem("bc_out")
        s_b_in = sem("b_in")
        s_c_in = sem("c_in")
        s_out_done = sem("out_done")
        s_consts = sem("consts")
        s_w_hi = sem("w_hi")
        s_w_lo = sem("w_lo")
        s_ln_step = sem("ln_step")
        s_ln_ve = sem("ln_ve")
        s_ln_r0 = sem("ln_r0")
        s_xn_ready = sem("xn_ready")
        s_xnT_ready = sem("xnT_ready")
        s_xT_hi = sem("xT_hi")
        s_xT_lo = sem("xT_lo")
        s_p1_ready = sem("p1_ready")
        s_p1_out = sem("p1_out")
        s_s1_ready = sem("s1_ready")
        s_s1_out = sem("s1_out")
        s_s1_max = sem("s1_max")
        s_s1_exp = sem("s1_exp")
        s_s1_sum = sem("s1_sum")
        s_s1_norm = sem("s1_norm")
        s_s1_T = sem("s1_T")
        s_s1_pT = sem("s1_pT")
        s_s1_pv = sem("s1_pv")
        s_o1_sum = sem("o1_sum")
        s_o1_hi = sem("o1_hi")
        s_o1_lo = sem("o1_lo")
        s_h_ready = sem("h_ready")
        s_h_hi = sem("h_hi")
        s_h_lo = sem("h_lo")
        s_q2_ready = sem("q2_ready")
        s_q2_out = sem("q2_out")
        s_ctx_hi = sem("ctx_hi")
        s_ctx_lo = sem("ctx_lo")
        s_kv_ready = sem("kv_ready")
        s_kv_hi = sem("kv_hi")
        s_kv_lo = sem("kv_lo")
        s_qb_hi = sem("qb_hi")
        s_qb_lo = sem("qb_lo")
        s_s2_ready = sem("s2_ready")
        s_s2_max = sem("s2_max")
        s_s2_exp = sem("s2_exp")
        s_s2_sum = sem("s2_sum")
        s_s2_norm = sem("s2_norm")
        s_s2_T = sem("s2_T")
        s_pT_hi = sem("pT_hi")
        s_pT_lo = sem("pT_lo")
        s_pv_ready = sem("pv_ready")
        s_o2_out = sem("o2_out")
        s_wo2_ready = sem("wo2_ready")
        s_x1_done = sem("x1_done")
        s_ln2_step = sem("ln2_step")
        s_ln2_stat = sem("ln2_stat")
        s_ln2_ve = sem("ln2_ve")
        s_ln2_r0 = sem("ln2_r0")
        s_xn2_ready = sem("xn2_ready")
        s_x2T_ready = sem("x2T_ready")
        s_x2T_out = sem("x2T_out")
        s_xp_ready = sem("xp_ready")
        s_bc_ready = sem("bc_ready")
        s_dtr_ready = sem("dtr_ready")
        s_dtp_ready = sem("dtp_ready")
        s_dt_z_ready = sem("dt_z_ready")
        s_dt_step = sem("dt_step")
        s_dt_ready = sem("dt_ready")
        s_dtx_ready = sem("dtx_ready")
        s_decay_arg = sem("decay_arg")
        s_decay_exp = sem("decay_exp")
        s_decay_zero = sem("decay_zero")
        s_drive_ready = sem("drive_ready")
        s_scan_done = sem("scan_done")
        s_hc_ready = sem("hc_ready")
        s_y_ready = sem("y_ready")
        s_yT_ready = sem("yT_ready")
        s_x2_done = sem("x2_done")
        s_a_ready = sem("a_ready")
        s_gate_in = sem("gate_in")
        s_gw_hi = sem("gw_hi")
        s_gw_lo = sem("gw_lo")
        s_ln3 = sem("ln3")
        s_ln3_ve = sem("ln3_ve")
        s_ln3_r0 = sem("ln3_r0")
        s_ln3_step = sem("ln3_step")
        s_xn3_ready = sem("xn3_ready")
        s_xn3T_ready = sem("xn3T_ready")
        s_x3_hi = sem("x3_hi")
        s_x3_lo = sem("x3_lo")
        s_logit_ready = sem("logit_ready")
        s_r_exp = sem("r_exp")
        s_r_step = sem("r_step")
        s_w_ready = sem("w_ready")
        s_wT_ready = sem("wT_ready")
        s_wT_out = sem("wT_out")
        s_w_stored = sem("w_stored")
        s_ones_ready = sem("ones_ready")
        s_gu_in0 = sem("gu_in0")
        s_gu_in1 = sem("gu_in1")
        s_dn_in0 = sem("dn_in0")
        s_dn_in1 = sem("dn_in1")
        s_wb_in0 = sem("wb_in0")
        s_wb_in1 = sem("wb_in1")
        s_gu_hi = sem("gu_hi")
        s_gu_lo = sem("gu_lo")
        s_dn_hi = sem("dn_hi")
        s_dn_lo = sem("dn_lo")
        s_gu_ready = sem("gu_ready")
        s_silu_done = sem("silu_done")
        s_gated = sem("gated")
        s_h_ready2 = sem("h_ready2")
        s_h_hi2 = sem("h_hi2")
        s_h_lo2 = sem("h_lo2")
        s_moe_done = sem("moe_done")
        s_x3_done = sem("x3_done")

        block = es.enter_context(nc.Block())
        w_in = [s_w_in0, s_w_in1]
        ctx_in = [s_ctx_in0, s_ctx_in1]
        gu_in, dn_in, wb_in = [[s_gu_in0, s_gu_in1], [s_dn_in0, s_dn_in1], [s_wb_in0, s_wb_in1]]
        GU = 2 * KC * EI

        @block.sync
        def _(sp):
            sp.dma_start(x_tok[:, :, :], x.rearrange("(t p) d -> p t d", p=P)).then_inc(s_x_in, 16)
            for n in range(N_W):
                if n >= 2:
                    sp.wait_ge(s_w_lo, n - 1)
                sp.dma_start(raw[n % 2][:, :], w_proj[n]).then_inc(w_in[n % 2], 16)
                if n == WQ2:
                    sp.dma_start(wo2[:, :, :], w_proj[WO2].rearrange("p (k n) -> p k n", k=KC)).then_inc(s_wo2_in, 16)
                if n == 0:
                    sp.dma_start(smallp[:, :], small).then_inc(s_small_in, 16)
                    sp.dma_start(bo2_bc[:, :], bo2.partition_broadcast(P)).then_inc(s_small_in, 16)
                    sp.dma_start(wxp[:, :, :], w_xp).then_inc(s_small_in, 16)
                    sp.dma_start(wdt[:, :], w_dt).then_inc(s_small_in, 16)
                    sp.dma_start(gw_raw[:, :, :], gate_w).then_inc(s_gate_in, 16)
                    sp.dma_start(gb_bc[:, :], gate_b.partition_broadcast(P)).then_inc(s_gate_in, 16)
            sp.wait_ge(s_w_lo, N_W)
            with sp.Fori(0, NT) as tp:
                for j in range(2):
                    sp.wait_ge(s_ctx_lo, tp * 2 + (j + 1))
                    sp.dma_start(raw[j][:, :], ctx_t[bass.ds(tp * 2 + j, 1)].rearrange("a p n -> (a p) n")).then_inc(ctx_in[j], 16)
                sp.wait_ge(s_bc_ready, tp + 1)
                sp.dma_start(bc_dram[bass.ds(tp, 1)].rearrange("a r n -> (a r) n"), bc_sb[:, :]).then_inc(s_bc_out, 16)
                sp.wait_ge(s_bc_out, tp * 16 + 16)
                sp.dma_start(b_bc[:, :, :], bc_dram[bass.ds(tp, 1), 0:NS, :].rearrange("a r n -> (a r n)").partition_broadcast(P)).then_inc(s_b_in, 16)
                sp.dma_start(c_bc[:, :, :], bc_dram[bass.ds(tp, 1), NS:2 * NS, :].rearrange("a r n -> (a r n)").partition_broadcast(P)).then_inc(s_c_in, 16)
            sp.wait_ge(s_ctx_lo, B + 2)
            sp.wait_ge(s_y_ready, NT * KC)
            for j in range(2):
                sp.dma_start(raw[j][:, :], w_moe[j, :, 0:GU]).then_inc(gu_in[j], 16)
                sp.dma_start(raw_dn[j], w_moe[j, :, GU:]).then_inc(dn_in[j], 16)
            sp.wait_ge(s_ones_ready, 1)
            sp.dma_start(w_dram[0:NSH, :], ones).then_inc(s_w_stored, 16)
            sp.wait_ge(s_wT_out, 1)
            sp.dma_start(w_dram[NSH:NU, :], wT_sb).then_inc(s_w_stored, 16)
            sp.wait_ge(s_w_stored, 32)
            for j in range(2):
                sp.dma_start(w_bc[j], w_dram[j, :].partition_broadcast(P)).then_inc(wb_in[j], 16)
            with sp.Fori(0, NU // 2 - 1) as k:
                for j in range(2):
                    sp.wait_ge(s_gu_lo, k * 2 + (j + 1))
                    sp.dma_start(raw[j][:, :], w_moe[bass.ds(k * 2 + (j + 2), 1), :, 0:GU].rearrange("a p n -> (a p) n")).then_inc(gu_in[j], 16)
                    sp.wait_ge(s_dn_lo, k * 2 + (j + 1))
                    sp.dma_start(raw_dn[j], w_moe[bass.ds(k * 2 + (j + 2), 1), :, GU:].rearrange("a p n -> (a p) n")).then_inc(dn_in[j], 16)
                    sp.wait_ge(s_gated, k * 4 + (2 * j + 2))
                    sp.dma_start(w_bc[j], w_dram[bass.ds(k * 2 + (j + 2), 1), :].rearrange("a n -> (a n)").partition_broadcast(P)).then_inc(wb_in[j], 16)
            ov = out.rearrange("(t p) d -> p t d", p=P)
            for t in range(NT):
                sp.wait_ge(s_x3_done, t + 1)
                sp.dma_start(ov[:, t, :], x_tok[:, t, :]).then_inc(s_out_done, 16)
            sp.wait_ge(s_out_done, 16 * NT)

        @block.gpsimd
        def _(pool):
            pool.memset(ident[:, :], 0.0).then_inc(s_consts, 1)
            pool.memset(mask[:, :], 0.0).then_inc(s_consts, 1)
            pool.memset(zero[:, :], 0.0).then_inc(s_consts, 1)
            pool.wait_ge(s_consts, 3)
            pool.affine_select(out=ident[:, :], in_=ident[:, :], compare_op=ALU.not_equal, fill=1.0, base=0,
                               pattern=[[-1, P]], channel_multiplier=1).then_inc(s_consts, 1)
            pool.affine_select(out=mask[:, :], in_=mask[:, :], compare_op=ALU.is_ge, fill=LOWEST, base=0,
                               pattern=[[-1, P]], channel_multiplier=1).then_inc(s_consts, 1)
            pool.wait_ge(s_consts, 5)
            pool.affine_select(out=mask[S:P, :], in_=mask[S:P, :], compare_op=ALU.is_ge, fill=LOWEST, base=-S,
                               pattern=[[1, P]], channel_multiplier=0).then_inc(s_consts, 1)
            for u in range(16):
                pool.wait_ge(s_s1_sum, u + 1)
                v = scr1[u % 2][:, :].rearrange("p (h k) -> p h k", h=GH)
                pool.tensor_tensor(v, v, rs[:, 4 * u:4 * u + 4].unsqueeze(2).to_broadcast([P, GH, P]),
                                   ALU.mult).then_inc(s_s1_norm, 1)
            with pool.Fori(0, NT) as tp:
                for j in range(2):
                    b = tp * 2 + j
                    for u in range(8):
                        pool.wait_ge(s_s2_sum, b * 8 + (u + 1))
                        pool.tensor_tensor(prob[u % 2][:, :], prob[u % 2][:, :],
                                           rs[:, u:u + 1].to_broadcast([P, SC]), ALU.mult).then_inc(s_s2_norm, 1)
                pool.wait_ge(s_dt_ready, tp + 1)
                pool.tensor_tensor(dt_x[:, :], dt_z[:, :], x2T[:, :], ALU.mult).then_inc(s_dtx_ready, 1)
                dt3 = dt_z[:, :].rearrange("p (c n) -> p c n", c=KC)
                dx3 = dt_x[:, :].rearrange("p (c n) -> p c n", c=KC)
                for c in range(KC):
                    if c:
                        pool.wait_ge(s_scan_done, tp * KC + c)
                    pool.tensor_tensor(decay[:, :, :], a_pos[:, c, :].unsqueeze(2).to_broadcast([P, NS, P]),
                                       dt3[:, c, :].unsqueeze(1).to_broadcast([P, NS, P]), ALU.mult).then_inc(s_decay_arg, 1)
                    if c == 0:
                        pool.wait_ge(s_b_in, tp * 16 + 16)
                        pool.wait_ge(s_dtx_ready, tp + 1)
                    else:
                        pool.wait_ge(s_y_ready, tp * KC + c)
                    pool.tensor_tensor(drive[:, :, :], dx3[:, c, :].unsqueeze(1).to_broadcast([P, NS, P]),
                                       b_bc[:, :, :], ALU.mult).then_inc(s_drive_ready, 1)
                    if c == 0:
                        pool.wait_ge(s_c_in, tp * 16 + 16)
                    pool.wait_ge(s_scan_done, tp * KC + (c + 1))
                    pool.tensor_tensor(drive[:, :, :], drive[:, :, :], c_bc[:, :, :], ALU.mult).then_inc(s_hc_ready, 1)

            pool.wait_ge(s_y_ready, NT * KC)
            pool.memset(ones, 1.0).then_inc(s_ones_ready, 1)

            def weigh(k, j):
                pool.wait_ge(wb_in[j], k * 16 + 16)
                for i in range(IC):
                    pool.wait_ge(s_silu_done, k * 4 + (2 * j + i + 1))
                    pool.tensor_tensor(silu[i][:, :], silu[i][:, :], w_bc[j], ALU.mult).then_inc(s_gated, 1)

            with pool.Fori(0, NU // 2 - 1) as k:
                for j in range(2):
                    weigh(k, j)
            for j in range(2):
                weigh(NU // 2 - 1, j)

        @block.scalar
        def _(act):
            act.preload_act_table_set("natural_log_exp_and_others")
            def split_weight(n):
                act.wait_ge(w_in[n % 2], 16 * (n // 2 + 1))
                if n == WQ2:
                    act.wait_ge(s_p1_ready, 12)
                if n == WK2:
                    act.wait_ge(s_p1_ready, 4)
                if n == WV2:
                    act.wait_ge(s_p1_ready, 8)
                act.activation(w_of[n][0].rearrange("p k n -> p (k n)"), raw[n % 2][:, :], ACT.Copy).then_inc(s_w_hi, 1)

            def rstd(ve, r0, tmpv, waited, count, sem_out, step):
                act.wait_ge(waited, count)
                act.activation(tmpv, ve, ACT.Ln).then_inc(step, 1)
                act.wait_ge(step, count)
                act.activation(r0, tmpv, ACT.Exp, scale=-0.5).then_inc(sem_out, 1)

            split_weight(WQ1)
            rstd(ln[:, 0, :], ln[:, 1, :], ln[:, 2, :], s_ln_ve, 1, s_ln_r0, s_ln_step)
            split_weight(WK1)
            for kc in range(KC):
                act.wait_ge(s_xnT_ready, NT)
                act.activation(xT[0][:, kc, :], bank[kc][:, :], ACT.Copy).then_inc(s_xT_hi, 1)
            split_weight(WV1)
            split_weight(WO1)
            act.wait_ge(s_small_in, 64)
            act.activation(a_pos[:, :, :], smallp[:, ALOG:ALOG + KC * NS].rearrange("p (c n) -> p c n", c=KC),
                           ACT.Exp).then_inc(s_a_ready, 1)
            for n in (8, 9, 10, 11):
                act.wait_ge(s_p1_ready, n + 1)
                act.activation(v1[:, n - 8, :], bank[n % 8][:, :], ACT.Copy).then_inc(s_p1_out, 1)
            split_weight(WQ2)
            split_weight(WK2)

            def exp1(u):
                act.wait_ge(s_s1_max, u + 1)
                for g in range(GH):
                    e = act.activation(scr1[u % 2][:, g * P:(g + 1) * P], scr1[u % 2][:, g * P:(g + 1) * P], ACT.Exp,
                                       bias=nm[:, 8 * (u % 2) + g:8 * (u % 2) + g + 1], accum_out=sm[:, 4 * u + g:4 * u + g + 1])
                e.then_inc(s_s1_exp, 1)

            def pt1(u):
                act.wait_ge(s_s1_T, u + 1)
                if u >= 2:
                    act.wait_ge(s_s1_pv, u - 1)
                act.activation(prob[u % 2][:, :], bank[2 + u % 2][:, :], ACT.Copy).then_inc(s_s1_pT, 1)
            def o1_hi(t):
                act.wait_ge(s_o1_sum, t + 1)
                act.activation(o1T[0][:, :, t * P:(t + 1) * P], tmp[2 + t % 2][:, :].rearrange("p (g n) -> p g n", g=KC),
                               ACT.Copy).then_inc(s_o1_hi, 1)

            exp1(0)
            exp1(1)
            for u in range(16):
                pt1(u)
                if u + 2 < 16:
                    exp1(u + 2)
                if u % 4 == 1 and u > 4:
                    o1_hi(u // 4 - 1)
            o1_hi(3)
            for m in range(KC):
                act.wait_ge(s_h_ready, m + 1)
                act.activation(hT[0][:, m, :], bank[m][:, :], ACT.Identity, bias=bias(BO1 + m)).then_inc(s_h_hi, 1)
            split_weight(WV2)
            act.wait_ge(s_q2_out, KC)
            for n in range(2):
                act.nop().then_inc(s_s2_exp, 1)

            def hi_kv(b, k):
                act.wait_ge(s_kv_ready, b * 8 + (k + 1))
                if k < 4:
                    act.activation(k2[0][:, k, :], bank[k % 2][:, :], ACT.Identity, bias=bias(BK2 + k)).then_inc(s_kv_hi, 1)
                else:
                    act.activation(v2[0][:, k - 4, :], bank[k % 2][:, :], ACT.Copy).then_inc(s_kv_hi, 1)

            def exp2(b, u):
                act.wait_ge(s_s2_max, b * 8 + (u + 1))
                act.wait_ge(s_s2_T, b * 8 + (u + 1))
                act.activation(prob[u % 2][:, :], bank[2 + u % 2][:, :], ACT.Exp, bias=nm[:, u:u + 1],
                               accum_out=sm[:, u:u + 1]).then_inc(s_s2_exp, 1)

            with act.Fori(0, NT) as tp:
                for j in range(2):
                    b = tp * 2 + j
                    act.wait_ge(ctx_in[j], tp * 16 + 16)
                    act.activation(ctxT[0].rearrange("p k n -> p (k n)"), raw[j][:, :], ACT.Copy).then_inc(s_ctx_hi, 1)
                    hi_kv(b, 0)
                    for i in range(GH):
                        act.activation(qb[0][HD * i:HD * (i + 1), :, i // 2, (i % 2) * S:(i % 2 + 1) * S],
                                       q2[HD * i:HD * (i + 1), :, bass.ds(b * S, S)], ACT.Copy).then_inc(s_qb_hi, 1)
                    for k in range(1, 8):
                        hi_kv(b, k)
                    exp2(b, 0)
                    exp2(b, 1)
                    for u in range(8):
                        act.wait_ge(s_s2_T, b * 8 + (u + 3))
                        if u >= 2 and u % 2 == 0:
                            act.wait_ge(s_pv_ready, b * 4 + u // 2)
                        act.activation(pT[0][:, :, (u % 2) * P:(u % 2 + 1) * P],
                                       bank[4 + u % 2][:, :].rearrange("p (c n) -> p c n", c=4), ACT.Copy).then_inc(s_pT_hi, 1)
                        if u + 2 < 8:
                            exp2(b, u + 2)
                rstd(ln[:, 0, 0:1], ln[:, 1, 0:1], ln[:, 2, 0:1], s_ln2_ve, tp + 1, s_ln2_r0, s_ln2_step)
                act.wait_ge(s_x2T_ready, tp + 1)
                act.activation(x2T[:, :], bank[6][:, :], ACT.Copy).then_inc(s_x2T_out, 1)
                act.wait_ge(s_xp_ready, tp + 1)
                act.activation(bc_sb[:, :], bank[7][0:2 * NS, 0:P], ACT.Copy).then_inc(s_bc_ready, 1)
                act.activation(dtr[:, :], bank[7][0:RANK, P:2 * P], ACT.Copy).then_inc(s_dtr_ready, 1)
                act.wait_ge(s_dt_z_ready, tp + 1)
                act.activation(dt_e[:, :], dt_z[:, :], ACT.Abs).then_inc(s_dt_step, 1)
                act.wait_ge(s_dt_step, tp * 3 + 1)
                act.activation(dt_e[:, :], dt_e[:, :], ACT.Exp, scale=-1.0).then_inc(s_dt_step, 1)
                act.wait_ge(s_dt_step, tp * 3 + 2)
                act.activation(dt_e[:, :], dt_e[:, :], ACT.Ln, bias=1.0).then_inc(s_dt_step, 1)
                for c in range(KC):
                    act.wait_ge(s_decay_arg, tp * KC + (c + 1))
                    act.activation(decay[:, :, :], decay[:, :, :], ACT.Exp, scale=-1.0).then_inc(s_decay_exp, 1)

            rstd(ln[:, 0, :], ln[:, 1, :], ln[:, 2, :], s_ln3_ve, 1, s_ln3_r0, s_ln3_step)
            act.wait_ge(s_gate_in, 32)
            act.activation(gw[0][:, :, :], gw_raw[:, :, :], ACT.Copy).then_inc(s_gw_hi, 1)

            def hi_gu(k, j):
                act.wait_ge(gu_in[j], k * 16 + 16)
                act.activation(gu_w[j][0], raw[j][:, :], ACT.Copy).then_inc(s_gu_hi, 1)

            def hi_dn(k, j):
                act.wait_ge(dn_in[j], k * 16 + 16)
                act.activation(dn_w[j][0], raw_dn[j], ACT.Copy).then_inc(s_dn_hi, 1)

            def silus(k, j):
                for i in range(IC):
                    act.wait_ge(s_gu_ready, k * 4 + (2 * j + i + 1))
                    act.activation(silu[i][:, :], bank[2 * i][:, :], ACT.Silu).then_inc(s_silu_done, 1)
                for i in range(IC):
                    act.wait_ge(s_h_ready2, k * 4 + (2 * j + i + 1))
                    act.activation(inner[j][0][:, i, :], act_f[i][:, :], ACT.Copy).then_inc(s_h_hi2, 1)

            for kc in range(KC):
                act.wait_ge(s_xn3T_ready, NT)
                act.activation(xT[0][:, kc, :], bank[kc][:, :], ACT.Copy).then_inc(s_x3_hi, 1)
            hi_gu(0, 0)
            hi_gu(0, 1)
            hi_dn(0, 0)
            act.wait_ge(s_logit_ready, 1)
            act.activation(rt[:, 0, :, :], bank[4][:, 0:NT * E].rearrange("p (t e) -> p t e", t=NT), ACT.Exp, scale=-1.0).then_inc(s_r_exp, 1)
            act.wait_ge(s_wT_ready, 1)
            act.activation(wT_sb, bank[5][0:E, :], ACT.Copy).then_inc(s_wT_out, 1)
            with act.Fori(0, NU // 2 - 1) as k:
                for j in range(2):
                    silus(k, j)
                    hi_gu(k + 1, j)
                    act.wait_ge(s_moe_done, k * 2 + (j + 1))
                    hi_dn(k + j, 1 - j)
            silus(NU // 2 - 1, 0)
            act.wait_ge(s_moe_done, NU - 1)
            hi_dn(NU // 2 - 1, 1)
            silus(NU // 2 - 1, 1)

        @block.vector
        def _(dve):
            for n in range(2):
                dve.nop().then_inc(s_kv_lo, 1)
            for n in range(2):
                dve.nop().then_inc(s_pT_lo, 1)
            for n in range(2):
                dve.nop().then_inc(s_o2_out, 1)
            for n in range(2):
                dve.nop().then_inc(s_ctx_lo, 1)

            def lo_weight(n):
                dve.wait_ge(s_w_hi, n + 1)
                dve.tensor_tensor(w_of[n][1].rearrange("p k n -> p (k n)"), raw[n % 2][:, :],
                                  w_of[n][0].rearrange("p k n -> p (k n)").bitcast(fp32), ALU.subtract).then_inc(s_w_lo, 1)

            def newton(ve, r0, a, r, waited, count, step, base):
                dve.wait_ge(waited, count)
                dve.tensor_tensor(a, r0, r0, ALU.mult).then_inc(step, 1)
                dve.wait_ge(step, base + 1)
                dve.tensor_tensor(a, a, ve, ALU.mult).then_inc(step, 1)
                dve.wait_ge(step, base + 2)
                dve.tensor_scalar(a, a, -0.5, 1.5, ALU.mult, ALU.add).then_inc(step, 1)
                dve.wait_ge(step, base + 3)
                dve.tensor_tensor(r, a, r0, ALU.mult).then_inc(step, 1)
                dve.wait_ge(step, base + 4)

            dve.wait_ge(s_x_in, 16)
            for t in range(NT):
                dve.bn_stats(st[:, t, :], x_tok[:, t, :]).then_inc(s_xn_ready, 1)
            dve.wait_ge(s_xn_ready, 4)
            for t in range(NT):
                dve.bn_aggr(mv[:, t, :], st[:, t, :]).then_inc(s_xn_ready, 1)
            dve.wait_ge(s_xn_ready, 8)
            dve.tensor_scalar(ln[:, 0, :], mv[:, :, 1], EPS, None, ALU.add).then_inc(s_ln_ve, 1)
            lo_weight(WQ1)
            dve.wait_ge(s_ln_ve, 1)
            newton(ln[:, 0, :], ln[:, 1, :], ln[:, 3, :], ln[:, 4, :], s_ln_r0, 1, s_xn_ready, 8)
            for t in range(NT):
                dve.tensor_scalar(xn_all[:, t, :], x_tok[:, t, :], mv[:, t, 0:1], ln[:, 4, t:t + 1],
                                  ALU.subtract, ALU.mult).then_inc(s_xn_ready, 1)
            lo_weight(WK1)
            for kc in range(KC):
                dve.wait_ge(s_xT_hi, kc + 1)
                dve.tensor_tensor(xT[1][:, kc, :], bank[kc][:, :], xT[0][:, kc, :].bitcast(fp32), ALU.subtract).then_inc(s_xT_lo, 1)
            dve.wait_ge(s_small_in, 64)
            for t in range(NT):
                dve.tensor_tensor(x_tok[:, t, :], x_tok[:, t, :], bo2_bc[:, :], ALU.add).then_inc(s_x1_done, 1)
            lo_weight(WV1)
            for n in range(8):
                dve.wait_ge(s_p1_ready, n + 1)
                if n < 4:
                    dve.tensor_scalar(q1[:, n, :], bank[4 + n][:, :], bias(BQ1 + n), QSCALE, ALU.add, ALU.mult).then_inc(s_s1_out, 1)
                else:
                    dve.tensor_scalar(k1[:, n - 4, :], bank[n - 4][:, :], bias(BK1 + n - 4), None, ALU.add).then_inc(s_s1_out, 1)
            lo_weight(WO1)
            lo_weight(WQ2)
            lo_weight(WK2)

            def soft1(u):
                dve.wait_ge(s_s1_ready, u + 1)
                dve.tensor_tensor(scr1[u % 2][:, :].rearrange("p (h k) -> p h k", h=GH),
                                  bank[u % 2][:, :].rearrange("p (h k) -> p h k", h=GH),
                                  mask[:, :].unsqueeze(1).to_broadcast([P, GH, P]), ALU.add).then_inc(s_s1_out, 1)
                dve.wait_ge(s_s1_out, 8 + u + 1)
                dve.tensor_reduce(nm[:, 8 * (u % 2):8 * (u % 2) + 4], scr1[u % 2][:, :].rearrange("p (h k) -> p h k", h=GH),
                                  AX.X, ALU.max, negate=True).then_inc(s_s1_max, 1)

            def recip1(u):
                dve.wait_ge(s_s1_exp, u + 1)
                dve.reciprocal(rs[:, 4 * u:4 * u + 4], sm[:, 4 * u:4 * u + 4]).then_inc(s_s1_sum, 1)

            def o1_tile(t):
                dve.wait_ge(s_s1_pv, 4 * t + 4)
                if t >= 2:
                    dve.wait_ge(s_o1_lo, t - 1)
                dve.tensor_tensor(tmp[2 + t % 2][:, :].rearrange("p (g n) -> p g n", g=KC),
                                  bank[4 + t % 2][:, :].rearrange("p (g n) -> p g n", g=KC),
                                  smallp[:, BV1:BV1 + KC].unsqueeze(2).to_broadcast([P, KC, P]), ALU.add).then_inc(s_o1_sum, 1)
                dve.wait_ge(s_o1_hi, t + 1)
                dve.tensor_tensor(o1T[1][:, :, t * P:(t + 1) * P], tmp[2 + t % 2][:, :].rearrange("p (g n) -> p g n", g=KC),
                                  o1T[0][:, :, t * P:(t + 1) * P].bitcast(fp32), ALU.subtract).then_inc(s_o1_lo, 1)

            soft1(0)
            soft1(1)
            recip1(0)
            for u in range(16):
                if u + 1 < 16:
                    recip1(u + 1)
                if u + 2 < 16:
                    dve.wait_ge(s_s1_T, u + 1)
                    soft1(u + 2)
                if u % 4 == 1 and u > 4:
                    o1_tile(u // 4 - 1)
            o1_tile(3)
            for m in range(KC):
                dve.wait_ge(s_h_hi, m + 1)
                dve.scalar_tensor_tensor(hT[1][:, m, :], bank[m][:, :], bias(BO1 + m), hT[0][:, m, :].bitcast(fp32),
                                         ALU.add, ALU.subtract).then_inc(s_h_lo, 1)
            for m in range(KC):
                dve.wait_ge(s_q2_ready, m + 1)
                dve.tensor_scalar(q2[:, m, :], bank[4 + m][:, :], bias(BQ2 + m), QSCALE, ALU.add, ALU.mult).then_inc(s_q2_out, 1)
            for n in range(2):
                dve.memset(qb[n].rearrange("p g h q -> p (g h q)").bitcast(fp32), 0.0).then_inc(s_consts, 1)
            lo_weight(WV2)

            def lo_kv(b, k):
                dve.wait_ge(s_kv_hi, b * 8 + (k + 1))
                if k < 4:
                    dve.scalar_tensor_tensor(k2[1][:, k, :], bank[k % 2][:, :], bias(BK2 + k), k2[0][:, k, :].bitcast(fp32),
                                             ALU.add, ALU.subtract).then_inc(s_kv_lo, 1)
                else:
                    dve.tensor_tensor(v2[1][:, k - 4, :], bank[k % 2][:, :], v2[0][:, k - 4, :].bitcast(fp32),
                                      ALU.subtract).then_inc(s_kv_lo, 1)

            def max2(b, u):
                dve.wait_ge(s_s2_ready, b * 8 + (u + 1))
                dve.tensor_reduce(nm[:, u:u + 1], bank[2 + u % 2][:, :], AX.X, ALU.max, negate=True).then_inc(s_s2_max, 1)

            def recip2(b, u):
                dve.wait_ge(s_s2_exp, b * 8 + (u + 3))
                dve.reciprocal(rs[:, u:u + 1], sm[:, u:u + 1]).then_inc(s_s2_sum, 1)

            def o2_group(b, j, g):
                dve.wait_ge(s_pv_ready, b * 4 + (g + 1))
                for i in range(GH):
                    last = dve.tensor_scalar(
                        o2f[HD * i:HD * (i + 1), g * P + j * S:g * P + (j + 1) * S],
                        bank[6 + g % 2][HD * i:HD * (i + 1), i * S:(i + 1) * S],
                        smallp[HD * i:HD * (i + 1), BV2 + g:BV2 + g + 1], None, ALU.add)
                last.then_inc(s_o2_out, 1)

            with dve.Fori(0, NT) as tp:
                for j in range(2):
                    b = tp * 2 + j
                    dve.wait_ge(s_ctx_hi, b + 1)
                    dve.tensor_tensor(ctxT[1].rearrange("p k n -> p (k n)"), raw[j][:, :],
                                      ctxT[0].rearrange("p k n -> p (k n)").bitcast(fp32), ALU.subtract).then_inc(s_ctx_lo, 1)
                    lo_kv(b, 0)
                    for i in range(GH):
                        dve.wait_ge(s_qb_hi, b * 4 + (i + 1))
                        dve.tensor_tensor(qb[1][HD * i:HD * (i + 1), :, i // 2, (i % 2) * S:(i % 2 + 1) * S],
                                          q2[HD * i:HD * (i + 1), :, bass.ds(b * S, S)],
                                          qb[0][HD * i:HD * (i + 1), :, i // 2, (i % 2) * S:(i % 2 + 1) * S].bitcast(fp32),
                                          ALU.subtract).then_inc(s_qb_lo, 1)
                    for k in range(1, 8):
                        lo_kv(b, k)
                    max2(b, 0)
                    recip2(b, 0)
                    max2(b, 1)
                    recip2(b, 1)
                    for u in range(8):
                        if u + 2 < 8:
                            max2(b, u + 2)
                        dve.wait_ge(s_pT_hi, b * 8 + (u + 1))
                        dve.tensor_tensor(pT[1][:, :, (u % 2) * P:(u % 2 + 1) * P],
                                          bank[4 + u % 2][:, :].rearrange("p (c n) -> p c n", c=4),
                                          pT[0][:, :, (u % 2) * P:(u % 2 + 1) * P].bitcast(fp32), ALU.subtract).then_inc(s_pT_lo, 1)
                        if u + 2 < 8:
                            recip2(b, u + 2)
                        if u >= 2 and u % 2 == 0:
                            o2_group(b, j, u // 2 - 1)
                    o2_group(b, j, 3)
                xt = x_tok[:, bass.ds(tp, 1), :].rearrange("p a n -> p (a n)")
                dve.wait_ge(s_wo2_ready, tp + 1)
                dve.tensor_tensor(x1s[:, :], xt, bank[6][:, :], ALU.add).then_inc(s_x1_done, 1)
                dve.wait_ge(s_x1_done, tp + 5)
                dve.bn_stats(st[:, 0, :], x1s[:, :]).then_inc(s_xn2_ready, 1)
                dve.wait_ge(s_xn2_ready, tp * 6 + 1)
                half = st[:, 1, :]
                dve.tensor_tensor(half[:, 0:3], st[:, 0, 0:3], st[:, 0, 3:6], ALU.add).then_inc(s_ln2_stat, 1)
                dve.tensor_tensor(half[:, 3:4], st[:, 0, 1:2], st[:, 0, 4:5], ALU.subtract).then_inc(s_ln2_stat, 1)
                dve.wait_ge(s_ln2_stat, tp * 5 + 2)
                dve.tensor_scalar(mv[:, 0, 0:1], half[:, 1:2], 0.5, None, ALU.mult).then_inc(s_ln2_stat, 1)
                dve.tensor_scalar(half[:, 4:5], half[:, 2:3], 1.0 / D, EPS, ALU.mult, ALU.add).then_inc(s_ln2_stat, 1)
                dve.scalar_tensor_tensor(half[:, 5:6], half[:, 3:4], 0.25, half[:, 3:4], ALU.mult, ALU.mult).then_inc(s_ln2_stat, 1)
                dve.wait_ge(s_ln2_stat, tp * 5 + 5)
                dve.tensor_tensor(ln[:, 0, 0:1], half[:, 4:5], half[:, 5:6], ALU.add).then_inc(s_ln2_ve, 1)
                newton(ln[:, 0, 0:1], ln[:, 1, 0:1], ln[:, 3, 0:1], ln[:, 4, 0:1], s_ln2_r0, tp + 1, s_xn2_ready, tp * 6 + 1)
                dve.tensor_scalar(xn2[:, :], x1s[:, :], mv[:, 0, 0:1], ln[:, 4, 0:1], ALU.subtract, ALU.mult).then_inc(s_xn2_ready, 1)
                dve.wait_ge(s_dtp_ready, tp + 1)
                dve.tensor_tensor(dt_z[:, :].rearrange("p (c n) -> p c n", c=KC), bank[6][:, :].rearrange("p (c n) -> p c n", c=KC),
                                  smallp[:, BDT:BDT + KC].unsqueeze(2).to_broadcast([P, KC, P]), ALU.add).then_inc(s_dt_z_ready, 1)
                dve.wait_ge(s_dt_step, tp * 3 + 3)
                dve.scalar_tensor_tensor(dt_z[:, :], dt_z[:, :], 0.0, dt_e[:, :], ALU.max, ALU.add).then_inc(s_dt_ready, 1)
                for c in range(KC):
                    dve.wait_ge(s_decay_exp, tp * KC + (c + 1))
                    dve.memset(decay[:, :, 0:P:S], 0.0).then_inc(s_decay_zero, 1)
                    dve.wait_ge(s_decay_zero, tp * KC + (c + 1))
                    dve.wait_ge(s_drive_ready, tp * KC + (c + 1))
                    flat = drive[:, :, :].rearrange("p s n -> p (s n)")
                    dve.tensor_tensor_scan(flat, decay[:, :, :].rearrange("p s n -> p (s n)"), flat, 0.0,
                                           ALU.mult, ALU.add).then_inc(s_scan_done, 1)
                    dve.wait_ge(s_hc_ready, tp * KC + (c + 1))
                    dve.tensor_reduce(yT[:, c * P:(c + 1) * P], drive[:, :, :].rearrange("p s n -> p n s"),
                                      AX.X, ALU.add).then_inc(s_y_ready, 1)
                dve.wait_ge(s_yT_ready, tp + 1)
                dve.tensor_tensor(xt, x1s[:, :], bank[7][:, :], ALU.add).then_inc(s_x2_done, 1)

            dve.wait_ge(s_x2_done, NT)
            for t in range(NT):
                dve.bn_stats(st[:, t, :], x_tok[:, t, :]).then_inc(s_ln3, 1)
            dve.wait_ge(s_ln3, NT)
            for t in range(NT):
                dve.bn_aggr(mv[:, t, :], st[:, t, :]).then_inc(s_ln3, 1)
            dve.wait_ge(s_ln3, 2 * NT)
            dve.tensor_scalar(ln[:, 0, :], mv[:, :, 1], EPS, None, ALU.add).then_inc(s_ln3_ve, 1)
            newton(ln[:, 0, :], ln[:, 1, :], ln[:, 3, :], ln[:, 4, :], s_ln3_r0, 1, s_ln3, 2 * NT)
            for t in range(NT):
                dve.tensor_scalar(xn_all[:, t, :], x_tok[:, t, :], mv[:, t, 0:1], ln[:, 4, t:t + 1],
                                  ALU.subtract, ALU.mult).then_inc(s_xn3_ready, 1)
            dve.wait_ge(s_gw_hi, 1)
            dve.tensor_tensor(gw[1][:, :, :], gw_raw[:, :, :], gw[0][:, :, :].bitcast(fp32), ALU.subtract).then_inc(s_gw_lo, 1)
            for kc in range(KC):
                dve.wait_ge(s_x3_hi, kc + 1)
                dve.tensor_tensor(xT[1][:, kc, :], bank[kc][:, :], xT[0][:, kc, :].bitcast(fp32), ALU.subtract).then_inc(s_x3_lo, 1)

            def lo_gu(k, j):
                dve.wait_ge(s_gu_hi, k * 2 + (j + 1))
                dve.tensor_tensor(gu_w[j][1], raw[j][:, :], gu_w[j][0].bitcast(fp32), ALU.subtract).then_inc(s_gu_lo, 1)

            def lo_dn(e, j):
                dve.wait_ge(s_dn_hi, e + 1)
                dve.tensor_tensor(dn_w[j][1], raw_dn[j], dn_w[j][0].bitcast(fp32), ALU.subtract).then_inc(s_dn_lo, 1)

            lo_gu(0, 0)
            lo_gu(0, 1)
            lo_dn(0, 0)

            steps = [0]

            def link(ins):
                steps[0] += 1
                ins.then_inc(s_r_step, 1)
                dve.wait_ge(s_r_step, steps[0])

            sg, sc, ch, mk, wt = [rt[:, n, :, :] for n in range(5)]
            gs, c1, rank, gm = [grp[:, n, :, :] for n in range(4)]
            dve.wait_ge(s_r_exp, 1)
            link(dve.tensor_scalar(sg, sg, 1.0, None, ALU.add))
            link(dve.reciprocal(sc, sg))
            link(dve.tensor_tensor(ch, sc, gb_bc[:, :].unsqueeze(1).to_broadcast([P, NT, E]), ALU.add))
            for t in range(NT):
                for g in range(NG):
                    last = dve.max(top[:, t, g, :], ch[:, t, g * EG:(g + 1) * EG])
            link(last)
            link(dve.tensor_tensor(gs, top[:, :, :, 0], top[:, :, :, 1], ALU.add))
            for g in range(NG):
                last = dve.memset(rank[:, :, g:g + 1], float(g))
            link(last)
            for d in range(1, NG):
                link(dve.tensor_tensor(c1[:, :, 0:NG - d], gs[:, :, d:NG], gs[:, :, 0:NG - d], ALU.is_gt))
                link(dve.tensor_tensor(rank[:, :, 0:NG - d], rank[:, :, 0:NG - d], c1[:, :, 0:NG - d], ALU.add))
                link(dve.tensor_tensor(rank[:, :, d:NG], rank[:, :, d:NG], c1[:, :, 0:NG - d], ALU.subtract))
            link(dve.tensor_scalar(gm, rank, 1.5, None, ALU.is_lt))
            link(dve.tensor_tensor(mk.rearrange("p t (g e) -> p t g e", g=NG), ch.rearrange("p t (g e) -> p t g e", g=NG),
                                   gm.unsqueeze(3).to_broadcast([P, NT, NG, EG]), ALU.mult))
            for t in range(NT):
                last = dve.max(top8[:, t, :], mk[:, t, :])
            link(last)
            for t in range(NT):
                last = dve.match_replace(wt[:, t, :], top8[:, t, :], mk[:, t, :], LOWEST)
            link(last)
            link(dve.tensor_tensor(wt, wt, mk, ALU.not_equal))
            link(dve.tensor_tensor(wt, wt, sc, ALU.mult))
            link(dve.tensor_reduce(rsum[:, :], wt, AX.X, ALU.add))
            link(dve.tensor_scalar(rsum[:, :], rsum[:, :], 1e-20, None, ALU.add))
            link(dve.reciprocal(rsum[:, :], rsum[:, :]))
            link(dve.tensor_tensor(wt, wt, rsum[:, :].unsqueeze(2).to_broadcast([P, NT, E]), ALU.mult))
            dve.tensor_scalar(wt, wt, ROUTED_SCALING, None, ALU.mult).then_inc(s_w_ready, 1)

            def gates(k, j):
                for i in range(IC):
                    dve.wait_ge(s_gated, k * 4 + (2 * j + i + 1))
                    dve.tensor_tensor(act_f[i][:, :], silu[i][:, :], bank[2 * i + 1][:, :], ALU.mult).then_inc(s_h_ready2, 1)
                for i in range(IC):
                    dve.wait_ge(s_h_hi2, k * 4 + (2 * j + i + 1))
                    dve.tensor_tensor(inner[j][1][:, i, :], act_f[i][:, :], inner[j][0][:, i, :].bitcast(fp32),
                                      ALU.subtract).then_inc(s_h_lo2, 1)

            with dve.Fori(0, NU // 2 - 1) as k:
                for j in range(2):
                    gates(k, j)
                    lo_gu(k + 1, j)
                    lo_dn(k * 2 + (j + 1), 1 - j)
                    dve.wait_ge(s_h_lo2, k * 4 + (2 * j + 2))
            gates(NU // 2 - 1, 0)
            lo_dn(NU - 1, 1)
            dve.wait_ge(s_h_lo2, 2 * NU - 2)
            gates(NU // 2 - 1, 1)
            for t in range(NT):
                dve.wait_ge(s_moe_done, NU + 1)
                dve.tensor_tensor(x_tok[:, t, :], x_tok[:, t, :], bank[4 + t][:, :], ALU.add).then_inc(s_x3_done, 1)

        @block.tensor
        def _(pe):
            def mm3(o, w, xx, first, last):
                pe.matmul(o, w[1], xx[0], start=first, stop=False)
                pe.matmul(o, w[0], xx[1], start=False, stop=False)
                return pe.matmul(o, w[0], xx[0], start=False, stop=last)

            def project(o, w, xx, m):
                for kc in range(KC):
                    mm = mm3(o, [w[k][:, kc, m * P:(m + 1) * P] for k in range(2)],
                             [xx[k][:, kc, :] for k in range(2)], kc == 0, kc == KC - 1)
                return mm

            for n in range(2):
                pe.nop().then_inc(s_s2_T, 1)
            pe.wait_ge(s_consts, 6)
            for t in range(NT):
                pe.wait_ge(s_xn_ready, 12 + t + 1)
                for kc in range(KC):
                    mm = pe.transpose(bank[kc][:, t * P:(t + 1) * P], xn_all[:, t, kc * P:(kc + 1) * P], ident[:, :])
                mm.then_inc(s_xnT_ready, 1)
            pe.wait_ge(s_w_lo, 1)
            pe.wait_ge(s_xT_lo, 4)
            for m in range(KC):
                project(bank[4 + m][:, :], w_of[WQ1], xT, m).then_inc(s_p1_ready, 1)
            pe.wait_ge(s_w_lo, 2)
            for m in range(KC):
                project(bank[m][:, :], w_of[WK1], xT, m).then_inc(s_p1_ready, 1)
            pe.wait_ge(s_w_lo, 3)
            for t in range(NT):
                pe.wait_ge(s_s1_out, t + 5)
                project(bank[t][:, :], xT, w_of[WV1], t).then_inc(s_p1_ready, 1)

            def scores1(u):
                t, i = divmod(u, 4)
                if u < 2:
                    pe.wait_ge(s_p1_out, 4)
                if u >= 2:
                    pe.wait_ge(s_s1_out, 8 + u - 1)
                r = slice(HD * i, HD * (i + 1))
                for g in range(KC):
                    mm = pe.matmul(bank[u % 2][:, g * P:(g + 1) * P], q1[r, g, t * P:(t + 1) * P], k1[r, g, t * P:(t + 1) * P],
                                   start=True, stop=True)
                mm.then_inc(s_s1_ready, 1)

            def transpose1(u):
                pe.wait_ge(s_s1_norm, u + 1)
                if u >= 2:
                    pe.wait_ge(s_s1_pT, u - 1)
                for g in range(KC):
                    mm = pe.transpose(bank[2 + u % 2][:, g * P:(g + 1) * P], scr1[u % 2][:, g * P:(g + 1) * P], ident[:, :])
                mm.then_inc(s_s1_T, 1)

            def pv1(u):
                t, i = divmod(u, 4)
                pe.wait_ge(s_s1_pT, u + 1)
                if t >= 2 and i == 0:
                    pe.wait_ge(s_o1_sum, t - 1)
                for g in range(KC):
                    c = g * P + HD * i
                    mm = pe.matmul(bank[4 + t % 2][HD * i:HD * (i + 1), g * P:(g + 1) * P], v1[:, t, c:c + HD],
                                   prob[u % 2][:, g * P:(g + 1) * P], start=True, stop=True)
                mm.then_inc(s_s1_pv, 1)

            scores1(0)
            scores1(1)
            for u in range(16):
                transpose1(u)
                if u + 2 < 16:
                    scores1(u + 2)
                pv1(u)
            pe.wait_ge(s_w_lo, 4)
            pe.wait_ge(s_o1_lo, NT)
            for m in range(KC):
                project(bank[m][:, :], w_of[WO1], o1T, m).then_inc(s_h_ready, 1)
            pe.wait_ge(s_w_lo, 5)
            pe.wait_ge(s_h_lo, KC)
            for m in range(KC):
                project(bank[4 + m][:, :], w_of[WQ2], hT, m).then_inc(s_q2_ready, 1)
            pe.wait_ge(s_w_lo, N_W)
            pe.wait_ge(s_wo2_in, 16)

            def scores2(b, u):
                pe.wait_ge(s_s2_exp, b * 8 + (u + 1))
                g, h = divmod(u, 2)
                mm3(bank[2 + u % 2][:, :], [qb[k][:, g, h, :] for k in range(2)], [k2[k][:, g, :] for k in range(2)],
                    True, True).then_inc(s_s2_ready, 1)

            def transpose2(b, u):
                pe.wait_ge(s_s2_norm, b * 8 + (u + 1))
                pe.wait_ge(s_pT_lo, b * 8 + (u + 1))
                for c in range(4):
                    mm = pe.transpose(bank[4 + u % 2][:, c * P:(c + 1) * P], prob[u % 2][:, c * P:(c + 1) * P], ident[:, :])
                mm.then_inc(s_s2_T, 1)

            def pv2(b, g):
                pe.wait_ge(s_pT_lo, b * 8 + (2 * g + 4))
                pe.wait_ge(s_o2_out, b * 4 + (g + 1))
                for c in range(4):
                    mm = mm3(bank[6 + g % 2][:, 0:2 * P], [v2[k][:, c, g * P:(g + 1) * P] for k in range(2)],
                             [pT[k][:, c, :] for k in range(2)], c == 0, c == 3)
                mm.then_inc(s_pv_ready, 1)

            with pe.Fori(0, NT) as tp:
                for j in range(2):
                    b = tp * 2 + j
                    pe.wait_ge(s_ctx_lo, b + 3)
                    for k in range(8):
                        pe.wait_ge(s_kv_lo, b * 8 + (k + 1))
                        if k < 4:
                            mm = project(bank[k % 2][:, :], w_of[WK2], ctxT, k)
                        else:
                            mm = project(bank[k % 2][:, :], ctxT, w_of[WV2], k - 4)
                        mm.then_inc(s_kv_ready, 1)
                    pe.wait_ge(s_qb_lo, b * 4 + 4)
                    pe.wait_ge(s_kv_lo, b * 8 + 10)
                    scores2(b, 0)
                    scores2(b, 1)
                    for u in range(8):
                        transpose2(b, u)
                        if u + 2 < 8:
                            scores2(b, u + 2)
                        if u >= 2 and u % 2 == 0:
                            pv2(b, u // 2 - 1)
                    pv2(b, 3)
                pe.wait_ge(s_o2_out, tp * 8 + 10)
                for kc in range(KC):
                    mm = pe.matmul(bank[6][:, :], o2f[:, kc * P:(kc + 1) * P], wo2[:, kc, :], start=kc == 0, stop=kc == KC - 1)
                mm.then_inc(s_wo2_ready, 1)
                pe.wait_ge(s_xn2_ready, tp * 6 + 6)
                for kc in range(KC):
                    mm = pe.transpose(bank[6][:, kc * P:(kc + 1) * P], xn2[:, kc * P:(kc + 1) * P], ident[:, :])
                mm.then_inc(s_x2T_ready, 1)
                pe.wait_ge(s_x2T_out, tp + 1)
                x3 = x2T[:, :].rearrange("p (k n) -> p k n", k=KC)
                for kc in range(KC):
                    pe.matmul(bank[7][0:2 * NS, 0:P], wxp[:, kc, 0:2 * NS], x3[:, kc, :], start=kc == 0, stop=kc == KC - 1)
                for kc in range(KC):
                    mm = pe.matmul(bank[7][0:RANK, P:2 * P], wxp[:, kc, 2 * NS:], x3[:, kc, :], start=kc == 0, stop=kc == KC - 1)
                mm.then_inc(s_xp_ready, 1)
                pe.wait_ge(s_dtr_ready, tp + 1)
                for c in range(KC):
                    mm = pe.matmul(bank[6][:, c * P:(c + 1) * P], wdt[:, c * P:(c + 1) * P], dtr[:, :], start=True, stop=True)
                mm.then_inc(s_dtp_ready, 1)
                pe.wait_ge(s_y_ready, tp * KC + KC)
                for c in range(KC):
                    mm = pe.transpose(bank[7][:, c * P:(c + 1) * P], yT[:, c * P:(c + 1) * P], ident[:, :])
                mm.then_inc(s_yT_ready, 1)

            for t in range(NT):
                pe.wait_ge(s_xn3_ready, t + 1)
                for kc in range(KC):
                    mm = pe.transpose(bank[kc][:, t * P:(t + 1) * P], xn_all[:, t, kc * P:(kc + 1) * P], ident[:, :])
                mm.then_inc(s_xn3T_ready, 1)
            pe.wait_ge(s_x3_lo, KC)
            pe.wait_ge(s_gw_lo, 1)
            for t in range(NT):
                for kc in range(KC):
                    mm = mm3(bank[4][:, t * E:(t + 1) * E], [xT[k][:, kc, t * P:(t + 1) * P] for k in range(2)],
                             [gw[k][:, kc, :] for k in range(2)], kc == 0, kc == KC - 1)
            mm.then_inc(s_logit_ready, 1)

            def gate_up(k, j, first=False):
                pe.wait_ge(s_gu_lo, k * 2 + (j + 1))
                w = [gu_w[j][n].rearrange("p (s c i) -> p s c i", s=2, c=KC) for n in range(2)]
                for i in range(IC):
                    if not first:
                        pe.wait_ge(s_h_ready2, k * 4 + (2 * j + i - 1))
                    for sel in range(2):
                        for kc in range(KC):
                            mm = mm3(bank[2 * i + sel][:, :], [w[n][:, sel, kc, i * P:(i + 1) * P] for n in range(2)],
                                     [xT[n][:, kc, :] for n in range(2)], kc == 0, kc == KC - 1)
                    mm.then_inc(s_gu_ready, 1)

            def down(e, j):
                pe.wait_ge(s_dn_lo, e + 1)
                pe.wait_ge(s_h_lo2, e * 2 + 2)
                w = [dn_w[j][n].rearrange("p (i d) -> p i d", i=IC) for n in range(2)]
                for t in range(NT):
                    for i in range(IC):
                        a = [inner[j][n][:, i, t * P:(t + 1) * P] for n in range(2)]
                        for aa, ww in ((a[1], w[0]), (a[0], w[1]), (a[0], w[0])):
                            mm = pe.matmul(bank[4 + t][:, :], aa, ww[:, i, :], start=False, stop=False, skip_group_check=True)
                mm.then_inc(s_moe_done, 1)

            gate_up(0, 0, True)
            pe.wait_ge(s_w_ready, 1)
            for t in range(NT):
                mm = pe.transpose(bank[5][0:E, t * P:(t + 1) * P], rt[:, 4, t, :], ident[:, :])
            mm.then_inc(s_wT_ready, 1)
            pe.wait_ge(s_wT_out, 1)
            for t in range(NT):
                mm = pe.matmul(bank[4 + t][:, :], zero[:, :], x_tok[:, t, :], start=True, stop=False, skip_group_check=True)
            mm.then_inc(s_moe_done, 1)
            with pe.Fori(0, NU // 2 - 1) as k:
                for j in range(2):
                    gate_up(k + j, 1 - j)
                    down(k * 2 + j, j)
            gate_up(NU // 2 - 1, 1)
            down(NU - 2, 0)
            down(NU - 1, 1)


def layouts(i):
    c = np.ascontiguousarray

    def chunks(w):
        return w.reshape(KC, P, -1).transpose(1, 0, 2).reshape(P, -1)

    def heads(w):
        return w.transpose(1, 0, 2).reshape(D, D)

    a = {n: np.asarray(v) for n, v in i.items()}
    xa = "L0_xattn_"
    mats = [heads(a[xa + "Wq1"]), heads(a[xa + "Wk1"]), heads(a[xa + "Wv1"]), a[xa + "Wo1"],
            heads(a[xa + "Wq2"]), heads(a[xa + "Wk2"]), heads(a[xa + "Wv2"]), a[xa + "Wo2"]]
    cols = [a[xa + n].reshape(KC, P).T for n in ("bq1", "bk1", "bv1", "bo1", "bq2", "bk2", "bv2")]
    cols.append(a["L0_attn_b_dt"].reshape(KC, P).T)
    cols.append(a["L0_attn_A_log"].reshape(NS, KC, P).transpose(2, 1, 0).reshape(P, KC * NS))
    f = "L0_ffn_"

    def units(shared, routed):
        return np.concatenate([shared, routed], axis=0)

    def inner(w):
        return w.transpose(0, 2, 1).reshape(NU, KC, P, EI).transpose(0, 2, 1, 3).reshape(NU, P, KC * EI)

    gate = inner(units(a[f + "shared_gate"].reshape(NSH, EI, D), a[f + "expert_gate"]))
    up = inner(units(a[f + "shared_up"].reshape(NSH, EI, D), a[f + "expert_up"]))
    down = units(a[f + "shared_down"].reshape(D, NSH, EI).transpose(1, 0, 2), a[f + "expert_down"])
    down = down.transpose(0, 2, 1).reshape(NU, IC, P, D).transpose(0, 2, 1, 3).reshape(NU, P, IC * D)
    return {
        "x": c(a["x"].reshape(T, D)),
        "ctx_t": c(a["ctx_1024"].transpose(0, 2, 1).reshape(B, KC, P, SC).transpose(0, 2, 1, 3).reshape(B, P, KC * SC)),
        "w_proj": c(np.stack([chunks(m) for m in mats])),
        "small": c(np.concatenate(cols, axis=1)),
        "bo2": c(a[xa + "bo2"]),
        "w_xp": c(a["L0_attn_W_xproj"].reshape(KC, P, -1).transpose(1, 0, 2)),
        "w_dt": c(a["L0_attn_W_dt"]),
        "gate_w": c(a[f + "gate_w"].T.reshape(KC, P, E).transpose(1, 0, 2)),
        "gate_b": c(a[f + "gate_bias"]),
        "w_moe": c(np.concatenate([gate, up, down], axis=2)),
    }


def kernel(**inputs):
    import concourse.bacc as _bacc
    from concourse.bass_utils import run_bass_kernel_spmd as _run

    nc = _bacc.Bacc("TRN2", target_bir_lowering=False, num_devices=1)
    arrays = layouts(inputs)
    args = {n: nc.dram_tensor(n + "_dram", v.shape, mybir.dt.float32, kind="ExternalInput").ap() for n, v in arrays.items()}
    out = nc.dram_tensor("out_dram", (T, D), mybir.dt.float32, kind="ExternalOutput").ap()
    perceiver_block(nc, **args, out=out)
    r = _run(nc, [{n + "_dram": v for n, v in arrays.items()}], core_ids=[0])
    return r.results[0]["out_dram"].reshape(B, S, D)
```

```python
from contextlib import ExitStack

import numpy as np
import concourse.bass as bass
from concourse import mybir

P = 128
B, S, D = 8, 64, 512
SC = 512
H, HD = 16, 32
T = B * S
NT = T // P
KC = D // P
GH = P // HD
NS = 16
RANK = 64
E, EI = 32, 256
NG, EG = 4, 8
NSH = 2
NU = E + NSH
IC = EI // P
EPS = 1e-5
QSCALE = float(HD) ** -0.5
ROUTED_SCALING = 2.5
LOWEST = -3.0e38
N_W = 7
WQ1, WK1, WV1, WO1, WQ2, WK2, WV2, WO2 = range(N_W + 1)
BQ1, BK1, BV1, BO1, BQ2, BK2, BV2, BDT = [KC * n for n in range(8)]
ALOG = KC * 8
N_SMALL = ALOG + KC * NS


def perceiver_block(nc, x, ctx_t, w_proj, small, bo2, w_xp, w_dt, gate_w, gate_b, w_moe, out):
    fp32 = mybir.dt.float32
    f32r = mybir.dt.float32r
    ALU = mybir.AluOpType
    ACT = mybir.ActivationFunctionType
    AX = mybir.AxisListType

    es = ExitStack()
    with es:
        def sb(name, shape, dt=fp32):
            return es.enter_context(nc.sbuf_tensor(name, shape, dt))

        def sem(name):
            return es.enter_context(nc.semaphore(name))

        HALF = KC * D
        RA, RB, RC, RD, RX, RQ = [sb(n, [P, 2 * HALF], f32r) for n in ("RA", "RB", "RC", "RD", "RX", "RQ")]

        def pair(r):
            return [r[:, k * HALF:(k + 1) * HALF].rearrange("p (k n) -> p k n", k=KC) for k in range(2)]

        xT = pair(RX)
        w_of = {WQ1: pair(RA), WK1: pair(RB), WV1: pair(RC), WO1: pair(RD),
                WQ2: pair(RX), WK2: pair(RA), WV2: pair(RB)}
        o1T = pair(RC)
        hT = pair(RQ)
        ctxT = pair(RD)
        k2 = pair(RC)
        v2 = pair(RX)
        qb = [RQ[:, k * 1024:(k + 1) * 1024].rearrange("p (g h q) -> p g h q", g=KC, h=2) for k in range(2)]
        pT = [RQ[:, 2048 + k * 1024:2048 + (k + 1) * 1024].rearrange("p (c q) -> p c q", c=4) for k in range(2)]
        gu_w = [[r[:, k * HALF:(k + 1) * HALF] for k in range(2)] for r in (RA, RB)]
        dn_w = [[RC[:, j * HALF + k * IC * D:j * HALF + (k + 1) * IC * D] for k in range(2)] for j in range(2)]
        inner = [[RD[:, j * HALF + k * IC * T:j * HALF + (k + 1) * IC * T].rearrange("p (i n) -> p i n", i=IC)
                  for k in range(2)] for j in range(2)]
        gw = [RQ[:, k * KC * E:(k + 1) * KC * E].rearrange("p (k e) -> p k e", k=KC) for k in range(2)]

        arena = sb("arena", [P, 3 * HALF])
        xn_all = arena[:, 0:HALF].rearrange("p (t n) -> p t n", t=NT)
        q1, k1, v1 = [arena[:, n * HALF:(n + 1) * HALF].rearrange("p (k n) -> p k n", k=KC) for n in range(3)]
        scan_tiles = [arena[:, n * NS * S:(n + 1) * NS * S].rearrange("p (s n) -> p s n", s=NS) for n in range(6)]
        decay, drive, b_bc, c_bc = scan_tiles[0:2], scan_tiles[2:4], scan_tiles[4], scan_tiles[5]
        wo2 = sb("wo2", [P, KC, D])
        x_tok = sb("x_tok", [P, NT, D])
        q2 = sb("q2", [P, KC, T])
        raw = [sb(f"raw{j}", [P, HALF]) for j in range(2)]
        prob = [sb(f"prob{j}", [P, 512]) for j in range(2)]
        tmp = [sb(f"tmp{j}", [P, 512]) for j in range(6)]
        scr1 = tmp[0:2]
        x_in, x1s, xn2 = [t[0:S, :] for t in tmp[0:3]]
        x1r, x2s = [t[:, 0:KC * S] for t in tmp[3:5]]
        xn2_rows = tmp[2]
        o2f = tmp[5][:, 0:KC * S]
        x2T, dt_z, dt_x, dt_e, yT = [sb(n, [P, KC * S]) for n in ("x2T", "dt_z", "dt_x", "dt_e", "yT")]
        raw_dn = [arena[:, HALF + j * IC * D:HALF + (j + 1) * IC * D] for j in range(2)]
        w_bc = [q2.rearrange("p k n -> p (k n)")[:, j * T:(j + 1) * T] for j in range(2)]
        silu = tmp[0:2]
        act_f = tmp[2:4]
        gw_raw = sb("gw_raw", [P, KC, E])
        gb_bc = sb("gb_bc", [P, E])
        post = sb("post", [P, 2048])
        wT_sb = post[0:E, 0:T]
        ones = post[0:NSH, T:2 * T]
        rt = post[:, 2 * T:2 * T + 5 * NT * E].rearrange("p (a t e) -> p a t e", a=5, t=NT)
        top = sb("top", [P, NT, NG, 8])
        grp = sb("grp", [P, 4, NT, NG])
        top8 = sb("top8", [P, NT, 8])
        rsum = sb("rsum", [P, NT])
        zero = sb("zero", [P, P])
        smallp = sb("smallp", [P, N_SMALL])
        a_pos = sb("a_pos", [P, KC, NS])
        bo2_bc = prob[0]
        ident = sb("ident", [P, P])
        mask = sb("mask", [P, P])
        wxp = sb("wxp", [P, KC, 2 * NS + RANK])
        wdt = sb("wdt", [RANK, D])
        bc_sb = sb("bc_sb", [2 * NS, S])
        dtr = sb("dtr", [RANK, S])
        st2 = sb("st2", [S, 12])
        ln2 = sb("ln2", [S, 8])
        st = sb("st", [P, NT, 6])
        mv = sb("mv", [P, NT, 2])
        ln = sb("ln", [P, 5, NT])
        nm = sb("nm", [P, 16])
        sm = sb("sm", [P, 64])
        rs = sb("rs", [P, 64])
        bank = [es.enter_context(nc.psum_tensor(f"bank{n}", [P, 512], fp32)) for n in range(8)]

        def bias(col):
            return smallp[:, col:col + 1]

        w_dram = nc.dram_tensor("route_scratch", (NU, T), fp32, kind="Internal").ap()
        bc_dram = nc.dram_tensor("bc_scratch", (B, 2 * NS, S), fp32, kind="Internal").ap()
        xb_dram = nc.dram_tensor("x_plus_bias", (T, D), fp32, kind="Internal").ap()
        x1_dram = nc.dram_tensor("x_after_attention", (T, D), fp32, kind="Internal").ap()
        x2_dram = nc.dram_tensor("x_after_scan", (T, D), fp32, kind="Internal").ap()

        s_x_in = sem("x_in")
        s_wo2_in = sem("wo2_in")
        s_small_in = sem("small_in")
        s_w_in0 = sem("w_in0")
        s_w_in1 = sem("w_in1")
        s_ctx_in = sem("ctx_in")
        s_bc_out = sem("bc_out")
        s_xb_ready = sem("xb_ready")
        s_xb_out = sem("xb_out")
        s_xb_in = sem("xb_in")
        s_x1_out = sem("x1_out")
        s_x1r_in = sem("x1r_in")
        s_x2_out = sem("x2_out")
        s_x2_in = sem("x2_in")
        s_b_in = sem("b_in")
        s_c_in = sem("c_in")
        s_out_done = sem("out_done")
        s_consts = sem("consts")
        s_w_hi = sem("w_hi")
        s_w_lo = sem("w_lo")
        s_ln_step = sem("ln_step")
        s_ln_ve = sem("ln_ve")
        s_ln_r0 = sem("ln_r0")
        s_xn_ready = sem("xn_ready")
        s_xnT_ready = sem("xnT_ready")
        s_xT_hi = sem("xT_hi")
        s_xT_lo = sem("xT_lo")
        s_p1_ready = sem("p1_ready")
        s_p1_out = sem("p1_out")
        s_s1_ready = sem("s1_ready")
        s_s1_out = sem("s1_out")
        s_s1_max = sem("s1_max")
        s_s1_exp = sem("s1_exp")
        s_s1_sum = sem("s1_sum")
        s_s1_norm = sem("s1_norm")
        s_s1_T = sem("s1_T")
        s_s1_pT = sem("s1_pT")
        s_s1_pv = sem("s1_pv")
        s_o1_sum = sem("o1_sum")
        s_o1_hi = sem("o1_hi")
        s_o1_lo = sem("o1_lo")
        s_h_ready = sem("h_ready")
        s_h_hi = sem("h_hi")
        s_h_lo = sem("h_lo")
        s_q2_ready = sem("q2_ready")
        s_q2_out = sem("q2_out")
        s_ctx_hi = sem("ctx_hi")
        s_ctx_lo = sem("ctx_lo")
        s_kv_ready = sem("kv_ready")
        s_kv_hi = sem("kv_hi")
        s_kv_lo = sem("kv_lo")
        s_qb_hi = sem("qb_hi")
        s_qb_lo = sem("qb_lo")
        s_s2_ready = sem("s2_ready")
        s_s2_max = sem("s2_max")
        s_s2_exp = sem("s2_exp")
        s_s2_sum = sem("s2_sum")
        s_s2_norm = sem("s2_norm")
        s_s2_T = sem("s2_T")
        s_pT_hi = sem("pT_hi")
        s_pT_lo = sem("pT_lo")
        s_pv_ready = sem("pv_ready")
        s_o2_out = sem("o2_out")
        s_wo2_ready = sem("wo2_ready")
        s_x1_done = sem("x1_done")
        s_ln2_step = sem("ln2_step")
        s_ln2_stat = sem("ln2_stat")
        s_ln2_ve = sem("ln2_ve")
        s_ln2_r0 = sem("ln2_r0")
        s_xn2_ready = sem("xn2_ready")
        s_x2T_ready = sem("x2T_ready")
        s_x2T_out = sem("x2T_out")
        s_xp_ready = sem("xp_ready")
        s_bc_ready = sem("bc_ready")
        s_dtr_ready = sem("dtr_ready")
        s_dtp_ready = sem("dtp_ready")
        s_dt_z_ready = sem("dt_z_ready")
        s_dt_step = sem("dt_step")
        s_dt_ready = sem("dt_ready")
        s_dtx_ready = sem("dtx_ready")
        s_decay_arg = sem("decay_arg")
        s_decay_exp = sem("decay_exp")
        s_decay_zero = sem("decay_zero")
        s_drive_ready = sem("drive_ready")
        s_scan_done = sem("scan_done")
        s_hc_ready = sem("hc_ready")
        s_y_ready = sem("y_ready")
        s_yT_ready = sem("yT_ready")
        s_x2_done = sem("x2_done")
        s_a_ready = sem("a_ready")
        s_gate_in = sem("gate_in")
        s_gw_hi = sem("gw_hi")
        s_gw_lo = sem("gw_lo")
        s_ln3 = sem("ln3")
        s_ln3_ve = sem("ln3_ve")
        s_ln3_r0 = sem("ln3_r0")
        s_ln3_step = sem("ln3_step")
        s_xn3_ready = sem("xn3_ready")
        s_xn3T_ready = sem("xn3T_ready")
        s_x3_hi = sem("x3_hi")
        s_x3_lo = sem("x3_lo")
        s_logit_ready = sem("logit_ready")
        s_r_exp = sem("r_exp")
        s_r_step = sem("r_step")
        s_w_ready = sem("w_ready")
        s_wT_ready = sem("wT_ready")
        s_wT_out = sem("wT_out")
        s_w_stored = sem("w_stored")
        s_ones_ready = sem("ones_ready")
        s_gu_in0 = sem("gu_in0")
        s_gu_in1 = sem("gu_in1")
        s_dn_in0 = sem("dn_in0")
        s_dn_in1 = sem("dn_in1")
        s_wb_in0 = sem("wb_in0")
        s_wb_in1 = sem("wb_in1")
        s_gu_hi = sem("gu_hi")
        s_gu_lo = sem("gu_lo")
        s_dn_hi = sem("dn_hi")
        s_dn_lo = sem("dn_lo")
        s_gu_ready = sem("gu_ready")
        s_silu_done = sem("silu_done")
        s_gated = sem("gated")
        s_h_ready2 = sem("h_ready2")
        s_h_hi2 = sem("h_hi2")
        s_h_lo2 = sem("h_lo2")
        s_moe_done = sem("moe_done")
        s_x3_done = sem("x3_done")

        block = es.enter_context(nc.Block())
        w_in = [s_w_in0, s_w_in1]
        gu_in, dn_in, wb_in = [[s_gu_in0, s_gu_in1], [s_dn_in0, s_dn_in1], [s_wb_in0, s_wb_in1]]
        GU = 2 * KC * EI

        def run_batches(eng, start, attend, advance, scan):
            def window(w, lags, attends=True, more=True):
                for u in range(8):
                    if attends:
                        attend(w, u, more)
                    for g in reversed(lags):
                        scan(w - (1 + g), 8 * g + u)
                if attends:
                    advance(w, more)

            start()
            window(0, [])
            window(1, [0])
            window(2, [0, 1])
            with eng.Fori(3, B - 1) as w:
                window(w, [0, 1, 2])
            window(B - 1, [0, 1, 2], more=False)
            for n in range(3):
                window(B + n, list(range(n, 3)), attends=False)

        def batch_rows(dram, m):
            return dram.rearrange("(b s) d -> b s d", s=S)[bass.ds(m, 1)].rearrange("a s d -> (a s) d")

        def chunk_rows(dram, m, h):
            return batch_rows(dram, m).rearrange("s (j h f) -> h s j f", h=2, f=P)[h]

        def half_rows(tile, h):
            return tile[h * S:(h + 1) * S, :].rearrange("s (j f) -> s j f", f=P)

        @block.sync
        def _(sp):
            sp.dma_start(x_tok[:, :, :], x.rearrange("(t p) d -> p t d", p=P)).then_inc(s_x_in, 16)
            for n in range(N_W):
                if n >= 2:
                    sp.wait_ge(s_w_lo, n - 1)
                sp.dma_start(raw[n % 2][:, :], w_proj[n]).then_inc(w_in[n % 2], 16)
                if n == WQ2:
                    sp.dma_start(wo2[:, :, :], w_proj[WO2].rearrange("p (k n) -> p k n", k=KC)).then_inc(s_wo2_in, 16)
                if n == 0:
                    sp.dma_start(smallp[:, :], small).then_inc(s_small_in, 16)
                    sp.dma_start(bo2_bc[:, :], bo2.partition_broadcast(P)).then_inc(s_small_in, 16)
                    sp.dma_start(wxp[:, :, :], w_xp).then_inc(s_small_in, 16)
                    sp.dma_start(wdt[:, :], w_dt).then_inc(s_small_in, 16)
                    sp.dma_start(gw_raw[:, :, :], gate_w).then_inc(s_gate_in, 16)
                    sp.dma_start(gb_bc[:, :], gate_b.partition_broadcast(P)).then_inc(s_gate_in, 16)
            sp.wait_ge(s_w_lo, N_W)
            def load_ctx(n):
                sp.dma_start(raw[0][:, :], ctx_t[bass.ds(n, 1)].rearrange("a p n -> (a p) n")).then_inc(s_ctx_in, 16)

            def window(w, ctx=True, lag0=True, lag2=True):
                if lag2:
                    if not (isinstance(w, int) and w == 3):
                        sp.wait_ge(s_x2_done, w - 3)
                    sp.wait_ge(s_x1_out, w * 16 - 32)
                    for h in range(2):
                        sp.dma_start(half_rows(x1r, h), chunk_rows(x1_dram, w - 3, h)).then_inc(s_x1r_in, 16)
                if ctx:
                    sp.wait_ge(s_ctx_lo, w + 2)
                    load_ctx(w + 2)
                if lag0:
                    sp.wait_ge(s_x1_done, w)
                    sp.dma_start(batch_rows(x1_dram, w - 1), x1s).then_inc(s_x1_out, 16)
                if lag2:
                    sp.wait_ge(s_x2_done, w - 2)
                    for h in range(2):
                        sp.dma_start(chunk_rows(x2_dram, w - 3, h), half_rows(x2s, h)).then_inc(s_x2_out, 16)
                if lag0:
                    if not (isinstance(w, int) and w == B):
                        sp.dma_start(x_in, batch_rows(xb_dram, w)).then_inc(s_xb_in, 16)
                    sp.wait_ge(s_bc_ready, w)
                    sp.dma_start(bc_dram[bass.ds(w - 1, 1)].rearrange("a r n -> (a r) n"), bc_sb[:, :]).then_inc(s_bc_out, 16)
                    sp.wait_ge(s_bc_out, w * 16)
                    if not (isinstance(w, int) and w == 1):
                        sp.wait_ge(s_drive_ready, w * KC - KC)
                    sp.dma_start(b_bc, bc_dram[bass.ds(w - 1, 1), 0:NS, :].rearrange("a r n -> (a r n)").partition_broadcast(P)).then_inc(s_b_in, 16)
                    if not (isinstance(w, int) and w == 1):
                        sp.wait_ge(s_hc_ready, w * KC - KC)
                    sp.dma_start(c_bc, bc_dram[bass.ds(w - 1, 1), NS:2 * NS, :].rearrange("a r n -> (a r n)").partition_broadcast(P)).then_inc(s_c_in, 16)

            sp.wait_ge(s_xb_ready, NT)
            sp.dma_start(xb_dram.rearrange("(t p) d -> p t d", p=P), x_tok[:, :, :]).then_inc(s_xb_out, 16)
            sp.wait_ge(s_w_lo, N_W)
            load_ctx(0)
            sp.wait_ge(s_ctx_lo, 1)
            load_ctx(1)
            sp.wait_ge(s_xb_out, 16)
            sp.wait_ge(s_o1_lo, NT)
            sp.dma_start(x_in, xb_dram[0:S, :]).then_inc(s_xb_in, 16)
            window(0, lag0=False, lag2=False)
            window(1, lag2=False)
            window(2, lag2=False)
            with sp.Fori(3, B - 2) as w:
                window(w)
            for w in range(B - 2, B + 3):
                window(w, ctx=w == B - 3, lag0=w <= B)
            sp.wait_ge(s_x2_out, 32 * B)
            sp.dma_start(x_tok[:, :, :], x2_dram.rearrange("(t p) d -> p t d", p=P)).then_inc(s_x2_in, 16)
            sp.wait_ge(s_ctx_lo, B)
            sp.wait_ge(s_y_ready, B * KC)
            for j in range(2):
                sp.dma_start(raw[j][:, :], w_moe[j, :, 0:GU]).then_inc(gu_in[j], 16)
                sp.dma_start(raw_dn[j], w_moe[j, :, GU:]).then_inc(dn_in[j], 16)
            sp.wait_ge(s_ones_ready, 1)
            sp.dma_start(w_dram[0:NSH, :], ones).then_inc(s_w_stored, 16)
            sp.wait_ge(s_wT_out, 1)
            sp.dma_start(w_dram[NSH:NU, :], wT_sb).then_inc(s_w_stored, 16)
            sp.wait_ge(s_w_stored, 32)
            for j in range(2):
                sp.dma_start(w_bc[j], w_dram[j, :].partition_broadcast(P)).then_inc(wb_in[j], 16)
            with sp.Fori(0, NU // 2 - 1) as k:
                for j in range(2):
                    sp.wait_ge(s_gu_lo, k * 2 + (j + 1))
                    sp.dma_start(raw[j][:, :], w_moe[bass.ds(k * 2 + (j + 2), 1), :, 0:GU].rearrange("a p n -> (a p) n")).then_inc(gu_in[j], 16)
                    sp.wait_ge(s_dn_lo, k * 2 + (j + 1))
                    sp.dma_start(raw_dn[j], w_moe[bass.ds(k * 2 + (j + 2), 1), :, GU:].rearrange("a p n -> (a p) n")).then_inc(dn_in[j], 16)
                    sp.wait_ge(s_gated, k * 4 + (2 * j + 2))
                    sp.dma_start(w_bc[j], w_dram[bass.ds(k * 2 + (j + 2), 1), :].rearrange("a n -> (a n)").partition_broadcast(P)).then_inc(wb_in[j], 16)
            ov = out.rearrange("(t p) d -> p t d", p=P)
            for t in range(NT):
                sp.wait_ge(s_x3_done, t + 1)
                sp.dma_start(ov[:, t, :], x_tok[:, t, :]).then_inc(s_out_done, 16)
            sp.wait_ge(s_out_done, 16 * NT)

        @block.gpsimd
        def _(pool):
            pool.memset(ident[:, :], 0.0).then_inc(s_consts, 1)
            pool.memset(mask[:, :], 0.0).then_inc(s_consts, 1)
            pool.memset(zero[:, :], 0.0).then_inc(s_consts, 1)
            pool.wait_ge(s_consts, 3)
            pool.affine_select(out=ident[:, :], in_=ident[:, :], compare_op=ALU.not_equal, fill=1.0, base=0,
                               pattern=[[-1, P]], channel_multiplier=1).then_inc(s_consts, 1)
            pool.affine_select(out=mask[:, :], in_=mask[:, :], compare_op=ALU.is_ge, fill=LOWEST, base=0,
                               pattern=[[-1, P]], channel_multiplier=1).then_inc(s_consts, 1)
            pool.wait_ge(s_consts, 5)
            pool.affine_select(out=mask[S:P, :], in_=mask[S:P, :], compare_op=ALU.is_ge, fill=LOWEST, base=-S,
                               pattern=[[1, P]], channel_multiplier=0).then_inc(s_consts, 1)
            for u in range(16):
                pool.wait_ge(s_s1_sum, u + 1)
                v = scr1[u % 2][:, :].rearrange("p (h k) -> p h k", h=GH)
                pool.tensor_tensor(v, v, rs[:, 4 * u:4 * u + 4].unsqueeze(2).to_broadcast([P, GH, P]),
                                   ALU.mult).then_inc(s_s1_norm, 1)
            def normalise(b, u):
                pool.wait_ge(s_s2_sum, b * 8 + (u + 1))
                pool.tensor_tensor(prob[u % 2][:, :], prob[u % 2][:, :],
                                   rs[:, u:u + 1].to_broadcast([P, SC]), ALU.mult).then_inc(s_s2_norm, 1)

            def attend(b, u, more):
                if u + 2 < 8:
                    normalise(b, u + 2)

            def advance(b, more):
                if more:
                    normalise(b + 1, 0)
                    normalise(b + 1, 1)

            def over_states(v, c):
                return v[:, c * S:(c + 1) * S].unsqueeze(1).to_broadcast([P, NS, S])

            def scan(m, step):
                first = isinstance(m, int) and m == 0
                if step == 6:
                    pool.wait_ge(s_dt_ready, m + 1)
                    if not first:
                        pool.wait_ge(s_drive_ready, m * KC)
                    pool.tensor_tensor(dt_x[:, :], dt_z[:, :], x2T[:, :], ALU.mult).then_inc(s_dtx_ready, 1)
                if step in (9, 11, 13, 15):
                    c = (step - 9) // 2
                    if c == 0:
                        pool.wait_ge(s_c_in, m * 16 + 16)
                    pool.wait_ge(s_scan_done, m * KC + (c + 1))
                    pool.tensor_tensor(drive[c % 2], drive[c % 2], c_bc, ALU.mult).then_inc(s_hc_ready, 1)
                if step in (6, 8, 10, 12):
                    c = (step - 6) // 2
                    if not (first and c < 2):
                        pool.wait_ge(s_scan_done, m * KC + (c - 1))
                    pool.tensor_tensor(decay[c % 2], a_pos[:, c, :].unsqueeze(2).to_broadcast([P, NS, S]),
                                       over_states(dt_z, c), ALU.mult).then_inc(s_decay_arg, 1)
                if step in (7, 9, 11, 13):
                    c = (step - 7) // 2
                    if c == 0:
                        pool.wait_ge(s_b_in, m * 16 + 16)
                        pool.wait_ge(s_dtx_ready, m + 1)
                    if not (first and c < 2):
                        pool.wait_ge(s_y_ready, m * KC + (c - 1))
                    pool.tensor_tensor(drive[c % 2], over_states(dt_x, c), b_bc, ALU.mult).then_inc(s_drive_ready, 1)

            run_batches(pool, lambda: advance(-1, True), attend, advance, scan)

            pool.wait_ge(s_y_ready, B * KC)
            pool.memset(ones, 1.0).then_inc(s_ones_ready, 1)

            def weigh(k, j):
                pool.wait_ge(wb_in[j], k * 16 + 16)
                for i in range(IC):
                    pool.wait_ge(s_silu_done, k * 4 + (2 * j + i + 1))
                    pool.tensor_tensor(silu[i][:, :], silu[i][:, :], w_bc[j], ALU.mult).then_inc(s_gated, 1)

            with pool.Fori(0, NU // 2 - 1) as k:
                for j in range(2):
                    weigh(k, j)
            for j in range(2):
                weigh(NU // 2 - 1, j)

        @block.scalar
        def _(act):
            act.preload_act_table_set("natural_log_exp_and_others")
            def split_weight(n):
                act.wait_ge(w_in[n % 2], 16 * (n // 2 + 1))
                if n == WQ2:
                    act.wait_ge(s_p1_ready, 12)
                if n == WK2:
                    act.wait_ge(s_p1_ready, 4)
                if n == WV2:
                    act.wait_ge(s_p1_ready, 8)
                act.activation(w_of[n][0].rearrange("p k n -> p (k n)"), raw[n % 2][:, :], ACT.Copy).then_inc(s_w_hi, 1)

            def rstd(ve, r0, tmpv, waited, count, sem_out, step):
                act.wait_ge(waited, count)
                act.activation(tmpv, ve, ACT.Ln).then_inc(step, 1)
                act.wait_ge(step, count)
                act.activation(r0, tmpv, ACT.Exp, scale=-0.5).then_inc(sem_out, 1)

            split_weight(WQ1)
            rstd(ln[:, 0, :], ln[:, 1, :], ln[:, 2, :], s_ln_ve, 1, s_ln_r0, s_ln_step)
            split_weight(WK1)
            for kc in range(KC):
                act.wait_ge(s_xnT_ready, NT)
                act.activation(xT[0][:, kc, :], bank[kc][:, :], ACT.Copy).then_inc(s_xT_hi, 1)
            split_weight(WV1)
            split_weight(WO1)
            act.wait_ge(s_small_in, 64)
            act.activation(a_pos[:, :, :], smallp[:, ALOG:ALOG + KC * NS].rearrange("p (c n) -> p c n", c=KC),
                           ACT.Exp).then_inc(s_a_ready, 1)
            for n in (8, 9, 10, 11):
                act.wait_ge(s_p1_ready, n + 1)
                act.activation(v1[:, n - 8, :], bank[n % 8][:, :], ACT.Copy).then_inc(s_p1_out, 1)
            split_weight(WQ2)
            split_weight(WK2)

            def exp1(u):
                act.wait_ge(s_s1_max, u + 1)
                for g in range(GH):
                    e = act.activation(scr1[u % 2][:, g * P:(g + 1) * P], scr1[u % 2][:, g * P:(g + 1) * P], ACT.Exp,
                                       bias=nm[:, 8 * (u % 2) + g:8 * (u % 2) + g + 1], accum_out=sm[:, 4 * u + g:4 * u + g + 1])
                e.then_inc(s_s1_exp, 1)

            def pt1(u):
                act.wait_ge(s_s1_T, u + 1)
                if u >= 2:
                    act.wait_ge(s_s1_pv, u - 1)
                act.activation(prob[u % 2][:, :], bank[2 + u % 2][:, :], ACT.Copy).then_inc(s_s1_pT, 1)
            def o1_hi(t):
                act.wait_ge(s_o1_sum, t + 1)
                act.activation(o1T[0][:, :, t * P:(t + 1) * P], tmp[2 + t % 2][:, :].rearrange("p (g n) -> p g n", g=KC),
                               ACT.Copy).then_inc(s_o1_hi, 1)

            exp1(0)
            exp1(1)
            for u in range(16):
                pt1(u)
                if u + 2 < 16:
                    exp1(u + 2)
                if u % 4 == 1 and u > 4:
                    o1_hi(u // 4 - 1)
            o1_hi(3)
            for m in range(KC):
                act.wait_ge(s_h_ready, m + 1)
                act.activation(hT[0][:, m, :], bank[m][:, :], ACT.Identity, bias=bias(BO1 + m)).then_inc(s_h_hi, 1)
            split_weight(WV2)
            act.wait_ge(s_q2_out, KC)
            for n in range(2):
                act.nop().then_inc(s_s2_exp, 1)
            act.nop().then_inc(s_o2_out, 1)

            def split_ctx(n):
                act.wait_ge(s_ctx_in, n * 16 + 16)
                act.activation(ctxT[0].rearrange("p k n -> p (k n)"), raw[0][:, :], ACT.Copy).then_inc(s_ctx_hi, 1)

            def hi_kv(b, k):
                act.wait_ge(s_kv_ready, b * 8 + (k + 1))
                if k < 4:
                    act.activation(k2[0][:, k, :], bank[k % 2][:, :], ACT.Identity, bias=bias(BK2 + k)).then_inc(s_kv_hi, 1)
                else:
                    act.activation(v2[0][:, k - 4, :], bank[k % 2][:, :], ACT.Copy).then_inc(s_kv_hi, 1)

            def hi_query(b):
                for i in range(GH):
                    act.activation(qb[0][HD * i:HD * (i + 1), :, i // 2, (i % 2) * S:(i % 2 + 1) * S],
                                   q2[HD * i:HD * (i + 1), :, bass.ds(b * S, S)], ACT.Copy).then_inc(s_qb_hi, 1)

            def exp2(b, u):
                act.wait_ge(s_s2_max, b * 8 + (u + 1))
                act.wait_ge(s_s2_T, b * 8 + (u + 1))
                act.activation(prob[u % 2][:, :], bank[2 + u % 2][:, :], ACT.Exp, bias=nm[:, u:u + 1],
                               accum_out=sm[:, u:u + 1]).then_inc(s_s2_exp, 1)

            def head_outputs(b, g):
                act.wait_ge(s_pv_ready, b * 4 + (g + 1))
                for i in range(GH):
                    r = slice(HD * i, HD * (i + 1))
                    last = act.activation(o2f[r, g * S:(g + 1) * S], bank[6][r, i * S:(i + 1) * S], ACT.Identity,
                                          bias=smallp[r, BV2 + g:BV2 + g + 1])
                last.then_inc(s_o2_out, 1)

            def start():
                split_ctx(0)
                for k in range(4):
                    hi_kv(0, k)
                hi_query(0)
                advance(-1, True)

            def attend(b, u, more):
                if u == 0 and more:
                    split_ctx(b + 1)
                act.wait_ge(s_s2_T, b * 8 + (u + 3))
                if u >= 2 and u % 2 == 0:
                    act.wait_ge(s_pv_ready, b * 4 + u // 2)
                act.activation(pT[0][:, :, (u % 2) * P:(u % 2 + 1) * P],
                               bank[4 + u % 2][:, :].rearrange("p (c n) -> p c n", c=4), ACT.Copy).then_inc(s_pT_hi, 1)
                if u + 2 < 8:
                    exp2(b, u + 2)
                if u >= 2 and u % 2 == 0:
                    head_outputs(b, u // 2 - 1)
                if u % 2 == 1 and more:
                    hi_kv(b + 1, u // 2)
                if u == 6 and more:
                    hi_query(b + 1)

            def advance(b, more):
                if more:
                    exp2(b + 1, 0)
                    exp2(b + 1, 1)
                if not (isinstance(b, int) and b < 0):
                    head_outputs(b, 3)
                if more:
                    for k in range(4, 8):
                        hi_kv(b + 1, k)

            def scan(m, step):
                if step == 1:
                    act.wait_ge(s_ln2_ve, m + 1)
                    act.activation(ln2[:, 2:3], ln2[:, 0:1], ACT.Ln).then_inc(s_ln2_step, 1)
                    act.wait_ge(s_ln2_step, m + 1)
                    act.activation(ln2[:, 1:2], ln2[:, 2:3], ACT.Exp, scale=-0.5).then_inc(s_ln2_r0, 1)
                if step == 3:
                    act.wait_ge(s_x2T_ready, m + 1)
                    act.activation(x2T[:, :].rearrange("p (k n) -> p k n", k=KC),
                                   bank[7][:, :].rearrange("p (k n) -> p k n", k=KC)[:, :, 0:S], ACT.Copy).then_inc(s_x2T_out, 1)
                if step == 4:
                    act.wait_ge(s_xp_ready, m + 1)
                    act.activation(dtr[:, :], bank[7][0:RANK, S:2 * S], ACT.Copy).then_inc(s_dtr_ready, 1)
                    if not (isinstance(m, int) and m == 0):
                        act.wait_ge(s_bc_out, m * 16)
                    act.activation(bc_sb[:, :], bank[7][0:2 * NS, 0:S], ACT.Copy).then_inc(s_bc_ready, 1)
                if step == 5:
                    act.wait_ge(s_dt_z_ready, m + 1)
                    act.activation(dt_e[:, :], dt_z[:, :], ACT.Abs).then_inc(s_dt_step, 1)
                    act.wait_ge(s_dt_step, m * 3 + 1)
                    act.activation(dt_e[:, :], dt_e[:, :], ACT.Exp, scale=-1.0).then_inc(s_dt_step, 1)
                    act.wait_ge(s_dt_step, m * 3 + 2)
                    act.activation(dt_e[:, :], dt_e[:, :], ACT.Ln, bias=1.0).then_inc(s_dt_step, 1)
                if step in (7, 9, 11, 13):
                    c = (step - 7) // 2
                    act.wait_ge(s_decay_arg, m * KC + (c + 1))
                    act.activation(decay[c % 2], decay[c % 2], ACT.Exp, scale=-1.0).then_inc(s_decay_exp, 1)

            run_batches(act, start, attend, advance, scan)

            rstd(ln[:, 0, :], ln[:, 1, :], ln[:, 2, :], s_ln3_ve, 1, s_ln3_r0, s_ln3_step)
            act.wait_ge(s_gate_in, 32)
            act.activation(gw[0][:, :, :], gw_raw[:, :, :], ACT.Copy).then_inc(s_gw_hi, 1)

            def hi_gu(k, j):
                act.wait_ge(gu_in[j], k * 16 + 16)
                act.activation(gu_w[j][0], raw[j][:, :], ACT.Copy).then_inc(s_gu_hi, 1)

            def hi_dn(k, j):
                act.wait_ge(dn_in[j], k * 16 + 16)
                act.activation(dn_w[j][0], raw_dn[j], ACT.Copy).then_inc(s_dn_hi, 1)

            def silus(k, j):
                for i in range(IC):
                    act.wait_ge(s_gu_ready, k * 4 + (2 * j + i + 1))
                    act.activation(silu[i][:, :], bank[2 * i][:, :], ACT.Silu).then_inc(s_silu_done, 1)
                for i in range(IC):
                    act.wait_ge(s_h_ready2, k * 4 + (2 * j + i + 1))
                    act.activation(inner[j][0][:, i, :], act_f[i][:, :], ACT.Copy).then_inc(s_h_hi2, 1)

            for kc in range(KC):
                act.wait_ge(s_xn3T_ready, NT)
                act.activation(xT[0][:, kc, :], bank[kc][:, :], ACT.Copy).then_inc(s_x3_hi, 1)
            hi_gu(0, 0)
            hi_gu(0, 1)
            hi_dn(0, 0)
            act.wait_ge(s_logit_ready, 1)
            act.activation(rt[:, 0, :, :], bank[4][:, 0:NT * E].rearrange("p (t e) -> p t e", t=NT), ACT.Exp, scale=-1.0).then_inc(s_r_exp, 1)
            act.wait_ge(s_wT_ready, 1)
            act.activation(wT_sb, bank[5][0:E, :], ACT.Copy).then_inc(s_wT_out, 1)
            with act.Fori(0, NU // 2 - 1) as k:
                for j in range(2):
                    silus(k, j)
                    hi_gu(k + 1, j)
                    act.wait_ge(s_moe_done, k * 2 + (j + 1))
                    hi_dn(k + j, 1 - j)
            silus(NU // 2 - 1, 0)
            act.wait_ge(s_moe_done, NU - 1)
            hi_dn(NU // 2 - 1, 1)
            silus(NU // 2 - 1, 1)

        @block.vector
        def _(dve):
            for n in range(2):
                dve.nop().then_inc(s_kv_lo, 1)
            for n in range(2):
                dve.nop().then_inc(s_pT_lo, 1)

            def lo_weight(n):
                dve.wait_ge(s_w_hi, n + 1)
                dve.tensor_tensor(w_of[n][1].rearrange("p k n -> p (k n)"), raw[n % 2][:, :],
                                  w_of[n][0].rearrange("p k n -> p (k n)").bitcast(fp32), ALU.subtract).then_inc(s_w_lo, 1)

            def newton(ve, r0, a, r, waited, count, step, base):
                dve.wait_ge(waited, count)
                dve.tensor_tensor(a, r0, r0, ALU.mult).then_inc(step, 1)
                dve.wait_ge(step, base + 1)
                dve.tensor_tensor(a, a, ve, ALU.mult).then_inc(step, 1)
                dve.wait_ge(step, base + 2)
                dve.tensor_scalar(a, a, -0.5, 1.5, ALU.mult, ALU.add).then_inc(step, 1)
                dve.wait_ge(step, base + 3)
                dve.tensor_tensor(r, a, r0, ALU.mult).then_inc(step, 1)
                dve.wait_ge(step, base + 4)

            dve.wait_ge(s_x_in, 16)
            for t in range(NT):
                dve.bn_stats(st[:, t, :], x_tok[:, t, :]).then_inc(s_xn_ready, 1)
            dve.wait_ge(s_xn_ready, 4)
            for t in range(NT):
                dve.bn_aggr(mv[:, t, :], st[:, t, :]).then_inc(s_xn_ready, 1)
            dve.wait_ge(s_xn_ready, 8)
            dve.tensor_scalar(ln[:, 0, :], mv[:, :, 1], EPS, None, ALU.add).then_inc(s_ln_ve, 1)
            lo_weight(WQ1)
            dve.wait_ge(s_ln_ve, 1)
            newton(ln[:, 0, :], ln[:, 1, :], ln[:, 3, :], ln[:, 4, :], s_ln_r0, 1, s_xn_ready, 8)
            for t in range(NT):
                dve.tensor_scalar(xn_all[:, t, :], x_tok[:, t, :], mv[:, t, 0:1], ln[:, 4, t:t + 1],
                                  ALU.subtract, ALU.mult).then_inc(s_xn_ready, 1)
            lo_weight(WK1)
            for kc in range(KC):
                dve.wait_ge(s_xT_hi, kc + 1)
                dve.tensor_tensor(xT[1][:, kc, :], bank[kc][:, :], xT[0][:, kc, :].bitcast(fp32), ALU.subtract).then_inc(s_xT_lo, 1)
            dve.wait_ge(s_small_in, 64)
            for t in range(NT):
                dve.tensor_tensor(x_tok[:, t, :], x_tok[:, t, :], bo2_bc[:, :], ALU.add).then_inc(s_xb_ready, 1)
            lo_weight(WV1)
            for n in range(8):
                dve.wait_ge(s_p1_ready, n + 1)
                if n < 4:
                    dve.tensor_scalar(q1[:, n, :], bank[4 + n][:, :], bias(BQ1 + n), QSCALE, ALU.add, ALU.mult).then_inc(s_s1_out, 1)
                else:
                    dve.tensor_scalar(k1[:, n - 4, :], bank[n - 4][:, :], bias(BK1 + n - 4), None, ALU.add).then_inc(s_s1_out, 1)
            lo_weight(WO1)
            lo_weight(WQ2)
            lo_weight(WK2)

            def soft1(u):
                dve.wait_ge(s_s1_ready, u + 1)
                dve.tensor_tensor(scr1[u % 2][:, :].rearrange("p (h k) -> p h k", h=GH),
                                  bank[u % 2][:, :].rearrange("p (h k) -> p h k", h=GH),
                                  mask[:, :].unsqueeze(1).to_broadcast([P, GH, P]), ALU.add).then_inc(s_s1_out, 1)
                dve.wait_ge(s_s1_out, 8 + u + 1)
                dve.tensor_reduce(nm[:, 8 * (u % 2):8 * (u % 2) + 4], scr1[u % 2][:, :].rearrange("p (h k) -> p h k", h=GH),
                                  AX.X, ALU.max, negate=True).then_inc(s_s1_max, 1)

            def recip1(u):
                dve.wait_ge(s_s1_exp, u + 1)
                dve.reciprocal(rs[:, 4 * u:4 * u + 4], sm[:, 4 * u:4 * u + 4]).then_inc(s_s1_sum, 1)

            def o1_tile(t):
                dve.wait_ge(s_s1_pv, 4 * t + 4)
                if t >= 2:
                    dve.wait_ge(s_o1_lo, t - 1)
                dve.tensor_tensor(tmp[2 + t % 2][:, :].rearrange("p (g n) -> p g n", g=KC),
                                  bank[4 + t % 2][:, :].rearrange("p (g n) -> p g n", g=KC),
                                  smallp[:, BV1:BV1 + KC].unsqueeze(2).to_broadcast([P, KC, P]), ALU.add).then_inc(s_o1_sum, 1)
                dve.wait_ge(s_o1_hi, t + 1)
                dve.tensor_tensor(o1T[1][:, :, t * P:(t + 1) * P], tmp[2 + t % 2][:, :].rearrange("p (g n) -> p g n", g=KC),
                                  o1T[0][:, :, t * P:(t + 1) * P].bitcast(fp32), ALU.subtract).then_inc(s_o1_lo, 1)

            soft1(0)
            soft1(1)
            recip1(0)
            for u in range(16):
                if u + 1 < 16:
                    recip1(u + 1)
                if u + 2 < 16:
                    dve.wait_ge(s_s1_T, u + 1)
                    soft1(u + 2)
                if u % 4 == 1 and u > 4:
                    o1_tile(u // 4 - 1)
            o1_tile(3)
            for m in range(KC):
                dve.wait_ge(s_h_hi, m + 1)
                dve.scalar_tensor_tensor(hT[1][:, m, :], bank[m][:, :], bias(BO1 + m), hT[0][:, m, :].bitcast(fp32),
                                         ALU.add, ALU.subtract).then_inc(s_h_lo, 1)
            for m in range(KC):
                dve.wait_ge(s_q2_ready, m + 1)
                dve.tensor_scalar(q2[:, m, :], bank[4 + m][:, :], bias(BQ2 + m), QSCALE, ALU.add, ALU.mult).then_inc(s_q2_out, 1)
            for n in range(2):
                dve.memset(qb[n].rearrange("p g h q -> p (g h q)").bitcast(fp32), 0.0).then_inc(s_consts, 1)
            lo_weight(WV2)

            def lo_kv(b, k):
                dve.wait_ge(s_kv_hi, b * 8 + (k + 1))
                if k < 4:
                    dve.scalar_tensor_tensor(k2[1][:, k, :], bank[k % 2][:, :], bias(BK2 + k), k2[0][:, k, :].bitcast(fp32),
                                             ALU.add, ALU.subtract).then_inc(s_kv_lo, 1)
                else:
                    dve.tensor_tensor(v2[1][:, k - 4, :], bank[k % 2][:, :], v2[0][:, k - 4, :].bitcast(fp32),
                                      ALU.subtract).then_inc(s_kv_lo, 1)

            def max2(b, u):
                dve.wait_ge(s_s2_ready, b * 8 + (u + 1))
                dve.tensor_reduce(nm[:, u:u + 1], bank[2 + u % 2][:, :], AX.X, ALU.max, negate=True).then_inc(s_s2_max, 1)

            def recip2(b, u):
                dve.wait_ge(s_s2_exp, b * 8 + (u + 3))
                dve.reciprocal(rs[:, u:u + 1], sm[:, u:u + 1]).then_inc(s_s2_sum, 1)

            def lo_ctx(n):
                dve.wait_ge(s_ctx_hi, n + 1)
                dve.tensor_tensor(ctxT[1].rearrange("p k n -> p (k n)"), raw[0][:, :],
                                  ctxT[0].rearrange("p k n -> p (k n)").bitcast(fp32), ALU.subtract).then_inc(s_ctx_lo, 1)

            def lo_query(b):
                for i in range(GH):
                    dve.wait_ge(s_qb_hi, b * 4 + (i + 1))
                    blk = (slice(HD * i, HD * (i + 1)), slice(None), i // 2, slice((i % 2) * S, (i % 2 + 1) * S))
                    dve.tensor_tensor(qb[1][blk], q2[HD * i:HD * (i + 1), :, bass.ds(b * S, S)], qb[0][blk].bitcast(fp32),
                                      ALU.subtract).then_inc(s_qb_lo, 1)

            def start():
                lo_ctx(0)
                for k in range(4):
                    lo_kv(0, k)
                lo_query(0)
                advance(-1, True)

            def attend(b, u, more):
                if u == 0 and more:
                    lo_ctx(b + 1)
                if u + 2 < 8:
                    max2(b, u + 2)
                dve.wait_ge(s_pT_hi, b * 8 + (u + 1))
                dve.tensor_tensor(pT[1][:, :, (u % 2) * P:(u % 2 + 1) * P],
                                  bank[4 + u % 2][:, :].rearrange("p (c n) -> p c n", c=4),
                                  pT[0][:, :, (u % 2) * P:(u % 2 + 1) * P].bitcast(fp32), ALU.subtract).then_inc(s_pT_lo, 1)
                if u + 2 < 8:
                    recip2(b, u + 2)
                if u % 2 == 1 and more:
                    lo_kv(b + 1, u // 2)
                if u == 6 and more:
                    lo_query(b + 1)

            def advance(b, more):
                if more:
                    max2(b + 1, 0)
                    max2(b + 1, 1)
                    recip2(b + 1, 0)
                    recip2(b + 1, 1)
                    for k in range(4, 8):
                        lo_kv(b + 1, k)

            def scan(m, step):
                first = isinstance(m, int) and m == 0
                if step == 1:
                    dve.wait_ge(s_wo2_ready, m + 1)
                    dve.wait_ge(s_xb_in, m * 16 + 16)
                    if not first:
                        dve.wait_ge(s_x1_out, m * 16)
                    dve.tensor_tensor(x1s, x_in, bank[7][0:S, :], ALU.add).then_inc(s_x1_done, 1)
                    dve.wait_ge(s_x1_done, m + 1)
                    dve.bn_stats(st2[:, 0:6], x1s).then_inc(s_ln2_stat, 1)
                    dve.wait_ge(s_ln2_stat, m * 6 + 1)
                    dve.tensor_tensor(st2[:, 6:9], st2[:, 0:3], st2[:, 3:6], ALU.add).then_inc(s_ln2_stat, 1)
                    dve.tensor_tensor(st2[:, 9:10], st2[:, 1:2], st2[:, 4:5], ALU.subtract).then_inc(s_ln2_stat, 1)
                    dve.wait_ge(s_ln2_stat, m * 6 + 3)
                    dve.tensor_scalar(ln2[:, 5:6], st2[:, 7:8], 0.5, None, ALU.mult).then_inc(s_ln2_stat, 1)
                    dve.tensor_scalar(st2[:, 10:11], st2[:, 8:9], 1.0 / D, EPS, ALU.mult, ALU.add).then_inc(s_ln2_stat, 1)
                    dve.scalar_tensor_tensor(st2[:, 11:12], st2[:, 9:10], 0.25, st2[:, 9:10], ALU.mult, ALU.mult).then_inc(s_ln2_stat, 1)
                    dve.wait_ge(s_ln2_stat, m * 6 + 6)
                    dve.tensor_tensor(ln2[:, 0:1], st2[:, 10:11], st2[:, 11:12], ALU.add).then_inc(s_ln2_ve, 1)
                if step == 2:
                    newton(ln2[:, 0:1], ln2[:, 1:2], ln2[:, 3:4], ln2[:, 4:5], s_ln2_r0, m + 1, s_xn2_ready, m * 5)
                    dve.tensor_scalar(xn2, x1s, ln2[:, 5:6], ln2[:, 4:5], ALU.subtract, ALU.mult).then_inc(s_xn2_ready, 1)
                if step == 5:
                    dve.wait_ge(s_dtp_ready, m + 1)
                    if not first:
                        dve.wait_ge(s_decay_arg, m * KC)
                    dve.tensor_tensor(dt_z[:, :].rearrange("p (c n) -> p c n", c=KC), bank[7][:, 0:KC * S].rearrange("p (c n) -> p c n", c=KC),
                                      smallp[:, BDT:BDT + KC].unsqueeze(2).to_broadcast([P, KC, S]), ALU.add).then_inc(s_dt_z_ready, 1)
                if step == 6:
                    dve.wait_ge(s_dt_step, m * 3 + 3)
                    dve.scalar_tensor_tensor(dt_z[:, :], dt_z[:, :], 0.0, dt_e[:, :], ALU.max, ALU.add).then_inc(s_dt_ready, 1)
                if step in (8, 10, 12, 14):
                    c = (step - 8) // 2
                    dve.wait_ge(s_decay_exp, m * KC + (c + 1))
                    dve.memset(decay[c % 2][:, :, 0:1], 0.0).then_inc(s_decay_zero, 1)
                    dve.wait_ge(s_decay_zero, m * KC + (c + 1))
                    dve.wait_ge(s_drive_ready, m * KC + (c + 1))
                    flat = drive[c % 2].rearrange("p s n -> p (s n)")
                    dve.tensor_tensor_scan(flat, decay[c % 2].rearrange("p s n -> p (s n)"), flat, 0.0,
                                           ALU.mult, ALU.add).then_inc(s_scan_done, 1)
                if step in (10, 12, 14, 16):
                    c = (step - 10) // 2
                    dve.wait_ge(s_hc_ready, m * KC + (c + 1))
                    if c == 0 and not first:
                        dve.wait_ge(s_yT_ready, m)
                    dve.tensor_reduce(yT[:, c * S:(c + 1) * S], drive[c % 2].rearrange("p s n -> p n s"),
                                      AX.X, ALU.add).then_inc(s_y_ready, 1)
                if step == 18:
                    dve.wait_ge(s_yT_ready, m + 1)
                    dve.wait_ge(s_x1r_in, m * 32 + 32)
                    if not first:
                        dve.wait_ge(s_x2_out, m * 32)
                    dve.tensor_tensor(x2s, x1r, bank[7][:, 0:KC * S], ALU.add).then_inc(s_x2_done, 1)

            run_batches(dve, start, attend, advance, scan)

            dve.wait_ge(s_x2_in, 16)
            for t in range(NT):
                dve.bn_stats(st[:, t, :], x_tok[:, t, :]).then_inc(s_ln3, 1)
            dve.wait_ge(s_ln3, NT)
            for t in range(NT):
                dve.bn_aggr(mv[:, t, :], st[:, t, :]).then_inc(s_ln3, 1)
            dve.wait_ge(s_ln3, 2 * NT)
            dve.tensor_scalar(ln[:, 0, :], mv[:, :, 1], EPS, None, ALU.add).then_inc(s_ln3_ve, 1)
            newton(ln[:, 0, :], ln[:, 1, :], ln[:, 3, :], ln[:, 4, :], s_ln3_r0, 1, s_ln3, 2 * NT)
            for t in range(NT):
                dve.tensor_scalar(xn_all[:, t, :], x_tok[:, t, :], mv[:, t, 0:1], ln[:, 4, t:t + 1],
                                  ALU.subtract, ALU.mult).then_inc(s_xn3_ready, 1)
            dve.wait_ge(s_gw_hi, 1)
            dve.tensor_tensor(gw[1][:, :, :], gw_raw[:, :, :], gw[0][:, :, :].bitcast(fp32), ALU.subtract).then_inc(s_gw_lo, 1)
            for kc in range(KC):
                dve.wait_ge(s_x3_hi, kc + 1)
                dve.tensor_tensor(xT[1][:, kc, :], bank[kc][:, :], xT[0][:, kc, :].bitcast(fp32), ALU.subtract).then_inc(s_x3_lo, 1)

            def lo_gu(k, j):
                dve.wait_ge(s_gu_hi, k * 2 + (j + 1))
                dve.tensor_tensor(gu_w[j][1], raw[j][:, :], gu_w[j][0].bitcast(fp32), ALU.subtract).then_inc(s_gu_lo, 1)

            def lo_dn(e, j):
                dve.wait_ge(s_dn_hi, e + 1)
                dve.tensor_tensor(dn_w[j][1], raw_dn[j], dn_w[j][0].bitcast(fp32), ALU.subtract).then_inc(s_dn_lo, 1)

            lo_gu(0, 0)
            lo_gu(0, 1)
            lo_dn(0, 0)

            steps = [0]

            def link(ins):
                steps[0] += 1
                ins.then_inc(s_r_step, 1)
                dve.wait_ge(s_r_step, steps[0])

            sg, sc, ch, mk, wt = [rt[:, n, :, :] for n in range(5)]
            gs, c1, rank, gm = [grp[:, n, :, :] for n in range(4)]
            dve.wait_ge(s_r_exp, 1)
            link(dve.tensor_scalar(sg, sg, 1.0, None, ALU.add))
            link(dve.reciprocal(sc, sg))
            link(dve.tensor_tensor(ch, sc, gb_bc[:, :].unsqueeze(1).to_broadcast([P, NT, E]), ALU.add))
            for t in range(NT):
                for g in range(NG):
                    last = dve.max(top[:, t, g, :], ch[:, t, g * EG:(g + 1) * EG])
            link(last)
            link(dve.tensor_tensor(gs, top[:, :, :, 0], top[:, :, :, 1], ALU.add))
            for g in range(NG):
                last = dve.memset(rank[:, :, g:g + 1], float(g))
            link(last)
            for d in range(1, NG):
                link(dve.tensor_tensor(c1[:, :, 0:NG - d], gs[:, :, d:NG], gs[:, :, 0:NG - d], ALU.is_gt))
                link(dve.tensor_tensor(rank[:, :, 0:NG - d], rank[:, :, 0:NG - d], c1[:, :, 0:NG - d], ALU.add))
                link(dve.tensor_tensor(rank[:, :, d:NG], rank[:, :, d:NG], c1[:, :, 0:NG - d], ALU.subtract))
            link(dve.tensor_scalar(gm, rank, 1.5, None, ALU.is_lt))
            link(dve.tensor_tensor(mk.rearrange("p t (g e) -> p t g e", g=NG), ch.rearrange("p t (g e) -> p t g e", g=NG),
                                   gm.unsqueeze(3).to_broadcast([P, NT, NG, EG]), ALU.mult))
            for t in range(NT):
                last = dve.max(top8[:, t, :], mk[:, t, :])
            link(last)
            for t in range(NT):
                last = dve.match_replace(wt[:, t, :], top8[:, t, :], mk[:, t, :], LOWEST)
            link(last)
            link(dve.tensor_tensor(wt, wt, mk, ALU.not_equal))
            link(dve.tensor_tensor(wt, wt, sc, ALU.mult))
            link(dve.tensor_reduce(rsum[:, :], wt, AX.X, ALU.add))
            link(dve.tensor_scalar(rsum[:, :], rsum[:, :], 1e-20, None, ALU.add))
            link(dve.reciprocal(rsum[:, :], rsum[:, :]))
            link(dve.tensor_tensor(wt, wt, rsum[:, :].unsqueeze(2).to_broadcast([P, NT, E]), ALU.mult))
            dve.tensor_scalar(wt, wt, ROUTED_SCALING, None, ALU.mult).then_inc(s_w_ready, 1)

            def gates(k, j):
                for i in range(IC):
                    dve.wait_ge(s_gated, k * 4 + (2 * j + i + 1))
                    dve.tensor_tensor(act_f[i][:, :], silu[i][:, :], bank[2 * i + 1][:, :], ALU.mult).then_inc(s_h_ready2, 1)
                for i in range(IC):
                    dve.wait_ge(s_h_hi2, k * 4 + (2 * j + i + 1))
                    dve.tensor_tensor(inner[j][1][:, i, :], act_f[i][:, :], inner[j][0][:, i, :].bitcast(fp32),
                                      ALU.subtract).then_inc(s_h_lo2, 1)

            with dve.Fori(0, NU // 2 - 1) as k:
                for j in range(2):
                    gates(k, j)
                    lo_gu(k + 1, j)
                    lo_dn(k * 2 + (j + 1), 1 - j)
                    dve.wait_ge(s_h_lo2, k * 4 + (2 * j + 2))
            gates(NU // 2 - 1, 0)
            lo_dn(NU - 1, 1)
            dve.wait_ge(s_h_lo2, 2 * NU - 2)
            gates(NU // 2 - 1, 1)
            for t in range(NT):
                dve.wait_ge(s_moe_done, NU + 1)
                dve.tensor_tensor(x_tok[:, t, :], x_tok[:, t, :], bank[4 + t][:, :], ALU.add).then_inc(s_x3_done, 1)

        @block.tensor
        def _(pe):
            def mm3(o, w, xx, first, last):
                pe.matmul(o, w[1], xx[0], start=first, stop=False)
                pe.matmul(o, w[0], xx[1], start=False, stop=False)
                return pe.matmul(o, w[0], xx[0], start=False, stop=last)

            def project(o, w, xx, m):
                for kc in range(KC):
                    mm = mm3(o, [w[k][:, kc, m * P:(m + 1) * P] for k in range(2)],
                             [xx[k][:, kc, :] for k in range(2)], kc == 0, kc == KC - 1)
                return mm

            for n in range(2):
                pe.nop().then_inc(s_s2_T, 1)
            pe.wait_ge(s_consts, 6)
            for t in range(NT):
                pe.wait_ge(s_xn_ready, 12 + t + 1)
                for kc in range(KC):
                    mm = pe.transpose(bank[kc][:, t * P:(t + 1) * P], xn_all[:, t, kc * P:(kc + 1) * P], ident[:, :])
                mm.then_inc(s_xnT_ready, 1)
            pe.wait_ge(s_w_lo, 1)
            pe.wait_ge(s_xT_lo, 4)
            for m in range(KC):
                project(bank[4 + m][:, :], w_of[WQ1], xT, m).then_inc(s_p1_ready, 1)
            pe.wait_ge(s_w_lo, 2)
            for m in range(KC):
                project(bank[m][:, :], w_of[WK1], xT, m).then_inc(s_p1_ready, 1)
            pe.wait_ge(s_w_lo, 3)
            for t in range(NT):
                pe.wait_ge(s_s1_out, t + 5)
                project(bank[t][:, :], xT, w_of[WV1], t).then_inc(s_p1_ready, 1)

            def scores1(u):
                t, i = divmod(u, 4)
                if u < 2:
                    pe.wait_ge(s_p1_out, 4)
                if u >= 2:
                    pe.wait_ge(s_s1_out, 8 + u - 1)
                r = slice(HD * i, HD * (i + 1))
                for g in range(KC):
                    mm = pe.matmul(bank[u % 2][:, g * P:(g + 1) * P], q1[r, g, t * P:(t + 1) * P], k1[r, g, t * P:(t + 1) * P],
                                   start=True, stop=True)
                mm.then_inc(s_s1_ready, 1)

            def transpose1(u):
                pe.wait_ge(s_s1_norm, u + 1)
                if u >= 2:
                    pe.wait_ge(s_s1_pT, u - 1)
                for g in range(KC):
                    mm = pe.transpose(bank[2 + u % 2][:, g * P:(g + 1) * P], scr1[u % 2][:, g * P:(g + 1) * P], ident[:, :])
                mm.then_inc(s_s1_T, 1)

            def pv1(u):
                t, i = divmod(u, 4)
                pe.wait_ge(s_s1_pT, u + 1)
                if t >= 2 and i == 0:
                    pe.wait_ge(s_o1_sum, t - 1)
                for g in range(KC):
                    c = g * P + HD * i
                    mm = pe.matmul(bank[4 + t % 2][HD * i:HD * (i + 1), g * P:(g + 1) * P], v1[:, t, c:c + HD],
                                   prob[u % 2][:, g * P:(g + 1) * P], start=True, stop=True)
                mm.then_inc(s_s1_pv, 1)

            scores1(0)
            scores1(1)
            for u in range(16):
                transpose1(u)
                if u + 2 < 16:
                    scores1(u + 2)
                pv1(u)
            pe.wait_ge(s_w_lo, 4)
            pe.wait_ge(s_o1_lo, NT)
            for m in range(KC):
                project(bank[m][:, :], w_of[WO1], o1T, m).then_inc(s_h_ready, 1)
            pe.wait_ge(s_w_lo, 5)
            pe.wait_ge(s_h_lo, KC)
            for m in range(KC):
                project(bank[4 + m][:, :], w_of[WQ2], hT, m).then_inc(s_q2_ready, 1)
            pe.wait_ge(s_w_lo, N_W)
            pe.wait_ge(s_wo2_in, 16)

            def scores2(b, u):
                g, h = divmod(u, 2)
                pe.wait_ge(s_s2_exp, b * 8 + (u + 1))
                pe.wait_ge(s_kv_lo, b * 8 + (g + 3))
                pe.wait_ge(s_qb_lo, b * 4 + 4)
                mm3(bank[2 + u % 2][:, :], [qb[k][:, g, h, :] for k in range(2)], [k2[k][:, g, :] for k in range(2)],
                    True, True).then_inc(s_s2_ready, 1)

            def transpose2(b, u):
                pe.wait_ge(s_s2_norm, b * 8 + (u + 1))
                pe.wait_ge(s_pT_lo, b * 8 + (u + 1))
                for c in range(4):
                    mm = pe.transpose(bank[4 + u % 2][:, c * P:(c + 1) * P], prob[u % 2][:, c * P:(c + 1) * P], ident[:, :])
                mm.then_inc(s_s2_T, 1)

            def weighted_values(b, g):
                pe.wait_ge(s_pT_lo, b * 8 + (2 * g + 4))
                pe.wait_ge(s_kv_lo, b * 8 + 10)
                pe.wait_ge(s_o2_out, b * 4 + (g + 1))
                for c in range(4):
                    mm = mm3(bank[6][:, 0:GH * S], [v2[k][:, c, g * P:(g + 1) * P] for k in range(2)],
                             [pT[k][:, c, :] for k in range(2)], c == 0, c == 3)
                mm.then_inc(s_pv_ready, 1)

            def keys_values(b, k):
                if k == 0:
                    pe.wait_ge(s_ctx_lo, b + 1)
                pe.wait_ge(s_kv_lo, b * 8 + (k + 1))
                if k < 4:
                    mm = project(bank[k % 2][:, :], w_of[WK2], ctxT, k)
                else:
                    mm = project(bank[k % 2][:, :], ctxT, w_of[WV2], k - 4)
                mm.then_inc(s_kv_ready, 1)

            def start():
                for k in range(4):
                    keys_values(0, k)
                advance(-1, True)

            def attend(b, u, more):
                transpose2(b, u)
                if u + 2 < 8:
                    scores2(b, u + 2)
                if u >= 2 and u % 2 == 0:
                    weighted_values(b, u // 2 - 1)
                if u % 2 == 1 and more:
                    keys_values(b + 1, u // 2)

            def advance(b, more):
                if more:
                    scores2(b + 1, 0)
                    scores2(b + 1, 1)
                if not (isinstance(b, int) and b < 0):
                    weighted_values(b, 3)
                if more:
                    for k in range(4, 8):
                        keys_values(b + 1, k)

            def scan(m, step):
                if step == 0:
                    pe.wait_ge(s_o2_out, m * 4 + 5)
                    if not (isinstance(m, int) and m == 0):
                        pe.wait_ge(s_dt_z_ready, m)
                    for kc in range(KC):
                        mm = pe.matmul(bank[7][0:S, :], o2f[:, kc * S:(kc + 1) * S], wo2[:, kc, :], start=kc == 0, stop=kc == KC - 1)
                    mm.then_inc(s_wo2_ready, 1)
                if step == 3:
                    pe.wait_ge(s_xn2_ready, m * 5 + 5)
                    if not (isinstance(m, int) and m < 2):
                        pe.wait_ge(s_x2_done, m - 1)
                    for kc in range(KC):
                        mm = pe.transpose(bank[7][:, kc * P:(kc + 1) * P], xn2_rows[:, kc * P:(kc + 1) * P], ident[:, :])
                    mm.then_inc(s_x2T_ready, 1)
                if step == 4:
                    pe.wait_ge(s_x2T_out, m + 1)
                    x3 = x2T[:, :].rearrange("p (k n) -> p k n", k=KC)
                    for kc in range(KC):
                        pe.matmul(bank[7][0:2 * NS, 0:S], wxp[:, kc, 0:2 * NS], x3[:, kc, :], start=kc == 0, stop=kc == KC - 1)
                    for kc in range(KC):
                        mm = pe.matmul(bank[7][0:RANK, S:2 * S], wxp[:, kc, 2 * NS:], x3[:, kc, :], start=kc == 0, stop=kc == KC - 1)
                    mm.then_inc(s_xp_ready, 1)
                if step == 5:
                    pe.wait_ge(s_dtr_ready, m + 1)
                    pe.wait_ge(s_bc_ready, m + 1)
                    for c in range(KC):
                        mm = pe.matmul(bank[7][:, c * S:(c + 1) * S], wdt[:, c * P:(c + 1) * P], dtr[:, :], start=True, stop=True)
                    mm.then_inc(s_dtp_ready, 1)
                if step == 17:
                    pe.wait_ge(s_y_ready, m * KC + KC)
                    if not isinstance(m, int) or m < B - 2:
                        pe.wait_ge(s_x1_done, m + 3)
                    elif m == B - 2:
                        pe.wait_ge(s_dt_z_ready, B)
                    else:
                        pe.wait_ge(s_x2_done, B - 1)
                    for j in range(KC // 2):
                        mm = pe.transpose(bank[7][:, j * P:(j + 1) * P], yT[:, j * P:(j + 1) * P], ident[:, :])
                    mm.then_inc(s_yT_ready, 1)

            run_batches(pe, start, attend, advance, scan)

            for t in range(NT):
                pe.wait_ge(s_xn3_ready, t + 1)
                for kc in range(KC):
                    mm = pe.transpose(bank[kc][:, t * P:(t + 1) * P], xn_all[:, t, kc * P:(kc + 1) * P], ident[:, :])
                mm.then_inc(s_xn3T_ready, 1)
            pe.wait_ge(s_x3_lo, KC)
            pe.wait_ge(s_gw_lo, 1)
            for t in range(NT):
                for kc in range(KC):
                    mm = mm3(bank[4][:, t * E:(t + 1) * E], [xT[k][:, kc, t * P:(t + 1) * P] for k in range(2)],
                             [gw[k][:, kc, :] for k in range(2)], kc == 0, kc == KC - 1)
            mm.then_inc(s_logit_ready, 1)

            def gate_up(k, j, first=False):
                pe.wait_ge(s_gu_lo, k * 2 + (j + 1))
                w = [gu_w[j][n].rearrange("p (s c i) -> p s c i", s=2, c=KC) for n in range(2)]
                for i in range(IC):
                    if not first:
                        pe.wait_ge(s_h_ready2, k * 4 + (2 * j + i - 1))
                    for sel in range(2):
                        for kc in range(KC):
                            mm = mm3(bank[2 * i + sel][:, :], [w[n][:, sel, kc, i * P:(i + 1) * P] for n in range(2)],
                                     [xT[n][:, kc, :] for n in range(2)], kc == 0, kc == KC - 1)
                    mm.then_inc(s_gu_ready, 1)

            def down(e, j):
                pe.wait_ge(s_dn_lo, e + 1)
                pe.wait_ge(s_h_lo2, e * 2 + 2)
                w = [dn_w[j][n].rearrange("p (i d) -> p i d", i=IC) for n in range(2)]
                for t in range(NT):
                    for i in range(IC):
                        a = [inner[j][n][:, i, t * P:(t + 1) * P] for n in range(2)]
                        for aa, ww in ((a[1], w[0]), (a[0], w[1]), (a[0], w[0])):
                            mm = pe.matmul(bank[4 + t][:, :], aa, ww[:, i, :], start=False, stop=False, skip_group_check=True)
                mm.then_inc(s_moe_done, 1)

            gate_up(0, 0, True)
            pe.wait_ge(s_w_ready, 1)
            for t in range(NT):
                mm = pe.transpose(bank[5][0:E, t * P:(t + 1) * P], rt[:, 4, t, :], ident[:, :])
            mm.then_inc(s_wT_ready, 1)
            pe.wait_ge(s_wT_out, 1)
            for t in range(NT):
                mm = pe.matmul(bank[4 + t][:, :], zero[:, :], x_tok[:, t, :], start=True, stop=False, skip_group_check=True)
            mm.then_inc(s_moe_done, 1)
            with pe.Fori(0, NU // 2 - 1) as k:
                for j in range(2):
                    gate_up(k + j, 1 - j)
                    down(k * 2 + j, j)
            gate_up(NU // 2 - 1, 1)
            down(NU - 2, 0)
            down(NU - 1, 1)


def layouts(i):
    c = np.ascontiguousarray

    def chunks(w):
        return w.reshape(KC, P, -1).transpose(1, 0, 2).reshape(P, -1)

    def heads(w):
        return w.transpose(1, 0, 2).reshape(D, D)

    a = {n: np.asarray(v) for n, v in i.items()}
    xa = "L0_xattn_"
    mats = [heads(a[xa + "Wq1"]), heads(a[xa + "Wk1"]), heads(a[xa + "Wv1"]), a[xa + "Wo1"],
            heads(a[xa + "Wq2"]), heads(a[xa + "Wk2"]), heads(a[xa + "Wv2"]), a[xa + "Wo2"]]
    cols = [a[xa + n].reshape(KC, P).T for n in ("bq1", "bk1", "bv1", "bo1", "bq2", "bk2", "bv2")]
    cols.append(a["L0_attn_b_dt"].reshape(KC, P).T)
    cols.append(a["L0_attn_A_log"].reshape(NS, KC, P).transpose(2, 1, 0).reshape(P, KC * NS))
    f = "L0_ffn_"

    def units(shared, routed):
        return np.concatenate([shared, routed], axis=0)

    def inner(w):
        return w.transpose(0, 2, 1).reshape(NU, KC, P, EI).transpose(0, 2, 1, 3).reshape(NU, P, KC * EI)

    gate = inner(units(a[f + "shared_gate"].reshape(NSH, EI, D), a[f + "expert_gate"]))
    up = inner(units(a[f + "shared_up"].reshape(NSH, EI, D), a[f + "expert_up"]))
    down = units(a[f + "shared_down"].reshape(D, NSH, EI).transpose(1, 0, 2), a[f + "expert_down"])
    down = down.transpose(0, 2, 1).reshape(NU, IC, P, D).transpose(0, 2, 1, 3).reshape(NU, P, IC * D)
    return {
        "x": c(a["x"].reshape(T, D)),
        "ctx_t": c(a["ctx_1024"].transpose(0, 2, 1).reshape(B, KC, P, SC).transpose(0, 2, 1, 3).reshape(B, P, KC * SC)),
        "w_proj": c(np.stack([chunks(m) for m in mats])),
        "small": c(np.concatenate(cols, axis=1)),
        "bo2": c(a[xa + "bo2"]),
        "w_xp": c(a["L0_attn_W_xproj"].reshape(KC, P, -1).transpose(1, 0, 2)),
        "w_dt": c(a["L0_attn_W_dt"]),
        "gate_w": c(a[f + "gate_w"].T.reshape(KC, P, E).transpose(1, 0, 2)),
        "gate_b": c(a[f + "gate_bias"]),
        "w_moe": c(np.concatenate([gate, up, down], axis=2)),
    }


def kernel(**inputs):
    import concourse.bacc as _bacc
    from concourse.bass_utils import run_bass_kernel_spmd as _run

    nc = _bacc.Bacc("TRN2", target_bir_lowering=False, num_devices=1)
    arrays = layouts(inputs)
    args = {n: nc.dram_tensor(n + "_dram", v.shape, mybir.dt.float32, kind="ExternalInput").ap() for n, v in arrays.items()}
    out = nc.dram_tensor("out_dram", (T, D), mybir.dt.float32, kind="ExternalOutput").ap()
    perceiver_block(nc, **args, out=out)
    r = _run(nc, [{n + "_dram": v for n, v in arrays.items()}], core_ids=[0])
    return r.results[0]["out_dram"].reshape(B, S, D)
```

```python
from contextlib import ExitStack

import numpy as np
import concourse.bass as bass
from concourse import mybir

P = 128
B, S, D = 8, 64, 512
SC = 512
NC = SC // 128
H, HD = 16, 32
T = B * S
NT = T // P
KC = D // P
GH = P // HD
NS = 16
RANK = 64
E, EI = 32, 256
NG, EG = 4, 8
NSH = 2
NU = E + NSH
IC = EI // P
TOPK = 8
UT = 256
UA = UT // P
assert T <= 2 * UT
MAXU = -(-(T * TOPK + E * (UT - 1)) // UT // 2) * 2
EPS = 1e-5
QSCALE = float(HD) ** -0.5
ROUTED_SCALING = 2.5
LOWEST = -3.0e38
N_W = 7
WQ1, WK1, WV1, WO1, WQ2, WK2, WV2, WO2 = range(N_W + 1)
BQ1, BK1, BV1, BO1, BQ2, BK2, BV2, BDT = [KC * n for n in range(8)]
ALOG = KC * 8
IOTA = ALOG + KC * NS
N_SMALL = IOTA + 1


def perceiver_block(nc, x, ctx_t, w_proj, small, bo2, w_xp, w_dt, gate_w, gate_b, w_moe, out):
    fp32 = mybir.dt.float32
    f32r = mybir.dt.float32r
    i32 = mybir.dt.int32
    ALU = mybir.AluOpType
    ACT = mybir.ActivationFunctionType
    AX = mybir.AxisListType

    es = ExitStack()
    with es:
        def sb(name, shape, dt=fp32):
            return es.enter_context(nc.sbuf_tensor(name, shape, dt))

        def sem(name):
            return es.enter_context(nc.semaphore(name))

        HALF = KC * D
        RA, RB, RC, RD, RX, RQ = [sb(n, [P, 2 * HALF], f32r) for n in ("RA", "RB", "RC", "RD", "RX", "RQ")]

        def pair(r):
            return [r[:, k * HALF:(k + 1) * HALF].rearrange("p (k n) -> p k n", k=KC) for k in range(2)]

        xT = pair(RX)
        w_of = {WQ1: pair(RA), WK1: pair(RB), WV1: pair(RC), WO1: pair(RD),
                WQ2: pair(RX), WK2: pair(RA), WV2: pair(RB)}
        o1T = pair(RC)
        hT = pair(RQ)
        ctxT = pair(RD)
        k2 = pair(RC)
        v2 = pair(RX)
        qb = [RQ[:, k * 1024:(k + 1) * 1024].rearrange("p (g h q) -> p g h q", g=KC, h=2) for k in range(2)]
        pT = [RQ[:, 2048 + k * 1024:2048 + (k + 1) * 1024].rearrange("p (c q) -> p c q", c=4) for k in range(2)]
        gu_w = [[r[:, k * HALF:(k + 1) * HALF] for k in range(2)] for r in (RA, RB)]
        dn_w = [[RC[:, j * HALF + k * IC * D:j * HALF + (k + 1) * IC * D] for k in range(2)] for j in range(2)]
        inner = [[RD[:, j * HALF + k * IC * T:j * HALF + (k + 1) * IC * T].rearrange("p (i n) -> p i n", i=IC)
                  for k in range(2)] for j in range(2)]
        gw = [RQ[:, k * KC * E:(k + 1) * KC * E].rearrange("p (k e) -> p k e", k=KC) for k in range(2)]

        arena = sb("arena", [P, 3 * HALF])
        xn_all = arena[:, 0:HALF].rearrange("p (t n) -> p t n", t=NT)
        q1, k1, v1 = [arena[:, n * HALF:(n + 1) * HALF].rearrange("p (k n) -> p k n", k=KC) for n in range(3)]
        scan_tiles = [arena[:, n * NS * S:(n + 1) * NS * S].rearrange("p (s n) -> p s n", s=NS) for n in range(6)]
        decay, drive, b_bc, c_bc = scan_tiles[0:2], scan_tiles[2:4], scan_tiles[4], scan_tiles[5]
        wo2 = sb("wo2", [P, KC, D])
        x_tok = sb("x_tok", [P, NT, D])
        q2 = sb("q2", [P, KC, T])
        raw = [sb(f"raw{j}", [P, HALF]) for j in range(2)]
        prob = [sb(f"prob{j}", [P, 512]) for j in range(2)]
        tmp = [sb(f"tmp{j}", [P, 512]) for j in range(6)]
        scr1 = [tmp[0], tmp[1], tmp[4]]
        pT1 = [prob[0], prob[1], tmp[5]]
        x_in, x1s, xn2 = [t[0:S, :] for t in tmp[0:3]]
        x1r, x2s = [t[:, 0:KC * S] for t in tmp[3:5]]
        xn2_rows = tmp[2]
        o2f = tmp[5][:, 0:KC * S]
        x2T, dt_z, dt_x, dt_e, yT = [sb(n, [P, KC * S]) for n in ("x2T", "dt_z", "dt_x", "dt_e", "yT")]
        raw_ctx = raw[0].rearrange("p (k n) -> p k n", k=KC)
        raw_dn = [arena[:, HALF + j * IC * D:HALF + (j + 1) * IC * D] for j in range(2)]
        q2f = q2.rearrange("p k n -> p (k n)")
        xg_tok = [q2f[:, j * UA * D:(j + 1) * UA * D] for j in range(2)]
        xg = [[RQ[:, (2 * j + k) * KC * UT:(2 * j + k + 1) * KC * UT].rearrange("p (c n) -> p c n", c=KC) for k in range(2)]
              for j in range(2)]
        y_sb = [arena[:, 2 * HALF + j * UA * D:2 * HALF + (j + 1) * UA * D] for j in range(2)]
        silu = tmp[0:2]
        act_f = tmp[2:4]
        unit_act = tmp[2][:, 0:IC * UT].rearrange("p (i n) -> p i n", i=IC)
        gw_raw = sb("gw_raw", [P, KC, E])
        gb_bc = sb("gb_bc", [P, E])
        post = sb("post", [P, 2048])
        rt = post[:, 0:5 * NT * E].rearrange("p (a t e) -> p a t e", a=5, t=NT)
        key = post[:, 640:640 + NT * E].rearrange("p (t e) -> p t e", t=NT)
        logitT = post[0:E, 768:768 + T]
        match = post[:, 768:768 + NT * TOPK * E].rearrange("p (t j e) -> p t j e", t=NT, j=TOPK)
        rows = post[:, 1792:1824].rearrange("p (t j) -> p t j", t=NT)
        no_slots = post[0:MAXU, 0:2 * UT].bitcast(i32).rearrange("u (s c) -> u s c", c=2)
        cnt_more, cnt_units, units_incl, base_row = [post[:, 1856 + n * 32:1888 + n * 32] for n in range(4)]
        row_idx = sb("row_idx", [P, NT * TOPK], i32)
        plan = sb("plan", [P, 2], i32)
        slots = sb("slots", [P, NT * TOPK, 2], i32)
        slot = [sb(f"slot{j}", [P, UA, 2], i32) for j in range(2)]
        gate_out = sb("gate_out", [P, 1])
        plan_f = sb("plan_f", [P, 1])
        before = sb("before", [P, P])
        ones = sb("ones", [P, P])
        top = sb("top", [P, NT, NG, 8])
        grp = sb("grp", [P, 4, NT, NG])
        top8 = sb("top8", [P, NT, 8])
        rsum = sb("rsum", [P, NT])
        zero = sb("zero", [P, P])
        smallp = sb("smallp", [P, N_SMALL])
        a_pos = sb("a_pos", [P, KC, NS])
        bo2_bc = prob[0]
        ident = sb("ident", [P, P])
        mask = sb("mask", [P, P])
        wxp = sb("wxp", [P, KC, 2 * NS + RANK])
        wdt = sb("wdt", [RANK, D])
        bc_sb = sb("bc_sb", [2 * NS, S])
        dtr = sb("dtr", [RANK, S])
        st2 = sb("st2", [S, 12])
        ln2 = sb("ln2", [S, 8])
        st = sb("st", [P, NT, 6])
        mv = sb("mv", [P, NT, 2])
        ln = sb("ln", [P, 5, NT])
        nm = sb("nm", [P, 16])
        sm = sb("sm", [P, 64])
        rs = sb("rs", [P, 64])
        bank = [es.enter_context(nc.psum_tensor(f"bank{n}", [P, 512], fp32)) for n in range(8)]

        def bias(col):
            return smallp[:, col:col + 1]

        slot_dram = nc.dram_tensor("unit_slots", (MAXU * UT, 2), i32, kind="Internal").ap()
        sum_dram = nc.dram_tensor("sums", (T + UT, D), fp32, kind="Internal").ap()
        u_dram = nc.dram_tensor("unit_rows", (MAXU * UT, D), fp32, kind="Internal").ap()
        plan_dram = nc.dram_tensor("plan_scratch", (P, 2), i32, kind="Internal").ap()
        bc_dram = nc.dram_tensor("bc_scratch", (B, 2 * NS, S), fp32, kind="Internal").ap()
        xb_dram = nc.dram_tensor("x_plus_bias", (T, D), fp32, kind="Internal").ap()
        x1_dram = nc.dram_tensor("x_after_attention", (T, D), fp32, kind="Internal").ap()
        x2_dram = nc.dram_tensor("x_after_scan", (T, D), fp32, kind="Internal").ap()

        s_x_in = sem("x_in")
        s_wo2_in = sem("wo2_in")
        s_small_in = sem("small_in")
        s_w_in0 = sem("w_in0")
        s_w_in1 = sem("w_in1")
        s_ctx_in = sem("ctx_in")
        s_bc_out = sem("bc_out")
        s_xb_ready = sem("xb_ready")
        s_xb_out = sem("xb_out")
        s_xb_in = sem("xb_in")
        s_x1_out = sem("x1_out")
        s_x1r_in = sem("x1r_in")
        s_x2_out = sem("x2_out")
        s_x2_in = sem("x2_in")
        s_b_in = sem("b_in")
        s_c_in = sem("c_in")
        s_out_done = sem("out_done")
        s_consts = sem("consts")
        s_w_hi = sem("w_hi")
        s_w_lo = sem("w_lo")
        s_ln_step = sem("ln_step")
        s_ln_ve = sem("ln_ve")
        s_ln_r0 = sem("ln_r0")
        s_xn_ready = sem("xn_ready")
        s_xnT_ready = sem("xnT_ready")
        s_xT_hi = sem("xT_hi")
        s_xT_lo = sem("xT_lo")
        s_p1_ready = sem("p1_ready")
        s_p1_out = sem("p1_out")
        s_s1_ready = sem("s1_ready")
        s_s1_out = sem("s1_out")
        s_s1_max = sem("s1_max")
        s_s1_exp = sem("s1_exp")
        s_s1_sum = sem("s1_sum")
        s_s1_norm = sem("s1_norm")
        s_s1_T = sem("s1_T")
        s_s1_pT = sem("s1_pT")
        s_s1_pv = sem("s1_pv")
        s_o1_sum = sem("o1_sum")
        s_o1_hi = sem("o1_hi")
        s_o1_lo = sem("o1_lo")
        s_h_ready = sem("h_ready")
        s_h_hi = sem("h_hi")
        s_h_lo = sem("h_lo")
        s_q2_ready = sem("q2_ready")
        s_q2_out = sem("q2_out")
        s_ctx_hi = sem("ctx_hi")
        s_ctx_lo = sem("ctx_lo")
        s_kv_ready = sem("kv_ready")
        s_kv_hi = sem("kv_hi")
        s_kv_lo = sem("kv_lo")
        s_qb_hi = sem("qb_hi")
        s_qb_lo = sem("qb_lo")
        s_s2_ready = sem("s2_ready")
        s_s2_max = sem("s2_max")
        s_s2_exp = sem("s2_exp")
        s_s2_sum = sem("s2_sum")
        s_s2_norm = sem("s2_norm")
        s_s2_T = sem("s2_T")
        s_pT_hi = sem("pT_hi")
        s_pT_lo = sem("pT_lo")
        s_pv_ready = sem("pv_ready")
        s_o2_out = sem("o2_out")
        s_wo2_ready = sem("wo2_ready")
        s_x1_done = sem("x1_done")
        s_ln2_step = sem("ln2_step")
        s_ln2_stat = sem("ln2_stat")
        s_ln2_ve = sem("ln2_ve")
        s_ln2_r0 = sem("ln2_r0")
        s_xn2_ready = sem("xn2_ready")
        s_x2T_ready = sem("x2T_ready")
        s_x2T_out = sem("x2T_out")
        s_xp_ready = sem("xp_ready")
        s_bc_ready = sem("bc_ready")
        s_dtr_ready = sem("dtr_ready")
        s_dtp_ready = sem("dtp_ready")
        s_dt_z_ready = sem("dt_z_ready")
        s_dt_step = sem("dt_step")
        s_dt_ready = sem("dt_ready")
        s_dtx_ready = sem("dtx_ready")
        s_decay_arg = sem("decay_arg")
        s_decay_exp = sem("decay_exp")
        s_decay_zero = sem("decay_zero")
        s_drive_ready = sem("drive_ready")
        s_scan_done = sem("scan_done")
        s_hc_ready = sem("hc_ready")
        s_y_ready = sem("y_ready")
        s_yT_ready = sem("yT_ready")
        s_x2_done = sem("x2_done")
        s_a_ready = sem("a_ready")
        s_gate_in = sem("gate_in")
        s_gw_hi = sem("gw_hi")
        s_gw_lo = sem("gw_lo")
        s_ln3 = sem("ln3")
        s_ln3_ve = sem("ln3_ve")
        s_ln3_r0 = sem("ln3_r0")
        s_ln3_step = sem("ln3_step")
        s_xn3_ready = sem("xn3_ready")
        s_xn3T_ready = sem("xn3T_ready")
        s_x3_hi = sem("x3_hi")
        s_x3_lo = sem("x3_lo")
        s_logit_ready = sem("logit_ready")
        s_logitT_ready = sem("logitT_ready")
        s_logitT_out = sem("logitT_out")
        s_x2_last = sem("x2_last")
        s_r_exp = sem("r_exp")
        s_r_step = sem("r_step")
        s_w_ready = sem("w_ready")
        s_fill = sem("fill")
        s_no_slots = sem("no_slots")
        s_before_ready = sem("before_ready")
        s_mask_ready = sem("mask_ready")
        s_pos_ready = sem("pos_ready")
        s_idx_ready = sem("idx_ready")
        s_plan_ready = sem("plan_ready")
        s_plan_stored = sem("plan_stored")
        s_scattered = sem("scattered")
        s_xg_in0 = sem("xg_in0")
        s_xg_in1 = sem("xg_in1")
        s_xg_T = sem("xg_T")
        s_xg_hi = sem("xg_hi")
        s_xg_lo = sem("xg_lo")
        s_act_hi = sem("act_hi")
        s_act_lo = sem("act_lo")
        s_dn_done = sem("dn_done")
        s_base_done = sem("base_done")
        s_y_evac = sem("y_evac")
        s_added0 = sem("added0")
        s_added1 = sem("added1")
        s_slots_ready = sem("slots_ready")
        s_slots_put = sem("slots_put")
        s_no_slots_ready = sem("no_slots_ready")
        s_slot_fill = sem("slot_fill")
        s_slot_in0 = sem("slot_in0")
        s_slot_in1 = sem("slot_in1")
        s_base_out = sem("base_out")
        s_gate = sem("gate")
        s_gu_in0 = sem("gu_in0")
        s_gu_in1 = sem("gu_in1")
        s_dn_in0 = sem("dn_in0")
        s_dn_in1 = sem("dn_in1")
        s_gu_hi = sem("gu_hi")
        s_gu_lo = sem("gu_lo")
        s_dn_hi = sem("dn_hi")
        s_dn_lo = sem("dn_lo")
        s_gu_ready = sem("gu_ready")
        s_silu_done = sem("silu_done")
        s_h_ready2 = sem("h_ready2")

        block = es.enter_context(nc.Block())
        w_in = [s_w_in0, s_w_in1]
        gu_in, dn_in, xg_in, slot_in, added = [[s_gu_in0, s_gu_in1], [s_dn_in0, s_dn_in1], [s_xg_in0, s_xg_in1], [s_slot_in0, s_slot_in1],
                                            [s_added0, s_added1]]
        SCORES, TRANSPOSED = (0, 1, 6), (2, 3, 7)
        split_at = {1: WQ2, 5: WK2, 9: WV2}

        def token_bank(u):
            return 4 if isinstance(u, int) and u == 1 else 6

        GU = 2 * KC * EI

        def run_batches(eng, start, attend, advance, scan):
            def window(w, lags, attends=True, more=True, ahead=True):
                for u in range(8):
                    if attends and attend:
                        attend(w, u, more)
                    for g in reversed(lags):
                        scan(w - (1 + g), 8 * g + u)
                if attends and attend:
                    advance(w, more, ahead)

            if start:
                start()
            window(0, [])
            window(1, [0])
            window(2, [0, 1])
            with eng.Fori(3, B - 2) as w:
                window(w, [0, 1, 2])
            window(B - 2, [0, 1, 2], ahead=False)
            window(B - 1, [0, 1, 2], more=False, ahead=False)
            for n in range(3):
                window(B + n, list(range(n, 3)), attends=False)

        def over_states(v, c):
            return v[:, c * S:(c + 1) * S].unsqueeze(1).to_broadcast([P, NS, S])

        def alone(m):
            return isinstance(m, int) and m >= B - 2

        def state_inputs(eng, m, c):
            if c == 0:
                eng.wait_ge(s_b_in, m * 16 + 16)
                eng.wait_ge(s_dtx_ready, m + 1)
            if not (isinstance(m, int) and m == 0 and c < 2):
                eng.wait_ge(s_y_ready, m * KC + (c - 1))
            eng.tensor_tensor(drive[c % 2], over_states(dt_x, c), b_bc, ALU.mult).then_inc(s_drive_ready, 1)

        def state_outputs(eng, m, c):
            if c < 2:
                eng.wait_ge(s_c_in, m * 16 + 16)
            if c:
                eng.wait_ge(s_hc_ready, m * KC + c)
            eng.wait_ge(s_scan_done, m * KC + (c + 1))
            eng.tensor_tensor(drive[c % 2], drive[c % 2], c_bc, ALU.mult).then_inc(s_hc_ready, 1)

        def batch_rows(dram, m):
            return dram.rearrange("(b s) d -> b s d", s=S)[bass.ds(m, 1)].rearrange("a s d -> (a s) d")

        def chunk_rows(dram, m, h):
            return batch_rows(dram, m).rearrange("s (j h f) -> h s j f", h=2, f=P)[h]

        def half_rows(tile, h):
            return tile[h * S:(h + 1) * S, :].rearrange("s (j f) -> s j f", f=P)

        def unit_rows(dram, u):
            return dram.rearrange("(u p a) d -> u p (a d)", a=UA, p=P)[bass.ds(u, 1)].rearrange("o p n -> (o p) n")

        def last_pair(eng):
            eng.wait_ge(s_plan_stored, 16)
            return eng.value_load(plan_dram[0:1, 1:2], min_val=T * TOPK // UT - 1, max_val=MAXU - 1) // 2

        @block.sync
        def _(sp):
            sp.dma_start(x_tok[:, :, :], x.rearrange("(t p) d -> p t d", p=P)).then_inc(s_x_in, 16)
            for n in range(N_W):
                if n >= 2:
                    sp.wait_ge(s_w_lo, n - 1)
                sp.dma_start(raw[n % 2][:, :], w_proj[n]).then_inc(w_in[n % 2], 16)
                if n == WQ2:
                    sp.dma_start(wo2[:, :, :], w_proj[WO2].rearrange("p (k n) -> p k n", k=KC)).then_inc(s_wo2_in, 16)
                if n == 0:
                    sp.dma_start(smallp[:, :], small).then_inc(s_small_in, 16)
                    sp.dma_start(bo2_bc[:, :], bo2.partition_broadcast(P)).then_inc(s_small_in, 16)
                    sp.dma_start(wxp[:, :, :], w_xp).then_inc(s_small_in, 16)
                    sp.dma_start(wdt[:, :], w_dt).then_inc(s_small_in, 16)
                    sp.dma_start(gw_raw[:, :, :], gate_w).then_inc(s_gate_in, 16)
                    sp.dma_start(gb_bc[:, :], gate_b.partition_broadcast(P)).then_inc(s_gate_in, 16)
            sp.wait_ge(s_w_lo, N_W)

            def load_ctx(n):
                sp.dma_start(raw[0][:, :], ctx_t[bass.ds(n, 1)].rearrange("a p n -> (a p) n")).then_inc(s_ctx_in, 16)

            def fill(w):
                n = MAXU * UT // 8 // P
                sp.dma_start(u_dram.rearrange("(c p n) d -> c p (n d)", c=8, p=P)[bass.ds(w, 1)].rearrange("o p (a f) -> (o p) a f", f=P),
                             zero[:, :].unsqueeze(1).to_broadcast([P, n * D // P, P])).then_inc(s_fill, 16)

            def window(w, ctx=True, lag0=True, lag2=True):
                ctx_split = (w + 2) * NC if isinstance(w, int) else sp.snap((w + 2) * NC, min_val=NC)
                if not (isinstance(w, int) and w >= B):
                    fill(w)
                if lag2:
                    if not (isinstance(w, int) and w == 3):
                        sp.wait_ge(s_x2_done, w - 3)
                    sp.wait_ge(s_x1_out, w * 16 - 32)
                    for h in range(2):
                        sp.dma_start(half_rows(x1r, h), chunk_rows(x1_dram, w - 3, h)).then_inc(s_x1r_in, 16)
                if isinstance(w, int) and w == B - 1:
                    sp.wait_ge(s_ctx_lo, B * NC)
                    for j in range(2):
                        sp.dma_start(raw[j][:, :], w_moe[j, :, 0:GU]).then_inc(gu_in[j], 16)
                if isinstance(w, int) and w == B + 2:
                    sp.wait_ge(s_x2_out, 32 * (B - 1))
                    sp.dma_start(x_tok[:, 0:NT - 1, :], x2_dram[0:T - P, :].rearrange("(t p) d -> p t d", p=P)).then_inc(s_x2_in, 16)
                    sp.dma_start(x_tok[0:S, NT - 1, :], x2_dram[T - P:T - S, :]).then_inc(s_x2_in, 16)
                if ctx:
                    sp.wait_ge(s_ctx_lo, ctx_split)
                    load_ctx(w + 2)
                if lag0:
                    sp.wait_ge(s_x1_done, w)
                    sp.dma_start(batch_rows(x1_dram, w - 1), x1s).then_inc(s_x1_out, 16)
                if lag2:
                    sp.wait_ge(s_x2_done, w - 2)
                    for h in range(2):
                        if isinstance(w, int) and w == B + 2:
                            rows = x_tok[S:P, NT - 1, :].rearrange("s (j n) -> s j n", n=2 * P)[:, :, h * P:(h + 1) * P]
                            sp.dma_start(rows, half_rows(x2s, h)).then_inc(s_x2_last, 16)
                        else:
                            sp.dma_start(chunk_rows(x2_dram, w - 3, h), half_rows(x2s, h)).then_inc(s_x2_out, 16)
                if lag0:
                    if not (isinstance(w, int) and w == B):
                        sp.dma_start(x_in, batch_rows(xb_dram, w)).then_inc(s_xb_in, 16)
                    sp.wait_ge(s_bc_ready, w)
                    sp.dma_start(bc_dram[bass.ds(w - 1, 1)].rearrange("a r n -> (a r) n"), bc_sb[:, :]).then_inc(s_bc_out, 16)
                    sp.wait_ge(s_bc_out, w * 16)
                    if not (isinstance(w, int) and w == 1):
                        sp.wait_ge(s_drive_ready, w * KC - KC)
                    sp.dma_start(b_bc, bc_dram[bass.ds(w - 1, 1), 0:NS, :].rearrange("a r n -> (a r n)").partition_broadcast(P)).then_inc(s_b_in, 16)
                    if not (isinstance(w, int) and w == 1):
                        sp.wait_ge(s_hc_ready, w * KC - KC)
                    sp.dma_start(c_bc, bc_dram[bass.ds(w - 1, 1), NS:2 * NS, :].rearrange("a r n -> (a r n)").partition_broadcast(P)).then_inc(s_c_in, 16)

            sp.wait_ge(s_xb_ready, NT)
            sp.dma_start(xb_dram.rearrange("(t p) d -> p t d", p=P), x_tok[:, :, :]).then_inc(s_xb_out, 16)
            sp.wait_ge(s_w_lo, N_W)
            load_ctx(0)
            sp.wait_ge(s_ctx_lo, NC)
            load_ctx(1)
            sp.wait_ge(s_xb_out, 16)
            sp.wait_ge(s_o1_lo, NT)
            sp.dma_start(x_in, xb_dram[0:S, :]).then_inc(s_xb_in, 16)
            sp.wait_ge(s_no_slots_ready, 1)
            sp.dma_start(slot_dram.rearrange("(u s) c -> u s c", s=UT), no_slots).then_inc(s_slot_fill, 16)
            sp.dma_start(sum_dram[T:T + UT, :].rearrange("(p a) (c f) -> p (a c) f", p=P, f=P),
                         zero[:, :].unsqueeze(1).to_broadcast([P, UA * KC, P])).then_inc(s_slot_fill, 16)
            window(0, lag0=False, lag2=False)
            window(1, lag2=False)
            window(2, lag2=False)
            with sp.Fori(3, B - 2) as w:
                window(w)
            for w in range(B - 2, B + 3):
                window(w, ctx=w == B - 3, lag0=w <= B)
            sp.wait_ge(s_y_ready, B * KC)
            for j in range(2):
                sp.dma_start(raw_dn[j], w_moe[j, :, GU:]).then_inc(dn_in[j], 16)
            sp.wait_ge(s_plan_ready, 1)
            sp.dma_start(plan_dram, plan[:, :]).then_inc(s_plan_stored, 16)

            def expert_of(u):
                return sp.value_load(plan_dram[bass.ds(u, 1), 0:1], min_val=0, max_val=E - 1) + NSH

            def load_gate_up(u, j):
                expert = expert_of(u)
                sp.wait_ge(s_gu_lo, u + 1)
                sp.dma_start(raw[j][:, :], w_moe[bass.ds(expert, 1), :, 0:GU].rearrange("a p n -> (a p) n")).then_inc(gu_in[j], 16)

            def load_down(u, j):
                expert = expert_of(u)
                sp.wait_ge(s_dn_lo, u + 1)
                sp.dma_start(raw_dn[j], w_moe[bass.ds(expert, 1), :, GU:].rearrange("a p n -> (a p) n")).then_inc(dn_in[j], 16)

            def load_tokens(u, j):
                sp.dma_start(xg_tok[j], unit_rows(u_dram, u)).then_inc(xg_in[j], 16)

            last = last_pair(sp)
            for j in range(2):
                load_gate_up(j, j)
            sp.wait_ge(s_scattered, NT * TOPK * 16)
            for j in range(2):
                load_tokens(j, j)
            for j in range(2):
                load_down(j, j)
            load_gate_up(2, 0)
            sp.wait_ge(s_base_done, NT)
            sp.dma_start(sum_dram[0:T, :].rearrange("(t p) d -> p t d", p=P), x_tok[:, :, :]).then_inc(s_base_out, 16)
            with sp.Fori(0, last) as k:
                for j in range(2):
                    load_gate_up(k * 2 + (j + 3), 1 - j)
                    sp.wait_ge(s_xg_T, k * 2 + (j + 1))
                    load_tokens(k * 2 + (j + 2), j)
                    load_down(k * 2 + (j + 2), j)
            sp.wait_ge(s_gate, last * 4 + 7)
            sp.wait_ge(s_base_out, 16)
            sp.dma_start(out, sum_dram[0:T, :]).then_inc(s_out_done, 16)
            sp.wait_ge(s_out_done, 16)

        @block.gpsimd
        def _(pool):
            pool.memset(ident[:, :], 0.0).then_inc(s_consts, 1)
            pool.memset(mask[:, :], 0.0).then_inc(s_consts, 1)
            pool.memset(zero[:, :], 0.0).then_inc(s_consts, 1)
            pool.wait_ge(s_consts, 3)
            pool.affine_select(out=ident[:, :], in_=ident[:, :], compare_op=ALU.not_equal, fill=1.0, base=0,
                               pattern=[[-1, P]], channel_multiplier=1).then_inc(s_consts, 1)
            pool.affine_select(out=mask[:, :], in_=mask[:, :], compare_op=ALU.is_ge, fill=LOWEST, base=0,
                               pattern=[[-1, P]], channel_multiplier=1).then_inc(s_consts, 1)
            pool.wait_ge(s_consts, 5)
            pool.affine_select(out=mask[S:P, :], in_=mask[S:P, :], compare_op=ALU.is_ge, fill=LOWEST, base=-S,
                               pattern=[[1, P]], channel_multiplier=0).then_inc(s_consts, 1)
            pool.wait_ge(s_consts, 6)
            pool.memset(before[:, :], 1.0).then_inc(s_before_ready, 1)
            pool.memset(ones[:, :], 1.0).then_inc(s_before_ready, 1)
            pool.wait_ge(s_before_ready, 2)
            pool.affine_select(out=before[:, :], in_=before[:, :], compare_op=ALU.is_ge, fill=0.0, base=-1,
                               pattern=[[1, P]], channel_multiplier=-1).then_inc(s_before_ready, 1)
            for u in range(16):
                pool.wait_ge(s_s1_sum, u + 1)
                v = scr1[u % 3][:, :].rearrange("p (h k) -> p h k", h=GH)
                pool.tensor_tensor(v, v, rs[:, 4 * u:4 * u + 4].unsqueeze(2).to_broadcast([P, GH, P]),
                                   ALU.mult).then_inc(s_s1_norm, 1)
            def scan(m, step):
                first = isinstance(m, int) and m == 0
                if step == 6:
                    pool.wait_ge(s_dt_ready, m + 1)
                    if not first:
                        pool.wait_ge(s_drive_ready, m * KC)
                    pool.tensor_tensor(dt_x[:, :], dt_z[:, :], x2T[:, :], ALU.mult).then_inc(s_dtx_ready, 1)
                if step in (9, 11, 13, 15) and not (alone(m) and step in (11, 15)):
                    state_outputs(pool, m, (step - 9) // 2)
                if step in (6, 8, 10, 12):
                    c = (step - 6) // 2
                    if not (first and c < 2):
                        pool.wait_ge(s_scan_done, m * KC + (c - 1))
                    pool.tensor_tensor(decay[c % 2], a_pos[:, c, :].unsqueeze(2).to_broadcast([P, NS, S]),
                                       over_states(dt_z, c), ALU.mult).then_inc(s_decay_arg, 1)
                if step in (7, 9, 11, 13) and not alone(m):
                    state_inputs(pool, m, (step - 7) // 2)

            run_batches(pool, None, None, None, scan)

            pool.wait_ge(s_fill, 8 * 16)
            pool.wait_ge(s_idx_ready, 1)
            for n in range(NT * TOPK):
                pool.indirect_dma_start(u_dram, bass.IndirectOffsetOnAxis(row_idx[:, n:n + 1], 0),
                                        xn_all[:, n // TOPK, :], None).then_inc(s_scattered, 16)
            pool.wait_ge(s_slot_fill, 2 * 16)
            pool.wait_ge(s_slots_ready, 1)
            for n in range(NT * TOPK):
                pool.indirect_dma_start(slot_dram, bass.IndirectOffsetOnAxis(row_idx[:, n:n + 1], 0),
                                        slots[:, n, :], None).then_inc(s_slots_put, 16)

            def load_slots(u, j):
                pool.dma_start(slot[j][:, :, :].rearrange("p a c -> p (a c)"), unit_rows(slot_dram, u)).then_inc(slot_in[j], 16)

            def gate(n):
                pool.wait_ge(s_gate, n + 3)
                pool.tensor_tensor(gate_out[:, :], zero[:, 0:1], zero[:, 0:1], ALU.add).then_inc(s_gate, 1)

            def add_outputs(u, j, k):
                pool.wait_ge(s_y_evac, u + 2)
                pool.wait_ge(slot_in[j], k * 16 + 16)
                gate(u * 2)
                for a in range(UA):
                    pool.indirect_dma_start(sum_dram, bass.IndirectOffsetOnAxis(slot[j][:, a, 1:2], 0),
                                            y_sb[j][:, a * D:(a + 1) * D], None, compute_op=ALU.add).then_inc(added[j], 16)
                pool.wait_ge(added[j], (k + 1) * (16 * UA))
                gate(u * 2 + 1)

            for n in range(3):
                pool.nop().then_inc(s_gate, 1)
            pool.wait_ge(s_base_out, 16)
            pool.wait_ge(s_slots_put, NT * TOPK * 16)
            for j in range(2):
                load_slots(j, j)
            last_k = last_pair(pool)
            with pool.Fori(0, last_k) as k:
                for j in range(2):
                    add_outputs(k * 2 + j, j, k)
                    load_slots(k * 2 + (j + 2), j)
            for j in range(2):
                add_outputs(last_k * 2 + j, j, last_k)

        @block.scalar
        def _(act):
            act.preload_act_table_set("natural_log_exp_and_others")
            def split_weight(n):
                act.wait_ge(w_in[n % 2], 16 * (n // 2 + 1))
                if n == WQ2:
                    act.wait_ge(s_p1_ready, 12)
                if n == WK2:
                    act.wait_ge(s_p1_ready, 4)
                if n == WV2:
                    act.wait_ge(s_p1_ready, 8)
                act.activation(w_of[n][0].rearrange("p k n -> p (k n)"), raw[n % 2][:, :], ACT.Copy).then_inc(s_w_hi, 1)

            def rstd(ve, r0, tmpv, waited, count, sem_out, step):
                act.wait_ge(waited, count)
                act.activation(tmpv, ve, ACT.Ln).then_inc(step, 1)
                act.wait_ge(step, count)
                act.activation(r0, tmpv, ACT.Exp, scale=-0.5).then_inc(sem_out, 1)

            rstd(ln[:, 0, :], ln[:, 1, :], ln[:, 2, :], s_ln_ve, 1, s_ln_r0, s_ln_step)
            split_weight(WQ1)
            for kc in range(KC):
                act.wait_ge(s_xnT_ready, NT)
                act.activation(xT[0][:, kc, :], bank[kc][:, :], ACT.Copy).then_inc(s_xT_hi, 1)
            split_weight(WK1)
            split_weight(WV1)
            split_weight(WO1)
            act.wait_ge(s_small_in, 64)
            act.activation(a_pos[:, :, :], smallp[:, ALOG:ALOG + KC * NS].rearrange("p (c n) -> p c n", c=KC),
                           ACT.Exp).then_inc(s_a_ready, 1)
            for n in (8, 9, 10, 11):
                act.wait_ge(s_p1_ready, n + 1)
                act.activation(v1[:, n - 8, :], bank[n % 8][:, :], ACT.Copy).then_inc(s_p1_out, 1)

            def hi_ctx(n, t):
                act.wait_ge(s_ctx_in, n * 16 + 16)
                act.activation(ctxT[0][:, :, t * P:(t + 1) * P], raw_ctx[:, :, t * P:(t + 1) * P], ACT.Copy).then_inc(s_ctx_hi, 1)

            def exp1(u):
                act.wait_ge(s_s1_max, u + 1)
                for g in range(GH):
                    e = act.activation(scr1[u % 3][:, g * P:(g + 1) * P], scr1[u % 3][:, g * P:(g + 1) * P], ACT.Exp,
                                       bias=nm[:, 4 * (u % 3) + g:4 * (u % 3) + g + 1], accum_out=sm[:, 4 * u + g:4 * u + g + 1])
                e.then_inc(s_s1_exp, 1)

            def pt1(u):
                act.wait_ge(s_s1_T, u + 1)
                if u >= 3:
                    act.wait_ge(s_s1_pv, u - 2)
                act.activation(pT1[u % 3][:, :], bank[TRANSPOSED[u % 3]][:, :], ACT.Copy).then_inc(s_s1_pT, 1)

            def o1_hi(t):
                act.wait_ge(s_o1_sum, t + 1)
                act.activation(o1T[0][:, :, t * P:(t + 1) * P], tmp[2 + t % 2][:, :].rearrange("p (g n) -> p g n", g=KC),
                               ACT.Copy).then_inc(s_o1_hi, 1)

            for u in range(3):
                exp1(u)
            for u in range(16):
                pt1(u)
                if u + 3 < 16:
                    exp1(u + 3)
                if u % 4 == 1 and u > 4:
                    o1_hi(u // 4 - 1)
                if u in split_at:
                    split_weight(split_at[u])
            o1_hi(3)
            for m in range(KC):
                act.wait_ge(s_h_ready, m + 1)
                act.activation(hT[0][:, m, :], bank[m][:, :], ACT.Identity, bias=bias(BO1 + m)).then_inc(s_h_hi, 1)
            for t in range(NC):
                hi_ctx(0, t)
            act.wait_ge(s_q2_out, KC)
            for n in range(2):
                act.nop().then_inc(s_s2_exp, 1)
            act.nop().then_inc(s_o2_out, 1)

            def hi_kv(b, k):
                act.wait_ge(s_kv_ready, b * 8 + (k + 1))
                if k < 4:
                    act.activation(k2[0][:, k, :], bank[k % 2][:, :], ACT.Identity, bias=bias(BK2 + k)).then_inc(s_kv_hi, 1)
                else:
                    act.activation(v2[0][:, k - 4, :], bank[k % 2][:, :], ACT.Copy).then_inc(s_kv_hi, 1)

            def hi_gu(n, j, k):
                act.wait_ge(gu_in[j], k * 16 + 16)
                if not (isinstance(n, int) and n < 2):
                    act.wait_ge(s_gu_ready, n * 2 - 2)
                act.activation(gu_w[j][0], raw[j][:, :], ACT.Copy).then_inc(s_gu_hi, 1)

            def hi_query(b):
                for i in range(GH):
                    act.activation(qb[0][HD * i:HD * (i + 1), :, i // 2, (i % 2) * S:(i % 2 + 1) * S],
                                   q2[HD * i:HD * (i + 1), :, bass.ds(b * S, S)], ACT.Copy).then_inc(s_qb_hi, 1)

            def exp2(b, u):
                act.wait_ge(s_s2_max, b * 8 + (u + 1))
                act.wait_ge(s_s2_T, b * 8 + (u + 1))
                act.activation(prob[u % 2][:, :], bank[2 + u % 2][:, :], ACT.Exp, bias=nm[:, u:u + 1],
                               accum_out=sm[:, u:u + 1]).then_inc(s_s2_exp, 1)

            def normalise(b, u):
                act.wait_ge(s_s2_sum, b * 8 + (u + 1))
                act.activation(prob[u % 2][:, :], prob[u % 2][:, :], ACT.Copy, scale=rs[:, u:u + 1]).then_inc(s_s2_norm, 1)

            def head_outputs(b, g):
                act.wait_ge(s_pv_ready, b * 4 + (g + 1))
                for i in range(GH):
                    r = slice(HD * i, HD * (i + 1))
                    last = act.activation(o2f[r, g * S:(g + 1) * S], bank[6][r, i * S:(i + 1) * S], ACT.Identity,
                                          bias=smallp[r, BV2 + g:BV2 + g + 1])
                last.then_inc(s_o2_out, 1)

            def start():
                for k in range(4):
                    hi_kv(0, k)
                act.wait_ge(s_consts, 8)
                hi_query(0)
                advance(-1, True)

            def attend(b, u, more):
                act.wait_ge(s_s2_T, b * 8 + (u + 3))
                if u >= 2 and u % 2 == 0:
                    act.wait_ge(s_pv_ready, b * 4 + u // 2)
                act.activation(pT[0][:, :, (u % 2) * P:(u % 2 + 1) * P],
                               bank[4 + u % 2][:, :].rearrange("p (c n) -> p c n", c=4), ACT.Copy).then_inc(s_pT_hi, 1)
                if u + 2 < 8:
                    exp2(b, u + 2)
                    normalise(b, u + 2)
                if u >= 2 and u % 2 == 0:
                    head_outputs(b, u // 2 - 1)
                if u % 2 == 1 and more:
                    hi_kv(b + 1, u // 2)
                if u in (3, 5) and not more:
                    hi_gu(u // 4, u // 4, 0)
                if u == 6 and more:
                    hi_query(b + 1)

            def advance(b, more, ahead=True):
                if more:
                    exp2(b + 1, 0)
                    exp2(b + 1, 1)
                    normalise(b + 1, 0)
                    normalise(b + 1, 1)
                if not (isinstance(b, int) and b < 0):
                    head_outputs(b, 3)
                if more:
                    for k in range(4, 8):
                        hi_kv(b + 1, k)
                        if ahead:
                            hi_ctx(b + 2, k - 4)

            def scan(m, step):
                if step == 1:
                    act.wait_ge(s_ln2_ve, m + 1)
                    act.activation(ln2[:, 2:3], ln2[:, 0:1], ACT.Ln).then_inc(s_ln2_step, 1)
                    act.wait_ge(s_ln2_step, m + 1)
                    act.activation(ln2[:, 1:2], ln2[:, 2:3], ACT.Exp, scale=-0.5).then_inc(s_ln2_r0, 1)
                if step == 3:
                    act.wait_ge(s_x2T_ready, m + 1)
                    act.activation(x2T[:, :].rearrange("p (k n) -> p k n", k=KC),
                                   bank[7][:, :].rearrange("p (k n) -> p k n", k=KC)[:, :, 0:S], ACT.Copy).then_inc(s_x2T_out, 1)
                if step == 4:
                    act.wait_ge(s_xp_ready, m + 1)
                    act.activation(dtr[:, :], bank[7][0:RANK, S:2 * S], ACT.Copy).then_inc(s_dtr_ready, 1)
                    if not (isinstance(m, int) and m == 0):
                        act.wait_ge(s_bc_out, m * 16)
                    act.activation(bc_sb[:, :], bank[7][0:2 * NS, 0:S], ACT.Copy).then_inc(s_bc_ready, 1)
                if step == 5:
                    act.wait_ge(s_dt_z_ready, m + 1)
                    act.activation(dt_e[:, :], dt_z[:, :], ACT.Abs).then_inc(s_dt_step, 1)
                    act.wait_ge(s_dt_step, m * 3 + 1)
                    act.activation(dt_e[:, :], dt_e[:, :], ACT.Exp, scale=-1.0).then_inc(s_dt_step, 1)
                    act.wait_ge(s_dt_step, m * 3 + 2)
                    act.activation(dt_e[:, :], dt_e[:, :], ACT.Ln, bias=1.0).then_inc(s_dt_step, 1)
                if step in (7, 9, 11, 13):
                    c = (step - 7) // 2
                    act.wait_ge(s_decay_arg, m * KC + (c + 1))
                    act.activation(decay[c % 2], decay[c % 2], ACT.Exp, scale=-1.0).then_inc(s_decay_exp, 1)

            run_batches(act, start, attend, advance, scan)

            act.wait_ge(s_gate_in, 32)
            act.activation(gw[0][:, :, :], gw_raw[:, :, :], ACT.Copy).then_inc(s_gw_hi, 1)
            rstd(ln[:, 0, :], ln[:, 1, :], ln[:, 2, :], s_ln3_ve, 1, s_ln3_r0, s_ln3_step)

            def hi_dn(n, j, k):
                act.wait_ge(dn_in[j], k * 16 + 16)
                if not (isinstance(n, int) and n < 2):
                    act.wait_ge(s_dn_done, n - 1)
                act.activation(dn_w[j][0], raw_dn[j], ACT.Copy).then_inc(s_dn_hi, 1)

            def shared_activations(n):
                for i in range(IC):
                    act.wait_ge(s_gu_ready, 2 * n + i + 1)
                    if n:
                        act.wait_ge(s_h_ready2, i + 1)
                    act.activation(silu[i][:, :], bank[2 * i][:, :], ACT.Silu).then_inc(s_silu_done, 1)
                for i in range(IC):
                    act.wait_ge(s_h_ready2, 2 * n + i + 1)
                    last = act.activation(inner[n][0][:, i, :], act_f[i][:, :], ACT.Copy)
                last.then_inc(s_act_hi, 1)

            def activations(u, j):
                for i in range(IC):
                    act.wait_ge(s_gu_ready, u * 2 + (5 + i))
                    act.wait_ge(s_h_ready2, u * 2 + (3 + i))
                    act.activation(silu[i][:, 0:UT], bank[2 * j + i][:, 0:UT], ACT.Silu).then_inc(s_silu_done, 1)
                act.wait_ge(s_h_ready2, u * 2 + 6)
                act.wait_ge(s_dn_done, u + 1)
                act.activation(inner[j][0][:, :, 0:UT], unit_act, ACT.Copy).then_inc(s_act_hi, 1)

            def hi_tokens(u, j):
                act.wait_ge(s_xg_T, u + 1)
                act.wait_ge(s_gu_ready, u * 2 + 2)
                for i in range(2):
                    act.activation(xg[j][0][:, 2 * i:2 * i + 2, :], bank[token_bank(u) + i][:, 0:2 * UT].rearrange("p (c n) -> p c n", c=2),
                                   ACT.Copy).then_inc(s_xg_hi, 1)

            def outputs(u, j, k):
                act.wait_ge(s_dn_done, u + 3)
                act.wait_ge(s_gate, u * 2 + 1)
                act.wait_ge(slot_in[j], k * 16 + 16)
                for a in range(UA):
                    last = act.activation(y_sb[j][:, a * D:(a + 1) * D], bank[4 + a][:, :], ACT.Copy,
                                          scale=slot[j][:, a, 0:1].bitcast(fp32))
                last.then_inc(s_y_evac, 1)

            for kc in range(KC):
                act.wait_ge(s_xn3T_ready, NT)
                act.activation(xT[0][:, kc, :], bank[kc][:, :], ACT.Copy).then_inc(s_x3_hi, 1)
            for n in range(2):
                hi_dn(n, n, 0)
            act.wait_ge(s_logitT_ready, 1)
            act.activation(logitT, bank[4][0:E, :], ACT.Copy).then_inc(s_logitT_out, 1)
            act.wait_ge(s_logit_ready, 1)
            act.activation(rt[:, 0, :, :], bank[5][:, 0:NT * E].rearrange("p (t e) -> p t e", t=NT), ACT.Exp, scale=-1.0).then_inc(s_r_exp, 1)
            act.nop().then_inc(s_y_evac, 1)
            shared_activations(0)
            hi_gu(2, 0, 1)
            shared_activations(1)
            hi_gu(3, 1, 1)
            hi_dn(2, 0, 1)
            hi_dn(3, 1, 1)
            hi_tokens(0, 0)
            activations(0, 0)
            hi_tokens(1, 1)
            hi_gu(4, 0, 2)
            last_k = last_pair(act)
            with act.Fori(0, last_k) as k:
                for j in range(2):
                    activations(k * 2 + (j + 1), 1 - j)
                    hi_tokens(k * 2 + (j + 2), j)
                    hi_gu(k * 2 + (j + 5), 1 - j, k + (j + 2))
                    outputs(k * 2 + j, j, k)
                    hi_dn(k * 2 + (j + 4), j, k + 2)
            activations(last_k * 2 + 1, 1)
            for j in range(2):
                outputs(last_k * 2 + j, j, last_k)

        @block.vector
        def _(dve):
            for n in range(2):
                dve.nop().then_inc(s_kv_lo, 1)
            for n in range(2):
                dve.nop().then_inc(s_pT_lo, 1)

            def lo_weight(n):
                dve.wait_ge(s_w_hi, n + 1)
                dve.tensor_tensor(w_of[n][1].rearrange("p k n -> p (k n)"), raw[n % 2][:, :],
                                  w_of[n][0].rearrange("p k n -> p (k n)").bitcast(fp32), ALU.subtract).then_inc(s_w_lo, 1)

            def newton(ve, r0, a, r, waited, count, step, base):
                dve.wait_ge(waited, count)
                dve.tensor_tensor(a, r0, r0, ALU.mult).then_inc(step, 1)
                dve.wait_ge(step, base + 1)
                dve.tensor_tensor(a, a, ve, ALU.mult).then_inc(step, 1)
                dve.wait_ge(step, base + 2)
                dve.tensor_scalar(a, a, -0.5, 1.5, ALU.mult, ALU.add).then_inc(step, 1)
                dve.wait_ge(step, base + 3)
                dve.tensor_tensor(r, a, r0, ALU.mult).then_inc(step, 1)
                dve.wait_ge(step, base + 4)

            dve.wait_ge(s_x_in, 16)
            for t in range(NT):
                dve.bn_stats(st[:, t, :], x_tok[:, t, :]).then_inc(s_xn_ready, 1)
            dve.wait_ge(s_xn_ready, 4)
            for t in range(NT):
                dve.bn_aggr(mv[:, t, :], st[:, t, :]).then_inc(s_xn_ready, 1)
            dve.wait_ge(s_xn_ready, 8)
            dve.tensor_scalar(ln[:, 0, :], mv[:, :, 1], EPS, None, ALU.add).then_inc(s_ln_ve, 1)
            dve.wait_ge(s_ln_ve, 1)
            newton(ln[:, 0, :], ln[:, 1, :], ln[:, 3, :], ln[:, 4, :], s_ln_r0, 1, s_xn_ready, 8)
            for t in range(NT):
                dve.tensor_scalar(xn_all[:, t, :], x_tok[:, t, :], mv[:, t, 0:1], ln[:, 4, t:t + 1],
                                  ALU.subtract, ALU.mult).then_inc(s_xn_ready, 1)
            lo_weight(WQ1)
            for kc in range(KC):
                dve.wait_ge(s_xT_hi, kc + 1)
                dve.tensor_tensor(xT[1][:, kc, :], bank[kc][:, :], xT[0][:, kc, :].bitcast(fp32), ALU.subtract).then_inc(s_xT_lo, 1)
            lo_weight(WK1)
            dve.wait_ge(s_small_in, 64)
            for t in range(NT):
                dve.tensor_tensor(x_tok[:, t, :], x_tok[:, t, :], bo2_bc[:, :], ALU.add).then_inc(s_xb_ready, 1)
            lo_weight(WV1)
            for n in range(8):
                dve.wait_ge(s_p1_ready, n + 1)
                if n < 4:
                    dve.tensor_scalar(q1[:, n, :], bank[4 + n][:, :], bias(BQ1 + n), QSCALE, ALU.add, ALU.mult).then_inc(s_s1_out, 1)
                else:
                    dve.tensor_scalar(k1[:, n - 4, :], bank[n - 4][:, :], bias(BK1 + n - 4), None, ALU.add).then_inc(s_s1_out, 1)
            lo_weight(WO1)

            def lo_ctx(n, t):
                part = (slice(None), slice(None), slice(t * P, (t + 1) * P))
                dve.wait_ge(s_ctx_hi, n * NC + (t + 1))
                dve.tensor_tensor(ctxT[1][part], raw_ctx[part], ctxT[0][part].bitcast(fp32), ALU.subtract).then_inc(s_ctx_lo, 1)

            def soft1(u):
                dve.wait_ge(s_s1_ready, u + 1)
                dve.tensor_tensor(scr1[u % 3][:, :].rearrange("p (h k) -> p h k", h=GH),
                                  bank[SCORES[u % 3]][:, :].rearrange("p (h k) -> p h k", h=GH),
                                  mask[:, :].unsqueeze(1).to_broadcast([P, GH, P]), ALU.add).then_inc(s_s1_out, 1)
                dve.wait_ge(s_s1_out, 8 + u + 1)
                dve.tensor_reduce(nm[:, 4 * (u % 3):4 * (u % 3) + 4], scr1[u % 3][:, :].rearrange("p (h k) -> p h k", h=GH),
                                  AX.X, ALU.max, negate=True).then_inc(s_s1_max, 1)

            def recip1(u):
                dve.wait_ge(s_s1_exp, u + 1)
                dve.reciprocal(rs[:, 4 * u:4 * u + 4], sm[:, 4 * u:4 * u + 4]).then_inc(s_s1_sum, 1)

            def o1_tile(t):
                dve.wait_ge(s_s1_pv, 4 * t + 4)
                if t >= 2:
                    dve.wait_ge(s_o1_lo, t - 1)
                dve.tensor_tensor(tmp[2 + t % 2][:, :].rearrange("p (g n) -> p g n", g=KC),
                                  bank[4 + t % 2][:, :].rearrange("p (g n) -> p g n", g=KC),
                                  smallp[:, BV1:BV1 + KC].unsqueeze(2).to_broadcast([P, KC, P]), ALU.add).then_inc(s_o1_sum, 1)
                dve.wait_ge(s_o1_hi, t + 1)
                dve.tensor_tensor(o1T[1][:, :, t * P:(t + 1) * P], tmp[2 + t % 2][:, :].rearrange("p (g n) -> p g n", g=KC),
                                  o1T[0][:, :, t * P:(t + 1) * P].bitcast(fp32), ALU.subtract).then_inc(s_o1_lo, 1)

            for u in range(3):
                soft1(u)
            recip1(0)
            dve.memset(post[0:MAXU, 0:2 * UT], 0.0).then_inc(s_no_slots, 1)
            dve.wait_ge(s_before_ready, 3)
            for h in range(UT // P):
                dve.tensor_tensor_scan(post[0:MAXU, 1024 + h * P:1024 + (h + 1) * P], ones[0:MAXU, :], ones[0:MAXU, :],
                                       float(T + h * P - 1), ALU.mult, ALU.add).then_inc(s_no_slots, 1)
            dve.wait_ge(s_no_slots, 1 + UT // P)
            dve.tensor_copy(no_slots[:, :, 1], post[0:MAXU, 1024:1024 + UT]).then_inc(s_no_slots_ready, 1)
            for u in range(16):
                if u + 1 < 16:
                    recip1(u + 1)
                if u + 3 < 16:
                    dve.wait_ge(s_s1_T, u + 1)
                    soft1(u + 3)
                if u % 4 == 1 and u > 4:
                    o1_tile(u // 4 - 1)
                if u - 2 in split_at:
                    lo_weight(split_at[u - 2])
            o1_tile(3)
            for m in range(KC):
                dve.wait_ge(s_h_hi, m + 1)
                dve.scalar_tensor_tensor(hT[1][:, m, :], bank[m][:, :], bias(BO1 + m), hT[0][:, m, :].bitcast(fp32),
                                         ALU.add, ALU.subtract).then_inc(s_h_lo, 1)
            for t in range(NC):
                lo_ctx(0, t)
            for m in range(KC):
                dve.wait_ge(s_q2_ready, m + 1)
                dve.tensor_scalar(q2[:, m, :], bank[4 + m][:, :], bias(BQ2 + m), QSCALE, ALU.add, ALU.mult).then_inc(s_q2_out, 1)
            def lo_kv(b, k):
                dve.wait_ge(s_kv_hi, b * 8 + (k + 1))
                if k < 4:
                    dve.scalar_tensor_tensor(k2[1][:, k, :], bank[k % 2][:, :], bias(BK2 + k), k2[0][:, k, :].bitcast(fp32),
                                             ALU.add, ALU.subtract).then_inc(s_kv_lo, 1)
                else:
                    dve.tensor_tensor(v2[1][:, k - 4, :], bank[k % 2][:, :], v2[0][:, k - 4, :].bitcast(fp32),
                                      ALU.subtract).then_inc(s_kv_lo, 1)

            def max2(b, u):
                dve.wait_ge(s_s2_ready, b * 8 + (u + 1))
                dve.tensor_reduce(nm[:, u:u + 1], bank[2 + u % 2][:, :], AX.X, ALU.max, negate=True).then_inc(s_s2_max, 1)

            def recip2(b, u):
                dve.wait_ge(s_s2_exp, b * 8 + (u + 3))
                dve.reciprocal(rs[:, u:u + 1], sm[:, u:u + 1]).then_inc(s_s2_sum, 1)

            def lo_gu(n, j):
                dve.wait_ge(s_gu_hi, n + 1)
                dve.tensor_tensor(gu_w[j][1], raw[j][:, :], gu_w[j][0].bitcast(fp32), ALU.subtract).then_inc(s_gu_lo, 1)

            def lo_query(b):
                for i in range(GH):
                    dve.wait_ge(s_qb_hi, b * 4 + (i + 1))
                    blk = (slice(HD * i, HD * (i + 1)), slice(None), i // 2, slice((i % 2) * S, (i % 2 + 1) * S))
                    dve.tensor_tensor(qb[1][blk], q2[HD * i:HD * (i + 1), :, bass.ds(b * S, S)], qb[0][blk].bitcast(fp32),
                                      ALU.subtract).then_inc(s_qb_lo, 1)

            def start():
                for k in range(4):
                    lo_kv(0, k)
                for n in range(2):
                    dve.memset(qb[n].rearrange("p g h q -> p (g h q)").bitcast(fp32), 0.0).then_inc(s_consts, 1)
                dve.wait_ge(s_consts, 8)
                lo_query(0)
                advance(-1, True)

            def attend(b, u, more):
                if u + 2 < 8:
                    max2(b, u + 2)
                dve.wait_ge(s_pT_hi, b * 8 + (u + 1))
                dve.tensor_tensor(pT[1][:, :, (u % 2) * P:(u % 2 + 1) * P],
                                  bank[4 + u % 2][:, :].rearrange("p (c n) -> p c n", c=4),
                                  pT[0][:, :, (u % 2) * P:(u % 2 + 1) * P].bitcast(fp32), ALU.subtract).then_inc(s_pT_lo, 1)
                if u + 2 < 8:
                    recip2(b, u + 2)
                if u % 2 == 1 and more:
                    lo_kv(b + 1, u // 2)
                if u in (3, 5) and not more:
                    lo_gu(u // 4, u // 4)
                if u == 6 and more:
                    lo_query(b + 1)

            def advance(b, more, ahead=True):
                if more:
                    max2(b + 1, 0)
                    max2(b + 1, 1)
                    recip2(b + 1, 0)
                    recip2(b + 1, 1)
                    for k in range(4, 8):
                        lo_kv(b + 1, k)
                        if ahead:
                            lo_ctx(b + 2, k - 4)

            def scan(m, step):
                first = isinstance(m, int) and m == 0
                if step == 1:
                    dve.wait_ge(s_wo2_ready, m + 1)
                    dve.wait_ge(s_xb_in, m * 16 + 16)
                    if not first:
                        dve.wait_ge(s_x1_out, m * 16)
                    dve.tensor_tensor(x1s, x_in, bank[7][0:S, :], ALU.add).then_inc(s_x1_done, 1)
                    dve.wait_ge(s_x1_done, m + 1)
                    dve.bn_stats(st2[:, 0:6], x1s).then_inc(s_ln2_stat, 1)
                    dve.wait_ge(s_ln2_stat, m * 6 + 1)
                    dve.tensor_tensor(st2[:, 6:9], st2[:, 0:3], st2[:, 3:6], ALU.add).then_inc(s_ln2_stat, 1)
                    dve.tensor_tensor(st2[:, 9:10], st2[:, 1:2], st2[:, 4:5], ALU.subtract).then_inc(s_ln2_stat, 1)
                    dve.wait_ge(s_ln2_stat, m * 6 + 3)
                    dve.tensor_scalar(ln2[:, 5:6], st2[:, 7:8], 0.5, None, ALU.mult).then_inc(s_ln2_stat, 1)
                    dve.tensor_scalar(st2[:, 10:11], st2[:, 8:9], 1.0 / D, EPS, ALU.mult, ALU.add).then_inc(s_ln2_stat, 1)
                    dve.scalar_tensor_tensor(st2[:, 11:12], st2[:, 9:10], 0.25, st2[:, 9:10], ALU.mult, ALU.mult).then_inc(s_ln2_stat, 1)
                    dve.wait_ge(s_ln2_stat, m * 6 + 6)
                    dve.tensor_tensor(ln2[:, 0:1], st2[:, 10:11], st2[:, 11:12], ALU.add).then_inc(s_ln2_ve, 1)
                if step == 2:
                    newton(ln2[:, 0:1], ln2[:, 1:2], ln2[:, 3:4], ln2[:, 4:5], s_ln2_r0, m + 1, s_xn2_ready, m * 5)
                    dve.tensor_scalar(xn2, x1s, ln2[:, 5:6], ln2[:, 4:5], ALU.subtract, ALU.mult).then_inc(s_xn2_ready, 1)
                if step == 5:
                    dve.wait_ge(s_dtp_ready, m + 1)
                    if not first:
                        dve.wait_ge(s_decay_arg, m * KC)
                    dve.tensor_tensor(dt_z[:, :].rearrange("p (c n) -> p c n", c=KC), bank[7][:, 0:KC * S].rearrange("p (c n) -> p c n", c=KC),
                                      smallp[:, BDT:BDT + KC].unsqueeze(2).to_broadcast([P, KC, S]), ALU.add).then_inc(s_dt_z_ready, 1)
                if step == 6:
                    dve.wait_ge(s_dt_step, m * 3 + 3)
                    dve.scalar_tensor_tensor(dt_z[:, :], dt_z[:, :], 0.0, dt_e[:, :], ALU.max, ALU.add).then_inc(s_dt_ready, 1)
                if step in (7, 9, 11, 13) and alone(m):
                    state_inputs(dve, m, (step - 7) // 2)
                if step in (11, 15) and alone(m):
                    state_outputs(dve, m, (step - 9) // 2)
                if step in (8, 10, 12, 14):
                    c = (step - 8) // 2
                    dve.wait_ge(s_decay_exp, m * KC + (c + 1))
                    dve.memset(decay[c % 2][:, :, 0:1], 0.0).then_inc(s_decay_zero, 1)
                    dve.wait_ge(s_decay_zero, m * KC + (c + 1))
                    dve.wait_ge(s_drive_ready, m * KC + (c + 1))
                    flat = drive[c % 2].rearrange("p s n -> p (s n)")
                    dve.tensor_tensor_scan(flat, decay[c % 2].rearrange("p s n -> p (s n)"), flat, 0.0,
                                           ALU.mult, ALU.add).then_inc(s_scan_done, 1)
                if step in (10, 12, 14, 16):
                    c = (step - 10) // 2
                    dve.wait_ge(s_hc_ready, m * KC + (c + 1))
                    if c == 0 and not first:
                        dve.wait_ge(s_yT_ready, m)
                    dve.tensor_reduce(yT[:, c * S:(c + 1) * S], drive[c % 2].rearrange("p s n -> p n s"),
                                      AX.X, ALU.add).then_inc(s_y_ready, 1)
                if step == 18:
                    dve.wait_ge(s_yT_ready, m + 1)
                    dve.wait_ge(s_x1r_in, m * 32 + 32)
                    if not first:
                        dve.wait_ge(s_x2_out, m * 32)
                    dve.tensor_tensor(x2s, x1r, bank[7][:, 0:KC * S], ALU.add).then_inc(s_x2_done, 1)

            run_batches(dve, start, attend, advance, scan)

            dve.wait_ge(s_gw_hi, 1)
            dve.tensor_tensor(gw[1][:, :, :], gw_raw[:, :, :], gw[0][:, :, :].bitcast(fp32), ALU.subtract).then_inc(s_gw_lo, 1)
            dve.wait_ge(s_x2_in, 32)
            for t in range(NT):
                if t == NT - 1:
                    dve.wait_ge(s_x2_last, 32)
                dve.bn_stats(st[:, t, :], x_tok[:, t, :]).then_inc(s_ln3, 1)
            dve.wait_ge(s_ln3, NT)
            for t in range(NT):
                dve.bn_aggr(mv[:, t, :], st[:, t, :]).then_inc(s_ln3, 1)
            dve.wait_ge(s_ln3, 2 * NT)
            dve.tensor_scalar(ln[:, 0, :], mv[:, :, 1], EPS, None, ALU.add).then_inc(s_ln3_ve, 1)
            newton(ln[:, 0, :], ln[:, 1, :], ln[:, 3, :], ln[:, 4, :], s_ln3_r0, 1, s_ln3, 2 * NT)
            for t in range(NT):
                dve.tensor_scalar(xn_all[:, t, :], x_tok[:, t, :], mv[:, t, 0:1], ln[:, 4, t:t + 1],
                                  ALU.subtract, ALU.mult).then_inc(s_xn3_ready, 1)
            for kc in range(KC):
                dve.wait_ge(s_x3_hi, kc + 1)
                dve.tensor_tensor(xT[1][:, kc, :], bank[kc][:, :], xT[0][:, kc, :].bitcast(fp32), ALU.subtract).then_inc(s_x3_lo, 1)

            def lo_dn(e, j):
                dve.wait_ge(s_dn_hi, e + 1)
                dve.tensor_tensor(dn_w[j][1], raw_dn[j], dn_w[j][0].bitcast(fp32), ALU.subtract).then_inc(s_dn_lo, 1)

            for n in range(2):
                lo_dn(n, n)

            steps = [0]

            def link(ins):
                steps[0] += 1
                ins.then_inc(s_r_step, 1)
                dve.wait_ge(s_r_step, steps[0])

            sg, sc, ch, mk, wt = [rt[:, n, :, :] for n in range(5)]
            gs, c1, rank, gm = [grp[:, n, :, :] for n in range(4)]
            dve.wait_ge(s_r_exp, 1)
            link(dve.tensor_scalar(sg, sg, 1.0, None, ALU.add))
            link(dve.reciprocal(sc, sg))
            link(dve.tensor_tensor(ch, sc, gb_bc[:, :].unsqueeze(1).to_broadcast([P, NT, E]), ALU.add))
            for t in range(NT):
                for g in range(NG):
                    last = dve.max(top[:, t, g, :], ch[:, t, g * EG:(g + 1) * EG])
            link(last)
            link(dve.tensor_tensor(gs, top[:, :, :, 0], top[:, :, :, 1], ALU.add))
            for g in range(NG):
                last = dve.memset(rank[:, :, g:g + 1], float(g))
            link(last)
            for d in range(1, NG):
                link(dve.tensor_tensor(c1[:, :, 0:NG - d], gs[:, :, d:NG], gs[:, :, 0:NG - d], ALU.is_gt))
                link(dve.tensor_tensor(rank[:, :, 0:NG - d], rank[:, :, 0:NG - d], c1[:, :, 0:NG - d], ALU.add))
                link(dve.tensor_tensor(rank[:, :, d:NG], rank[:, :, d:NG], c1[:, :, 0:NG - d], ALU.subtract))
            link(dve.tensor_scalar(gm, rank, 1.5, None, ALU.is_lt))
            link(dve.tensor_tensor(mk.rearrange("p t (g e) -> p t g e", g=NG), ch.rearrange("p t (g e) -> p t g e", g=NG),
                                   gm.unsqueeze(3).to_broadcast([P, NT, NG, EG]), ALU.mult))
            for t in range(NT):
                last = dve.max(top8[:, t, :], mk[:, t, :])
            link(last)
            for t in range(NT):
                last = dve.match_replace(wt[:, t, :], top8[:, t, :], mk[:, t, :], LOWEST)
            link(last)
            link(dve.tensor_tensor(mk, wt, mk, ALU.not_equal))
            dve.nop().then_inc(s_mask_ready, 1)
            link(dve.tensor_tensor(wt, mk, sc, ALU.mult))
            link(dve.tensor_reduce(rsum[:, :], wt, AX.X, ALU.add))
            link(dve.tensor_scalar(rsum[:, :], rsum[:, :], 1e-20, None, ALU.add))
            link(dve.reciprocal(rsum[:, :], rsum[:, :]))
            link(dve.tensor_tensor(wt, wt, rsum[:, :].unsqueeze(2).to_broadcast([P, NT, E]), ALU.mult))
            dve.tensor_scalar(wt, wt, ROUTED_SCALING, None, ALU.mult).then_inc(s_w_ready, 1)

            dve.wait_ge(s_pos_ready, 1)
            tokens_of = bank[5][:, NT * E:(NT + 1) * E]
            link(dve.tensor_scalar(cnt_more, tokens_of, float(UT) + 0.5, None, ALU.is_gt))
            link(dve.tensor_scalar(cnt_units, tokens_of, 0.5, None, ALU.is_gt))
            link(dve.tensor_tensor(cnt_units, cnt_units, cnt_more, ALU.add))
            link(dve.tensor_tensor_scan(units_incl, ones[:, 0:E], cnt_units, 0.0, ALU.mult, ALU.add))
            link(dve.tensor_tensor(base_row, units_incl, cnt_units, ALU.subtract))
            link(dve.tensor_scalar(base_row, base_row, float(UT), 1.0, ALU.mult, ALU.add))
            link(dve.tensor_tensor(key, bank[5][:, 0:NT * E].rearrange("p (t e) -> p t e", t=NT),
                                   base_row.unsqueeze(1).to_broadcast([P, NT, E]), ALU.add))
            link(dve.tensor_tensor(key, key, mk, ALU.mult))
            for t in range(NT):
                last = dve.max(rows[:, t, :], key[:, t, :])
            link(last)
            dve.tensor_scalar(row_idx[:, :].rearrange("p (t j) -> p t j", t=NT), rows, -1.0, None, ALU.add).then_inc(s_idx_ready, 1)
            link(dve.tensor_scalar(cnt_more, units_incl, smallp[:, IOTA:IOTA + 1], None, ALU.is_le))
            link(dve.tensor_reduce(plan_f[:, :], cnt_more, AX.X, ALU.add))
            dve.tensor_scalar(plan[:, 0:1], plan_f[:, :], float(E - 1), None, ALU.min)
            dve.tensor_scalar(plan[:, 1:2], units_incl[:, E - 1:E], -1.0, None, ALU.add).then_inc(s_plan_ready, 1)

            def shared_gates(n):
                for i in range(IC):
                    dve.wait_ge(s_silu_done, 2 * n + i + 1)
                    if n:
                        dve.wait_ge(s_act_hi, n)
                        dve.wait_ge(s_act_lo, n)
                    dve.tensor_tensor(act_f[i][:, :], silu[i][:, :], bank[2 * i + 1][:, :], ALU.mult).then_inc(s_h_ready2, 1)
                dve.wait_ge(s_act_hi, n + 1)
                dve.wait_ge(s_h_ready2, 2 * n + 2)
                for i in range(IC):
                    last = dve.tensor_tensor(inner[n][1][:, i, :], act_f[i][:, :], inner[n][0][:, i, :].bitcast(fp32), ALU.subtract)
                last.then_inc(s_act_lo, 1)

            def gates(u, j):
                dve.wait_ge(s_act_hi, u + 2)
                dve.wait_ge(s_act_lo, u + 2)
                for i in range(IC):
                    dve.wait_ge(s_silu_done, u * 2 + (5 + i))
                    dve.tensor_tensor(unit_act[:, i, :], silu[i][:, 0:UT], bank[2 * j + i][:, UT:2 * UT], ALU.mult).then_inc(s_h_ready2, 1)
                dve.wait_ge(s_act_hi, u + 3)
                dve.tensor_tensor(inner[j][1][:, :, 0:UT], unit_act, inner[j][0][:, :, 0:UT].bitcast(fp32),
                                  ALU.subtract).then_inc(s_act_lo, 1)

            def lo_tokens(u, j):
                for i in range(2):
                    dve.wait_ge(s_xg_hi, u * 2 + (i + 1))
                    part = (slice(None), slice(2 * i, 2 * i + 2), slice(None))
                    dve.tensor_tensor(xg[j][1][part], bank[token_bank(u) + i][:, 0:2 * UT].rearrange("p (c n) -> p c n", c=2),
                                      xg[j][0][part].bitcast(fp32), ALU.subtract).then_inc(s_xg_lo, 1)

            shared_gates(0)
            lo_gu(2, 0)
            shared_gates(1)
            lo_gu(3, 1)
            dve.wait_ge(s_w_ready, 1)
            link(dve.tensor_tensor(match, key.unsqueeze(2).to_broadcast([P, NT, TOPK, E]),
                                   rows.unsqueeze(3).to_broadcast([P, NT, TOPK, E]), ALU.is_equal))
            link(dve.tensor_tensor(match, match, wt.unsqueeze(2).to_broadcast([P, NT, TOPK, E]), ALU.mult))
            for t in range(NT):
                link(dve.tensor_scalar(slots[:, t * TOPK:(t + 1) * TOPK, 1], smallp[:, IOTA:IOTA + 1].to_broadcast([P, TOPK]),
                                       float(t * P), None, ALU.add))
            dve.tensor_reduce(slots[:, :, 0].bitcast(fp32), match.rearrange("p t j e -> p (t j) e"), AX.X, ALU.add).then_inc(s_slots_ready, 1)
            dve.wait_ge(s_dn_done, NSH)
            for t in range(NT):
                dve.tensor_tensor(x_tok[:, t, :], x_tok[:, t, :], bank[4 + t][:, :], ALU.add).then_inc(s_base_done, 1)
            lo_dn(2, 0)
            lo_dn(3, 1)
            lo_tokens(0, 0)
            gates(0, 0)
            lo_tokens(1, 1)
            lo_gu(4, 0)
            last_k = last_pair(dve)
            with dve.Fori(0, last_k) as k:
                for j in range(2):
                    gates(k * 2 + (j + 1), 1 - j)
                    lo_tokens(k * 2 + (j + 2), j)
                    lo_gu(k * 2 + (j + 5), 1 - j)
                    lo_dn(k * 2 + (j + 4), j)
            gates(last_k * 2 + 1, 1)

        @block.tensor
        def _(pe):
            def mm3(o, w, xx, first, last):
                pe.matmul(o, w[1], xx[0], start=first, stop=False)
                pe.matmul(o, w[0], xx[1], start=False, stop=False)
                return pe.matmul(o, w[0], xx[0], start=False, stop=last)

            def project(o, w, xx, m):
                for kc in range(KC):
                    mm = mm3(o, [w[k][:, kc, m * P:(m + 1) * P] for k in range(2)],
                             [xx[k][:, kc, :] for k in range(2)], kc == 0, kc == KC - 1)
                return mm

            for n in range(2):
                pe.nop().then_inc(s_s2_T, 1)
            pe.wait_ge(s_consts, 6)
            for t in range(NT):
                pe.wait_ge(s_xn_ready, 12 + t + 1)
                for kc in range(KC):
                    mm = pe.transpose(bank[kc][:, t * P:(t + 1) * P], xn_all[:, t, kc * P:(kc + 1) * P], ident[:, :])
                mm.then_inc(s_xnT_ready, 1)
            pe.wait_ge(s_w_lo, 1)
            pe.wait_ge(s_xT_lo, 4)
            for m in range(KC):
                project(bank[4 + m][:, :], w_of[WQ1], xT, m).then_inc(s_p1_ready, 1)
            pe.wait_ge(s_w_lo, 2)
            for m in range(KC):
                project(bank[m][:, :], w_of[WK1], xT, m).then_inc(s_p1_ready, 1)
            pe.wait_ge(s_w_lo, 3)
            for t in range(NT):
                pe.wait_ge(s_s1_out, t + 5)
                project(bank[t][:, :], xT, w_of[WV1], t).then_inc(s_p1_ready, 1)

            def scores1(u):
                t, i = divmod(u, 4)
                if u < 3:
                    pe.wait_ge(s_p1_out, 4)
                    pe.wait_ge(s_s1_out, 8)
                else:
                    pe.wait_ge(s_s1_out, 8 + u - 2)
                r = slice(HD * i, HD * (i + 1))
                for g in range(KC):
                    mm = pe.matmul(bank[SCORES[u % 3]][:, g * P:(g + 1) * P], q1[r, g, t * P:(t + 1) * P], k1[r, g, t * P:(t + 1) * P],
                                   start=True, stop=True)
                mm.then_inc(s_s1_ready, 1)

            def transpose1(u):
                pe.wait_ge(s_s1_norm, u + 1)
                if u >= 3:
                    pe.wait_ge(s_s1_pT, u - 2)
                for g in range(KC):
                    mm = pe.transpose(bank[TRANSPOSED[u % 3]][:, g * P:(g + 1) * P], scr1[u % 3][:, g * P:(g + 1) * P], ident[:, :])
                mm.then_inc(s_s1_T, 1)

            def pv1(u):
                t, i = divmod(u, 4)
                pe.wait_ge(s_s1_pT, u + 1)
                if t >= 2 and i == 0:
                    pe.wait_ge(s_o1_sum, t - 1)
                for g in range(KC):
                    c = g * P + HD * i
                    mm = pe.matmul(bank[4 + t % 2][HD * i:HD * (i + 1), g * P:(g + 1) * P], v1[:, t, c:c + HD],
                                   pT1[u % 3][:, g * P:(g + 1) * P], start=True, stop=True)
                mm.then_inc(s_s1_pv, 1)

            for u in range(3):
                scores1(u)
            for u in range(16):
                transpose1(u)
                if u + 3 < 16:
                    scores1(u + 3)
                if u:
                    pv1(u - 1)
            pv1(15)
            pe.wait_ge(s_w_lo, 4)
            pe.wait_ge(s_o1_lo, NT)
            for m in range(KC):
                project(bank[m][:, :], w_of[WO1], o1T, m).then_inc(s_h_ready, 1)
            pe.wait_ge(s_w_lo, 5)
            pe.wait_ge(s_h_lo, KC)
            for m in range(KC):
                project(bank[4 + m][:, :], w_of[WQ2], hT, m).then_inc(s_q2_ready, 1)
            pe.wait_ge(s_w_lo, N_W)
            pe.wait_ge(s_wo2_in, 16)

            def scores2(b, u):
                g, h = divmod(u, 2)
                pe.wait_ge(s_s2_exp, b * 8 + (u + 1))
                pe.wait_ge(s_kv_lo, b * 8 + (g + 3))
                pe.wait_ge(s_qb_lo, b * 4 + 4)
                mm3(bank[2 + u % 2][:, :], [qb[k][:, g, h, :] for k in range(2)], [k2[k][:, g, :] for k in range(2)],
                    True, True).then_inc(s_s2_ready, 1)

            def transpose2(b, u):
                pe.wait_ge(s_s2_norm, b * 8 + (u + 1))
                pe.wait_ge(s_pT_lo, b * 8 + (u + 1))
                for c in range(4):
                    mm = pe.transpose(bank[4 + u % 2][:, c * P:(c + 1) * P], prob[u % 2][:, c * P:(c + 1) * P], ident[:, :])
                mm.then_inc(s_s2_T, 1)

            def weighted_values(b, g):
                pe.wait_ge(s_pT_lo, b * 8 + (2 * g + 4))
                pe.wait_ge(s_kv_lo, b * 8 + 10)
                pe.wait_ge(s_o2_out, b * 4 + (g + 1))
                for c in range(4):
                    mm = mm3(bank[6][:, 0:GH * S], [v2[k][:, c, g * P:(g + 1) * P] for k in range(2)],
                             [pT[k][:, c, :] for k in range(2)], c == 0, c == 3)
                mm.then_inc(s_pv_ready, 1)

            def keys_values(b, k):
                if k == 0:
                    pe.wait_ge(s_ctx_lo, b * NC + NC)
                pe.wait_ge(s_kv_lo, b * 8 + (k + 1))
                if k < 4:
                    mm = project(bank[k % 2][:, :], w_of[WK2], ctxT, k)
                else:
                    mm = project(bank[k % 2][:, :], ctxT, w_of[WV2], k - 4)
                mm.then_inc(s_kv_ready, 1)

            def start():
                for k in range(4):
                    keys_values(0, k)
                advance(-1, True)

            def attend(b, u, more):
                transpose2(b, u)
                if u + 2 < 8:
                    scores2(b, u + 2)
                if u >= 2 and u % 2 == 0:
                    weighted_values(b, u // 2 - 1)
                if u % 2 == 1 and more:
                    keys_values(b + 1, u // 2)

            def advance(b, more, ahead=True):
                if more:
                    scores2(b + 1, 0)
                    scores2(b + 1, 1)
                if not (isinstance(b, int) and b < 0):
                    weighted_values(b, 3)
                if more:
                    for k in range(4, 8):
                        keys_values(b + 1, k)

            def scan(m, step):
                if step == 0:
                    pe.wait_ge(s_o2_out, m * 4 + 5)
                    if not (isinstance(m, int) and m == 0):
                        pe.wait_ge(s_dt_z_ready, m)
                    for kc in range(KC):
                        mm = pe.matmul(bank[7][0:S, :], o2f[:, kc * S:(kc + 1) * S], wo2[:, kc, :], start=kc == 0, stop=kc == KC - 1)
                    mm.then_inc(s_wo2_ready, 1)
                if step == 3:
                    pe.wait_ge(s_xn2_ready, m * 5 + 5)
                    if not (isinstance(m, int) and m < 2):
                        pe.wait_ge(s_x2_done, m - 1)
                    for kc in range(KC):
                        mm = pe.transpose(bank[7][:, kc * P:(kc + 1) * P], xn2_rows[:, kc * P:(kc + 1) * P], ident[:, :])
                    mm.then_inc(s_x2T_ready, 1)
                if step == 4:
                    pe.wait_ge(s_x2T_out, m + 1)
                    x3 = x2T[:, :].rearrange("p (k n) -> p k n", k=KC)
                    for kc in range(KC):
                        pe.matmul(bank[7][0:2 * NS, 0:S], wxp[:, kc, 0:2 * NS], x3[:, kc, :], start=kc == 0, stop=kc == KC - 1)
                    for kc in range(KC):
                        mm = pe.matmul(bank[7][0:RANK, S:2 * S], wxp[:, kc, 2 * NS:], x3[:, kc, :], start=kc == 0, stop=kc == KC - 1)
                    mm.then_inc(s_xp_ready, 1)
                if step == 5:
                    pe.wait_ge(s_dtr_ready, m + 1)
                    pe.wait_ge(s_bc_ready, m + 1)
                    for c in range(KC):
                        mm = pe.matmul(bank[7][:, c * S:(c + 1) * S], wdt[:, c * P:(c + 1) * P], dtr[:, :], start=True, stop=True)
                    mm.then_inc(s_dtp_ready, 1)
                if step == 17:
                    pe.wait_ge(s_y_ready, m * KC + KC)
                    if not isinstance(m, int) or m < B - 2:
                        pe.wait_ge(s_x1_done, m + 3)
                    elif m == B - 2:
                        pe.wait_ge(s_dt_z_ready, B)
                    else:
                        pe.wait_ge(s_x2_done, B - 1)
                    for j in range(KC // 2):
                        mm = pe.transpose(bank[7][:, j * P:(j + 1) * P], yT[:, j * P:(j + 1) * P], ident[:, :])
                    mm.then_inc(s_yT_ready, 1)

            run_batches(pe, start, attend, advance, scan)

            for t in range(NT):
                pe.wait_ge(s_xn3_ready, t + 1)
                for kc in range(KC):
                    mm = pe.transpose(bank[kc][:, t * P:(t + 1) * P], xn_all[:, t, kc * P:(kc + 1) * P], ident[:, :])
                mm.then_inc(s_xn3T_ready, 1)
            pe.wait_ge(s_x3_lo, KC)
            pe.wait_ge(s_gw_lo, 1)
            for kc in range(KC):
                mm = mm3(bank[4][0:E, :], [gw[k][:, kc, :] for k in range(2)], [xT[k][:, kc, :] for k in range(2)],
                         kc == 0, kc == KC - 1)
            mm.then_inc(s_logitT_ready, 1)
            pe.wait_ge(s_logitT_out, 1)
            for t in range(NT):
                mm = pe.transpose(bank[5][:, t * E:(t + 1) * E], logitT[:, t * P:(t + 1) * P], ident[0:E, 0:E])
            mm.then_inc(s_logit_ready, 1)

            def places():
                pe.wait_ge(s_before_ready, 3)
                pe.wait_ge(s_mask_ready, 1)
                pe.matmul(bank[5][:, 0:NT * E], before[:, :], rt[:, 3, :, :], start=True, stop=False, skip_group_check=True)
                for q in range(NT - 1):
                    pe.matmul(bank[5][:, (q + 1) * E:NT * E], ones[:, :], rt[:, 3, q, :].unsqueeze(1).to_broadcast([P, NT - 1 - q, E]),
                              start=False, stop=q == NT - 2, skip_group_check=True)
                for q in range(NT):
                    mm = pe.matmul(bank[5][:, NT * E:(NT + 1) * E], ones[:, :], rt[:, 3, q, :], start=q == 0, stop=q == NT - 1)
                mm.then_inc(s_pos_ready, 1)

            def shared_gate_up(n):
                pe.wait_ge(s_gu_lo, n + 1)
                w = [gu_w[n][h].rearrange("p (s c i) -> p s c i", s=2, c=KC) for h in range(2)]
                for i in range(IC):
                    if n:
                        pe.wait_ge(s_h_ready2, i + 1)
                    for sel in range(2):
                        if (n, i, sel) == (0, 1, 1):
                            places()
                        for kc in range(KC):
                            mm = mm3(bank[2 * i + sel][:, :], [w[h][:, sel, kc, i * P:(i + 1) * P] for h in range(2)],
                                     [xT[h][:, kc, :] for h in range(2)], kc == 0, kc == KC - 1)
                    mm.then_inc(s_gu_ready, 1)

            def shared_down(n):
                pe.wait_ge(s_dn_lo, n + 1)
                pe.wait_ge(s_act_lo, n + 1)
                w = [dn_w[n][h].rearrange("p (i d) -> p i d", i=IC) for h in range(2)]
                for t in range(NT):
                    for i in range(IC):
                        mm = mm3(bank[4 + t][:, :], [inner[n][h][:, i, t * P:(t + 1) * P] for h in range(2)],
                                 [w[h][:, i, :] for h in range(2)], n == 0 and i == 0, n == 1 and i == IC - 1)
                mm.then_inc(s_dn_done, 1)

            def transpose_tokens(u, j, k):
                pe.wait_ge(xg_in[j], k * 16 + 16)
                if isinstance(u, int):
                    pe.wait_ge(s_base_done, NT)
                else:
                    pe.wait_ge(s_xg_lo, u * 2)
                for c in range(KC):
                    for a in range(UA):
                        mm = pe.transpose(bank[token_bank(u) + c // 2][:, (c % 2) * UT + a * P:(c % 2) * UT + (a + 1) * P],
                                          xg_tok[j][:, a * D + c * P:a * D + (c + 1) * P], ident[:, :])
                mm.then_inc(s_xg_T, 1)

            def gate_up(u, j):
                pe.wait_ge(s_gu_lo, u + 3)
                pe.wait_ge(s_xg_lo, u * 2 + 2)
                if isinstance(u, int) and u == 0:
                    pe.wait_ge(s_h_ready2, 4)
                else:
                    pe.wait_ge(s_h_ready2, u * 2 + 2)
                w = [gu_w[j][h].rearrange("p (s c i) -> p s c i", s=2, c=KC) for h in range(2)]
                for i in range(IC):
                    for sel in range(2):
                        for kc in range(KC):
                            mm = mm3(bank[2 * j + i][:, sel * UT:(sel + 1) * UT], [w[h][:, sel, kc, i * P:(i + 1) * P] for h in range(2)],
                                     [xg[j][h][:, kc, :] for h in range(2)], kc == 0, kc == KC - 1)
                    mm.then_inc(s_gu_ready, 1)

            def down(u, j):
                pe.wait_ge(s_dn_lo, u + 3)
                pe.wait_ge(s_act_lo, u + 3)
                pe.wait_ge(s_y_evac, u + 1)
                w = [dn_w[j][h].rearrange("p (i d) -> p i d", i=IC) for h in range(2)]
                for a in range(UA):
                    for i in range(IC):
                        mm = mm3(bank[4 + a][:, :], [inner[j][h][:, i, a * P:(a + 1) * P] for h in range(2)],
                                 [w[h][:, i, :] for h in range(2)], i == 0, i == IC - 1)
                mm.then_inc(s_dn_done, 1)

            shared_gate_up(0)
            shared_gate_up(1)
            shared_down(0)
            shared_down(1)
            transpose_tokens(0, 0, 0)
            transpose_tokens(1, 1, 0)
            gate_up(0, 0)
            pe.wait_ge(s_xg_lo, 4)
            last_k = last_pair(pe)
            with pe.Fori(0, last_k) as k:
                for j in range(2):
                    gate_up(k * 2 + (j + 1), 1 - j)
                    transpose_tokens(k * 2 + (j + 2), j, k + 1)
                    down(k * 2 + j, j)
            gate_up(last_k * 2 + 1, 1)
            down(last_k * 2, 0)
            down(last_k * 2 + 1, 1)


def layouts(i):
    c = np.ascontiguousarray

    def chunks(w):
        return w.reshape(KC, P, -1).transpose(1, 0, 2).reshape(P, -1)

    def heads(w):
        return w.transpose(1, 0, 2).reshape(D, D)

    a = {n: np.asarray(v) for n, v in i.items()}
    xa = "L0_xattn_"
    mats = [heads(a[xa + "Wq1"]), heads(a[xa + "Wk1"]), heads(a[xa + "Wv1"]), a[xa + "Wo1"],
            heads(a[xa + "Wq2"]), heads(a[xa + "Wk2"]), heads(a[xa + "Wv2"]), a[xa + "Wo2"]]
    cols = [a[xa + n].reshape(KC, P).T for n in ("bq1", "bk1", "bv1", "bo1", "bq2", "bk2", "bv2")]
    cols.append(a["L0_attn_b_dt"].reshape(KC, P).T)
    iota = np.arange(P, dtype=np.float32).reshape(P, 1)
    cols.append(a["L0_attn_A_log"].reshape(NS, KC, P).transpose(2, 1, 0).reshape(P, KC * NS))
    f = "L0_ffn_"

    def units(shared, routed):
        return np.concatenate([shared, routed], axis=0)

    def inner(w):
        return w.transpose(0, 2, 1).reshape(NU, KC, P, EI).transpose(0, 2, 1, 3).reshape(NU, P, KC * EI)

    gate = inner(units(a[f + "shared_gate"].reshape(NSH, EI, D), a[f + "expert_gate"]))
    up = inner(units(a[f + "shared_up"].reshape(NSH, EI, D), a[f + "expert_up"]))
    down = units(a[f + "shared_down"].reshape(D, NSH, EI).transpose(1, 0, 2), a[f + "expert_down"])
    down = down.transpose(0, 2, 1).reshape(NU, IC, P, D).transpose(0, 2, 1, 3).reshape(NU, P, IC * D)
    return {
        "x": c(a["x"].reshape(T, D)),
        "ctx_t": c(a["ctx_1024"].transpose(0, 2, 1).reshape(B, KC, P, SC).transpose(0, 2, 1, 3).reshape(B, P, KC * SC)),
        "w_proj": c(np.stack([chunks(m) for m in mats])),
        "small": c(np.concatenate(cols + [iota], axis=1)),
        "bo2": c(a[xa + "bo2"]),
        "w_xp": c(a["L0_attn_W_xproj"].reshape(KC, P, -1).transpose(1, 0, 2)),
        "w_dt": c(a["L0_attn_W_dt"]),
        "gate_w": c(a[f + "gate_w"].T.reshape(KC, P, E).transpose(1, 0, 2)),
        "gate_b": c(a[f + "gate_bias"]),
        "w_moe": c(np.concatenate([gate, up, down], axis=2)),
    }


def kernel(**inputs):
    import concourse.bacc as _bacc
    from concourse.bass_utils import run_bass_kernel_spmd as _run

    nc = _bacc.Bacc("TRN2", target_bir_lowering=False, num_devices=1)
    arrays = layouts(inputs)
    args = {n: nc.dram_tensor(n + "_dram", v.shape, mybir.dt.float32, kind="ExternalInput").ap() for n, v in arrays.items()}
    out = nc.dram_tensor("out_dram", (T, D), mybir.dt.float32, kind="ExternalOutput").ap()
    perceiver_block(nc, **args, out=out)
    r = _run(nc, [{n + "_dram": v for n, v in arrays.items()}], core_ids=[0])
    return r.results[0]["out_dram"].reshape(B, S, D)
```
